# Optimizing a Trainium2 kernel written in Bass

```python
import numpy as np
import jax
import jax.numpy as jnp

def _softmax(x, axis=-1):
    return jax.nn.softmax(x, axis=axis)

def _gelu(x):
    return jax.nn.gelu(x, approximate=True)

def _silu(x):
    return jax.nn.silu(x)

def _sigmoid(x):
    return jax.nn.sigmoid(x)

def _layernorm(x, axis=-1, eps=1e-05):
    m = jnp.mean(x, axis=axis, keepdims=True)
    v = jnp.var(x, axis=axis, keepdims=True)
    return (x - m) / jnp.sqrt(v + eps)

def _scatter_add(tgt, idx, src, axis=0):
    return tgt.at[idx].add(src)

def _segment_sum(src, seg, n):
    return jax.ops.segment_sum(src, seg, n)
kernel_name = 'mk_decoder_postln_d2_seqx_r8_ad055e'

def setup_inputs(seed: int=0):
    np.random.seed(seed)
    _w = jnp.asarray

    def _rec_inputs():
        import jax
        import jax.numpy as jnp
        _rk = jax.random.key(seed)
        x = 7.22e-05 + 1 * jax.random.normal(jax.random.fold_in(_rk, 1), (4, 512, 128), jnp.float32)
        _lenS = 512 - jax.random.randint(jax.random.fold_in(_rk, 7), (4,), 0, max(1, 512 // 4) + 1, jnp.int32)
        _lenS2 = 154 - jax.random.randint(jax.random.fold_in(_rk, 8), (4,), 0, max(1, 154 // 4) + 1, jnp.int32)
        _ctx_768P = jax.random.normal(jax.random.fold_in(_rk, 11), (4, 16, 96), jnp.float32)
        _ctx_768c = jax.random.dirichlet(jax.random.fold_in(_rk, 511), 0.3 * jnp.ones((16,), jnp.float32), (4, 154))
        _ctx_768t = jnp.einsum('bsk,bkd->bsd', _ctx_768c, _ctx_768P)
        _ctx_768t = _ctx_768t * jax.lax.rsqrt(jnp.mean(jnp.square(_ctx_768t)) + 1e-12) * 0.953939
        ctx_768 = -0.000191848 + 0.999787 * (_ctx_768t + 0.3 * jax.random.normal(jax.random.fold_in(_rk, 611), (4, 154, 96), jnp.float32))
        _validS = jnp.arange(512)[None, :] < _lenS[:, None]
        _validS2 = jnp.arange(154)[None, :] < _lenS2[:, None]
        _causal = jnp.tril(jnp.ones((512, 512), dtype=bool))
        mask_BxS_bf1 = jnp.ones((4, 512), dtype=bool)
        mask_BxS2_bf1 = jnp.ones((4, 154), dtype=bool)
        return (x, ctx_768, mask_BxS_bf1, mask_BxS2_bf1)
    x, ctx_768, mask_BxS_bf1, mask_BxS2_bf1 = _rec_inputs()

    def _L0_attn_setup():
        import jax, jax.numpy as jnp
        import numpy as np
        import math
        D_MODEL = 128
        D_STATE = 128
        EXPAND = 2
        HEADDIM = 64
        NGROUPS = 1
        D_INNER = EXPAND * D_MODEL
        NHEADS = D_INNER // HEADDIM
        ROPE_FRACTION = 0.5
        SPLIT = int(D_STATE * ROPE_FRACTION)
        SPLIT -= SPLIT % 2
        NUM_ANGLES = SPLIT // 2
        A_FLOOR = 0.0001
        EPS = 1e-05
        DT_MIN, DT_MAX, DT_INIT_FLOOR = (0.001, 0.1, 0.0001)
        D_IN_PROJ = 2 * D_INNER + 2 * D_STATE * NGROUPS + 3 * NHEADS + NUM_ANGLES

        def _rmsnorm(x, w):
            xf = x.astype(jnp.float32)
            return xf * jax.lax.rsqrt(jnp.mean(xf * xf, axis=-1, keepdims=True) + EPS) * w

        def _rope(v, theta):
            v1 = v[..., :NUM_ANGLES]
            v2 = v[..., NUM_ANGLES:SPLIT]
            rest = v[..., SPLIT:]
            c, s = (jnp.cos(theta), jnp.sin(theta))
            return jnp.concatenate([v1 * c - v2 * s, v1 * s + v2 * c, rest], axis=-1)
        key = jax.random.key(seed)
        ks = jax.random.split(key, 6)
        b, l = (2, 128)
        u = jax.random.normal(ks[0], (b, l, D_MODEL), jnp.float32)
        W_in = jax.random.normal(ks[1], (D_IN_PROJ, D_MODEL), jnp.float32) * 0.02
        W_out = jax.random.normal(ks[2], (D_MODEL, D_INNER), jnp.float32) * 0.02
        _dt = jnp.exp(jax.random.uniform(ks[3], (NHEADS,), jnp.float32) * (math.log(DT_MAX) - math.log(DT_MIN)) + math.log(DT_MIN))
        _dt = jnp.clip(_dt, DT_INIT_FLOOR, None)
        dt_bias = _dt + jnp.log(-jnp.expm1(-_dt))
        B_bias = jnp.ones((NHEADS, D_STATE), jnp.float32)
        C_bias = jnp.ones((NHEADS, D_STATE), jnp.float32)
        B_norm_w = jnp.ones((D_STATE,), jnp.float32)
        C_norm_w = jnp.ones((D_STATE,), jnp.float32)
        D_param = jnp.ones((NHEADS,), jnp.float32)
        return {'u': u, 'W_in': W_in, 'W_out': W_out, 'dt_bias': dt_bias, 'B_bias': B_bias, 'C_bias': C_bias, 'B_norm_w': B_norm_w, 'C_norm_w': C_norm_w, 'D_param': D_param}
    _L0_attn_all = _L0_attn_setup()
    _L0_attn_in = {k: v for k, v in _L0_attn_all.items() if k in ('W_in', 'W_out', 'dt_bias', 'B_bias', 'C_bias', 'B_norm_w', 'C_norm_w', 'D_param')}
    del _L0_attn_all

    def _L0_xattn_setup():
        import jax, jax.numpy as jnp
        import numpy as np
        N_HEADS = 16
        key = jax.random.key(seed)
        ks = jax.random.split(key, 8)
        b, l, m = (8, 128, 128)
        d_embed, d_cross = (128, 96)
        s_q = 1.0 / np.sqrt(d_embed)
        s_kv = 1.0 / np.sqrt(d_cross)
        return {'x': jax.random.normal(ks[0], (b, l, d_embed), jnp.float32), 'y': jax.random.normal(ks[1], (b, m, d_cross), jnp.float32), 'Wq': jax.random.normal(ks[2], (d_embed, d_embed), jnp.float32) * s_q, 'bq': jax.random.normal(ks[3], (d_embed,), jnp.float32) * 0.01, 'Wkv': jax.random.normal(ks[4], (2 * d_embed, d_cross), jnp.float32) * s_kv, 'bkv': jax.random.normal(ks[5], (2 * d_embed,), jnp.float32) * 0.01, 'Wo': jax.random.normal(ks[6], (d_embed, d_embed), jnp.float32) * s_q, 'bo': jax.random.normal(ks[7], (d_embed,), jnp.float32) * 0.01}
    _L0_xattn_all = _L0_xattn_setup()
    _L0_xattn_in = {k: v for k, v in _L0_xattn_all.items() if k in ('Wq', 'bq', 'Wkv', 'bkv', 'Wo', 'bo')}
    del _L0_xattn_all

    def _L0_ffn_setup():
        import jax, jax.numpy as jnp
        import numpy as np
        B, T, H = (8, 256, 128)
        F = 512
        E = 8
        TOP_K = 2
        key = jax.random.key(seed)
        ks = jax.random.split(key, 6)
        s_h = 1.0 / np.sqrt(H)
        s_f = 1.0 / np.sqrt(F)
        return {'hidden_states': jax.random.normal(ks[0], (B, T, H), dtype=jnp.float32), 'gate_w': jax.random.uniform(ks[1], (H, E), minval=-s_h, maxval=s_h, dtype=jnp.float32), 'w1': jax.random.uniform(ks[2], (E, H, F), minval=-s_h, maxval=s_h, dtype=jnp.float32), 'b1': jax.random.uniform(ks[3], (E, F), minval=-s_h, maxval=s_h, dtype=jnp.float32), 'w2': jax.random.uniform(ks[4], (E, F, H), minval=-s_f, maxval=s_f, dtype=jnp.float32), 'b2': jax.random.uniform(ks[5], (E, H), minval=-s_f, maxval=s_f, dtype=jnp.float32)}
    _L0_ffn_all = _L0_ffn_setup()
    _L0_ffn_in = {k: v for k, v in _L0_ffn_all.items() if k in ('gate_w', 'w1', 'b1', 'w2', 'b2')}
    del _L0_ffn_all

    def _L1_attn_setup():
        import jax, jax.numpy as jnp
        import numpy as np
        MODEL_DIM = 128
        HEADS = 16
        HEAD_DIM = MODEL_DIM // HEADS
        B, T = (2, 256)
        TB_LEN = 500
        key = jax.random.key(seed)
        ks = jax.random.split(key, 12)
        s = 0.02
        d = MODEL_DIM
        return {'x': jax.random.normal(ks[0], (B, T, d), dtype=jnp.float32), 'Wq': jax.random.normal(ks[1], (d, d), dtype=jnp.float32) * s, 'bq': jnp.zeros((d,), jnp.float32), 'Wk': jax.random.normal(ks[2], (d, d), dtype=jnp.float32) * s, 'bk': jnp.zeros((d,), jnp.float32), 'Wv': jax.random.normal(ks[3], (d, d), dtype=jnp.float32) * s, 'bv': jnp.zeros((d,), jnp.float32), 'Wo': jax.random.normal(ks[4], (d, d), dtype=jnp.float32) * s, 'bo': jnp.zeros((d,), jnp.float32), 'et_gate': jax.random.normal(ks[5], (1, 1, 1), dtype=jnp.float32), 'is_gate': jax.random.normal(ks[6], (1, 1, 1), dtype=jnp.float32), 'time_bias': jnp.linspace(-1.0, 1.0, TB_LEN, dtype=jnp.float32).reshape(1, 1, TB_LEN)}
    _L1_attn_all = _L1_attn_setup()
    _L1_attn_in = {k: v for k, v in _L1_attn_all.items() if k in ('Wq', 'bq', 'Wk', 'bk', 'Wv', 'bv', 'Wo', 'bo', 'et_gate', 'is_gate', 'time_bias')}
    del _L1_attn_all

    def _L1_xattn_setup():
        import jax, jax.numpy as jnp
        import numpy as np
        B, T, DT, G, DV = (16, 64, 128, 72, 96)
        H, DH = (4, 32)
        INNER = H * DH
        HID = 4 * DT
        N_STATE = 64
        K_TOP = 32

        def layernorm(x, g, b, eps=1e-05):
            m = x.mean(-1, keepdims=True)
            v = x.var(-1, keepdims=True)
            return (x - m) * jax.lax.rsqrt(v + eps) * g + b

        def s4d(x, log_dt, A_re, A_im, C_re, C_im, D_skip):
            Bb, L, D = x.shape
            dt = jnp.exp(log_dt)
            A = A_re + 1j * A_im
            C = C_re + 1j * C_im
            dtA = dt[:, None] * A
            dC = C * (jnp.exp(dtA) - 1.0) / A
            powers = jnp.exp(dtA[:, :, None] * jnp.arange(L))
            K = 2.0 * jnp.einsum('dn,dnl->dl', dC, powers).real
            n = 2 * L
            Kf = jnp.fft.rfft(K, n=n, axis=-1)
            xf = jnp.fft.rfft(x, n=n, axis=1)
            y = jnp.fft.irfft(xf * Kf.T[None], n=n, axis=1)[:, :L]
            return y + x * D_skip
        key = jax.random.key(seed)
        ks = jax.random.split(key, 16)
        s = 0.02
        inp = {'x_text': jax.random.normal(ks[0], (B, T, DT), jnp.float32), 'x_vision': jax.random.normal(ks[1], (B, G, DV), jnp.float32), 'text_mask': jnp.ones((B, T), bool), 'vision_mask': jnp.ones((B, G), bool), 'Wq': jax.random.normal(ks[2], (DT, INNER), jnp.float32) * s, 'Wk': jax.random.normal(ks[3], (DV, INNER), jnp.float32) * s, 'Wv': jax.random.normal(ks[4], (DV, DT), jnp.float32) * s, 'W_film_in': jax.random.normal(ks[5], (DT, 2 * DT), jnp.float32) * s, 'b_film_in': jnp.zeros((2 * DT,), jnp.float32), 'W_film_out': jax.random.normal(ks[6], (DT, 2 * DT), jnp.float32) * s, 'b_film_out': jnp.zeros((2 * DT,), jnp.float32), 'g_norm_in': jnp.ones((DT,), jnp.float32), 'b_norm_in': jnp.zeros((DT,), jnp.float32), 'g_norm_out': jnp.ones((DT,), jnp.float32), 'b_norm_out': jnp.zeros((DT,), jnp.float32), 'g_ffn': jnp.ones((DT,), jnp.float32), 'b_ffn': jnp.zeros((DT,), jnp.float32), 'W1': jax.random.normal(ks[7], (DT, HID), jnp.float32) * s, 'b1': jnp.zeros((HID,), jnp.float32), 'W2': jax.random.normal(ks[8], (HID, DT), jnp.float32) * s, 'b2': jnp.zeros((DT,), jnp.float32), 'log_dt': jnp.log(0.001) + jax.random.uniform(ks[9], (DT,), jnp.float32) * (jnp.log(0.1) - jnp.log(0.001)), 'A_re': -0.5 * jnp.ones((DT, N_STATE), jnp.float32), 'A_im': jnp.tile(jnp.pi * jnp.arange(N_STATE, dtype=jnp.float32), (DT, 1)), 'C_re': jax.random.normal(ks[10], (DT, N_STATE), jnp.float32) * 0.5 ** 0.5, 'C_im': jax.random.normal(ks[11], (DT, N_STATE), jnp.float32) * 0.5 ** 0.5, 'D_skip': jax.random.normal(ks[12], (DT,), jnp.float32), 'mod_gate': jnp.array(0.5, jnp.float32)}
        return inp
    _L1_xattn_all = _L1_xattn_setup()
    _L1_xattn_in = {k: v for k, v in _L1_xattn_all.items() if k in ('Wq', 'Wk', 'Wv', 'W_film_in', 'b_film_in', 'W_film_out', 'b_film_out', 'g_norm_in', 'b_norm_in', 'g_norm_out', 'b_norm_out', 'g_ffn', 'b_ffn', 'W1', 'b1', 'W2', 'b2', 'log_dt', 'A_re', 'A_im', 'C_re', 'C_im', 'D_skip', 'mod_gate')}
    del _L1_xattn_all

    def _L1_ffn_setup():
        import jax, jax.numpy as jnp
        import numpy as np
        H, I, E, NS, C = (128, 128, 6, 2, 2)
        TOPK = 2
        TEMP = 1.0
        EPS = 1e-06
        key = jax.random.key(seed)
        ks = jax.random.split(key, 20)
        sd = 0.02
        inp = {'x': jax.random.normal(ks[0], (4, 256, H), jnp.float32), 'router_W': jax.random.normal(ks[1], (C, H, E), jnp.float32) * sd, 'router_b': jax.random.normal(ks[2], (C, E), jnp.float32) * sd, 'gate_bias': jax.random.normal(ks[3], (C, E), jnp.float32) * sd, 'exp_Wup': jax.random.normal(ks[4], (E, H, I), jnp.float32) * sd, 'exp_bup': jnp.zeros((E, I), jnp.float32), 'exp_Wg': jax.random.normal(ks[5], (E, I, I), jnp.float32) * sd, 'exp_bg': jnp.zeros((E, I), jnp.float32), 'exp_Wdown': jax.random.normal(ks[6], (E, I, H), jnp.float32) * sd, 'exp_bdown': jnp.zeros((E, H), jnp.float32), 'share_Wup': jax.random.normal(ks[7], (H, NS * I), jnp.float32) * sd, 'share_bup': jnp.zeros((NS * I,), jnp.float32), 'share_Wg': jax.random.normal(ks[8], (I, I), jnp.float32) * sd, 'share_bg': jnp.zeros((I,), jnp.float32), 'share_Wdown': jax.random.normal(ks[9], (I, H), jnp.float32) * sd, 'share_bdown': jnp.zeros((H,), jnp.float32), 'norm_w': jnp.ones((C, H), jnp.float32)}
        return inp
    _L1_ffn_all = _L1_ffn_setup()
    _L1_ffn_in = {k: v for k, v in _L1_ffn_all.items() if k in ('router_W', 'router_b', 'gate_bias', 'exp_Wup', 'exp_bup', 'exp_Wg', 'exp_bg', 'exp_Wdown', 'exp_bdown', 'share_Wup', 'share_bup', 'share_Wg', 'share_bg', 'share_Wdown', 'share_bdown', 'norm_w')}
    del _L1_ffn_all
    return {'x': x, 'ctx_768': ctx_768, 'mask_BxS_bf1': mask_BxS_bf1, 'mask_BxS2_bf1': mask_BxS2_bf1, 'L0_attn_W_in': _L0_attn_in['W_in'], 'L0_attn_W_out': _L0_attn_in['W_out'], 'L0_attn_dt_bias': _L0_attn_in['dt_bias'], 'L0_attn_B_bias': _L0_attn_in['B_bias'], 'L0_attn_C_bias': _L0_attn_in['C_bias'], 'L0_attn_B_norm_w': _L0_attn_in['B_norm_w'], 'L0_attn_C_norm_w': _L0_attn_in['C_norm_w'], 'L0_attn_D_param': _L0_attn_in['D_param'], 'L0_xattn_Wq': _L0_xattn_in['Wq'], 'L0_xattn_bq': _L0_xattn_in['bq'], 'L0_xattn_Wkv': _L0_xattn_in['Wkv'], 'L0_xattn_bkv': _L0_xattn_in['bkv'], 'L0_xattn_Wo': _L0_xattn_in['Wo'], 'L0_xattn_bo': _L0_xattn_in['bo'], 'L0_ffn_gate_w': _L0_ffn_in['gate_w'], 'L0_ffn_w1': _L0_ffn_in['w1'], 'L0_ffn_b1': _L0_ffn_in['b1'], 'L0_ffn_w2': _L0_ffn_in['w2'], 'L0_ffn_b2': _L0_ffn_in['b2'], 'L1_attn_Wq': _L1_attn_in['Wq'], 'L1_attn_bq': _L1_attn_in['bq'], 'L1_attn_Wk': _L1_attn_in['Wk'], 'L1_attn_bk': _L1_attn_in['bk'], 'L1_attn_Wv': _L1_attn_in['Wv'], 'L1_attn_bv': _L1_attn_in['bv'], 'L1_attn_Wo': _L1_attn_in['Wo'], 'L1_attn_bo': _L1_attn_in['bo'], 'L1_attn_et_gate': _L1_attn_in['et_gate'], 'L1_attn_is_gate': _L1_attn_in['is_gate'], 'L1_attn_time_bias': _L1_attn_in['time_bias'], 'L1_xattn_Wq': _L1_xattn_in['Wq'], 'L1_xattn_Wk': _L1_xattn_in['Wk'], 'L1_xattn_Wv': _L1_xattn_in['Wv'], 'L1_xattn_W_film_in': _L1_xattn_in['W_film_in'], 'L1_xattn_b_film_in': _L1_xattn_in['b_film_in'], 'L1_xattn_W_film_out': _L1_xattn_in['W_film_out'], 'L1_xattn_b_film_out': _L1_xattn_in['b_film_out'], 'L1_xattn_g_norm_in': _L1_xattn_in['g_norm_in'], 'L1_xattn_b_norm_in': _L1_xattn_in['b_norm_in'], 'L1_xattn_g_norm_out': _L1_xattn_in['g_norm_out'], 'L1_xattn_b_norm_out': _L1_xattn_in['b_norm_out'], 'L1_xattn_g_ffn': _L1_xattn_in['g_ffn'], 'L1_xattn_b_ffn': _L1_xattn_in['b_ffn'], 'L1_xattn_W1': _L1_xattn_in['W1'], 'L1_xattn_b1': _L1_xattn_in['b1'], 'L1_xattn_W2': _L1_xattn_in['W2'], 'L1_xattn_b2': _L1_xattn_in['b2'], 'L1_xattn_log_dt': _L1_xattn_in['log_dt'], 'L1_xattn_A_re': _L1_xattn_in['A_re'], 'L1_xattn_A_im': _L1_xattn_in['A_im'], 'L1_xattn_C_re': _L1_xattn_in['C_re'], 'L1_xattn_C_im': _L1_xattn_in['C_im'], 'L1_xattn_D_skip': _L1_xattn_in['D_skip'], 'L1_xattn_mod_gate': _L1_xattn_in['mod_gate'], 'L1_ffn_router_W': _L1_ffn_in['router_W'], 'L1_ffn_router_b': _L1_ffn_in['router_b'], 'L1_ffn_gate_bias': _L1_ffn_in['gate_bias'], 'L1_ffn_exp_Wup': _L1_ffn_in['exp_Wup'], 'L1_ffn_exp_bup': _L1_ffn_in['exp_bup'], 'L1_ffn_exp_Wg': _L1_ffn_in['exp_Wg'], 'L1_ffn_exp_bg': _L1_ffn_in['exp_bg'], 'L1_ffn_exp_Wdown': _L1_ffn_in['exp_Wdown'], 'L1_ffn_exp_bdown': _L1_ffn_in['exp_bdown'], 'L1_ffn_share_Wup': _L1_ffn_in['share_Wup'], 'L1_ffn_share_bup': _L1_ffn_in['share_bup'], 'L1_ffn_share_Wg': _L1_ffn_in['share_Wg'], 'L1_ffn_share_bg': _L1_ffn_in['share_bg'], 'L1_ffn_share_Wdown': _L1_ffn_in['share_Wdown'], 'L1_ffn_share_bdown': _L1_ffn_in['share_bdown'], 'L1_ffn_norm_w': _L1_ffn_in['norm_w']}

def reference(x, ctx_768, mask_BxS_bf1, mask_BxS2_bf1, L0_attn_W_in, L0_attn_W_out, L0_attn_dt_bias, L0_attn_B_bias, L0_attn_C_bias, L0_attn_B_norm_w, L0_attn_C_norm_w, L0_attn_D_param, L0_xattn_Wq, L0_xattn_bq, L0_xattn_Wkv, L0_xattn_bkv, L0_xattn_Wo, L0_xattn_bo, L0_ffn_gate_w, L0_ffn_w1, L0_ffn_b1, L0_ffn_w2, L0_ffn_b2, L1_attn_Wq, L1_attn_bq, L1_attn_Wk, L1_attn_bk, L1_attn_Wv, L1_attn_bv, L1_attn_Wo, L1_attn_bo, L1_attn_et_gate, L1_attn_is_gate, L1_attn_time_bias, L1_xattn_Wq, L1_xattn_Wk, L1_xattn_Wv, L1_xattn_W_film_in, L1_xattn_b_film_in, L1_xattn_W_film_out, L1_xattn_b_film_out, L1_xattn_g_norm_in, L1_xattn_b_norm_in, L1_xattn_g_norm_out, L1_xattn_b_norm_out, L1_xattn_g_ffn, L1_xattn_b_ffn, L1_xattn_W1, L1_xattn_b1, L1_xattn_W2, L1_xattn_b2, L1_xattn_log_dt, L1_xattn_A_re, L1_xattn_A_im, L1_xattn_C_re, L1_xattn_C_im, L1_xattn_D_skip, L1_xattn_mod_gate, L1_ffn_router_W, L1_ffn_router_b, L1_ffn_gate_bias, L1_ffn_exp_Wup, L1_ffn_exp_bup, L1_ffn_exp_Wg, L1_ffn_exp_bg, L1_ffn_exp_Wdown, L1_ffn_exp_bdown, L1_ffn_share_Wup, L1_ffn_share_bup, L1_ffn_share_Wg, L1_ffn_share_bg, L1_ffn_share_Wdown, L1_ffn_share_bdown, L1_ffn_norm_w):
    import jax
    import jax.numpy as jnp

    def _L0_attn_ref(u, W_in, W_out, dt_bias, B_bias, C_bias, B_norm_w, C_norm_w, D_param):
        import jax, jax.numpy as jnp
        import numpy as np
        import math
        D_MODEL = 128
        D_STATE = 128
        EXPAND = 2
        HEADDIM = 64
        NGROUPS = 1
        D_INNER = EXPAND * D_MODEL
        NHEADS = D_INNER // HEADDIM
        ROPE_FRACTION = 0.5
        SPLIT = int(D_STATE * ROPE_FRACTION)
        SPLIT -= SPLIT % 2
        NUM_ANGLES = SPLIT // 2
        A_FLOOR = 0.0001
        EPS = 1e-05
        DT_MIN, DT_MAX, DT_INIT_FLOOR = (0.001, 0.1, 0.0001)
        D_IN_PROJ = 2 * D_INNER + 2 * D_STATE * NGROUPS + 3 * NHEADS + NUM_ANGLES

        def _rmsnorm(x, w):
            xf = x.astype(jnp.float32)
            return xf * jax.lax.rsqrt(jnp.mean(xf * xf, axis=-1, keepdims=True) + EPS) * w

        def _rope(v, theta):
            v1 = v[..., :NUM_ANGLES]
            v2 = v[..., NUM_ANGLES:SPLIT]
            rest = v[..., SPLIT:]
            c, s = (jnp.cos(theta), jnp.sin(theta))
            return jnp.concatenate([v1 * c - v2 * s, v1 * s + v2 * c, rest], axis=-1)
        b, l, _ = u.shape
        proj = u @ W_in.T
        sizes = [D_INNER, D_INNER, D_STATE * NGROUPS, D_STATE * NGROUPS, NHEADS, NHEADS, NHEADS, NUM_ANGLES]
        splits = np.cumsum(sizes)[:-1]
        z, x, B, C, dd_dt, dd_A, trap, angles = jnp.split(proj, splits, axis=-1)
        z = z.reshape(b, l, NHEADS, HEADDIM)
        x = x.reshape(b, l, NHEADS, HEADDIM)
        B = B.reshape(b, l, NGROUPS, D_STATE)
        C = C.reshape(b, l, NGROUPS, D_STATE)
        a = -jax.nn.softplus(dd_A.astype(jnp.float32))
        a = jnp.minimum(a, -A_FLOOR)
        dt = jax.nn.softplus(dd_dt.astype(jnp.float32) + dt_bias)
        adt = a * dt
        theta = jnp.cumsum(angles[:, :, None, :].astype(jnp.float32) * dt[..., None], axis=1)
        Bn = _rmsnorm(B, B_norm_w)
        Cn = _rmsnorm(C, C_norm_w)
        head_group = np.repeat(np.arange(NGROUPS), NHEADS // NGROUPS)
        Bh = Bn[:, :, head_group, :] + B_bias
        Ch = Cn[:, :, head_group, :] + C_bias
        Bh = _rope(Bh, theta)
        Ch = _rope(Ch, theta)
        lam = jax.nn.sigmoid(trap.astype(jnp.float32))
        g = jnp.exp(adt)
        xs = (jnp.moveaxis(x.astype(jnp.float32), 1, 0), jnp.moveaxis(Bh, 1, 0), jnp.moveaxis(Ch, 1, 0), jnp.moveaxis(dt, 1, 0), jnp.moveaxis(g, 1, 0), jnp.moveaxis(lam, 1, 0))
        h0 = jnp.zeros((b, NHEADS, HEADDIM, D_STATE), jnp.float32)
        bx0 = jnp.zeros_like(h0)

        def step(carry, inp):
            h, bx_prev = carry
            x_t, B_t, C_t, dt_t, g_t, lam_t = inp
            bx_t = x_t[..., :, None] * B_t[..., None, :]
            ge = g_t[..., None, None]
            dte = dt_t[..., None, None]
            le = lam_t[..., None, None]
            h = ge * h + dte * (le * bx_t + (1.0 - le) * ge * bx_prev)
            y_t = jnp.einsum('bhpn,bhn->bhp', h, C_t)
            return ((h, bx_t), y_t)
        _, ys = jax.lax.scan(step, (h0, bx0), xs)
        y = jnp.moveaxis(ys, 0, 1) + D_param[:, None] * x
        y = y * jax.nn.silu(z)
        y = y.reshape(b, l, D_INNER).astype(u.dtype)
        return y @ W_out.T

    def _L0_xattn_ref(x, y, Wq, bq, Wkv, bkv, Wo, bo):
        import jax, jax.numpy as jnp
        import numpy as np
        N_HEADS = 16
        b, l, d = x.shape
        m = y.shape[1]
        h = N_HEADS
        dh = d // h
        q = (jnp.einsum('bld,ed->ble', x, Wq) + bq).reshape(b, l, h, dh)
        kv = (jnp.einsum('bmc,ec->bme', y, Wkv) + bkv).reshape(b, m, h, 2 * dh)
        k, v = (kv[..., :dh], kv[..., dh:])
        scale = 1.0 / jnp.sqrt(jnp.asarray(dh, x.dtype))
        att = jax.nn.softmax(jnp.einsum('blhd,bmhd->blmh', q, k) * scale, axis=2)
        out = jnp.einsum('blmh,bmhd->blhd', att, v).reshape(b, l, d)
        return jnp.einsum('bld,ed->ble', out, Wo) + bo

    def _L0_ffn_ref(hidden_states, gate_w, w1, b1, w2, b2):
        import jax, jax.numpy as jnp
        import numpy as np
        B, T, H = (8, 256, 128)
        F = 512
        E = 8
        TOP_K = 2
        b, t, h = hidden_states.shape
        seq_rep = hidden_states.mean(axis=1)
        router_logits = seq_rep @ gate_w
        probs = jax.nn.softmax(router_logits.astype(jnp.float32), axis=-1)
        top_w, top_i = jax.lax.top_k(probs, TOP_K)
        top_w = top_w / top_w.sum(axis=-1, keepdims=True)
        top_w = top_w.astype(hidden_states.dtype)
        combine = jnp.zeros((b, E), dtype=hidden_states.dtype)
        combine = combine.at[jnp.arange(b)[:, None], top_i].set(top_w)
        out = jnp.zeros_like(hidden_states)
        for e in range(E):
            hmid = jax.nn.gelu(jnp.einsum('bth,hf->btf', hidden_states, w1[e]) + b1[e], approximate=False)
            y = jnp.einsum('btf,fh->bth', hmid, w2[e]) + b2[e]
            out = out + combine[:, e][:, None, None] * y
        return out

    def _L1_attn_ref(x, Wq, bq, Wk, bk, Wv, bv, Wo, bo, et_gate, is_gate, time_bias):
        import jax, jax.numpy as jnp
        import numpy as np
        MODEL_DIM = 128
        HEADS = 16
        HEAD_DIM = MODEL_DIM // HEADS
        B, T = (2, 256)
        TB_LEN = 500
        Bb, Tt, D = x.shape
        H, hd = (HEADS, HEAD_DIM)
        Q = (x @ Wq.T + bq).reshape(Bb, Tt, H, hd).transpose(0, 2, 1, 3)
        K = (x @ Wk.T + bk).reshape(Bb, Tt, H, hd).transpose(0, 2, 1, 3)
        V = (x @ Wv.T + bv).reshape(Bb, Tt, H, hd).transpose(0, 2, 1, 3)
        scores = jnp.einsum('bhqd,bhkd->bhqk', Q, K) / jnp.sqrt(jnp.float32(hd))
        pos = jnp.arange(Tt)[None, :] - jnp.arange(Tt)[:, None]
        idx = jnp.clip(pos + TB_LEN // 2, 0, TB_LEN - 1)
        tp = time_bias[:, :, idx]
        tp = jnp.squeeze(tp, axis=1)[None, None]
        scores = scores + jax.nn.sigmoid(et_gate) * tp + is_gate
        attn = jax.nn.softmax(scores, axis=-1)
        context = jnp.matmul(attn, V)
        context = context.transpose(0, 2, 1, 3, 4).reshape(Bb, Tt, D)
        return context @ Wo.T + bo

    def _L1_xattn_ref(x_text, x_vision, text_mask, vision_mask, Wq, Wk, Wv, W_film_in, b_film_in, W_film_out, b_film_out, g_norm_in, b_norm_in, g_norm_out, b_norm_out, g_ffn, b_ffn, W1, b1, W2, b2, log_dt, A_re, A_im, C_re, C_im, D_skip, mod_gate):
        import jax, jax.numpy as jnp
        import numpy as np
        B, T, DT, G, DV = (16, 64, 128, 72, 96)
        H, DH = (4, 32)
        INNER = H * DH
        HID = 4 * DT
        N_STATE = 64
        K_TOP = 32

        def layernorm(x, g, b, eps=1e-05):
            m = x.mean(-1, keepdims=True)
            v = x.var(-1, keepdims=True)
            return (x - m) * jax.lax.rsqrt(v + eps) * g + b

        def s4d(x, log_dt, A_re, A_im, C_re, C_im, D_skip):
            Bb, L, D = x.shape
            dt = jnp.exp(log_dt)
            A = A_re + 1j * A_im
            C = C_re + 1j * C_im
            dtA = dt[:, None] * A
            dC = C * (jnp.exp(dtA) - 1.0) / A
            powers = jnp.exp(dtA[:, :, None] * jnp.arange(L))
            K = 2.0 * jnp.einsum('dn,dnl->dl', dC, powers).real
            n = 2 * L
            Kf = jnp.fft.rfft(K, n=n, axis=-1)
            xf = jnp.fft.rfft(x, n=n, axis=1)
            y = jnp.fft.irfft(xf * Kf.T[None], n=n, axis=1)[:, :L]
            return y + x * D_skip
        Bb, Tt, D = x_text.shape
        Gg = x_vision.shape[1]
        Q = (x_text @ Wq).reshape(Bb, Tt, H, DH)
        K = (x_vision @ Wk).reshape(Bb, Gg, H, DH)
        scores = jnp.einsum('bthd,bghd->bhtg', Q, K) / np.sqrt(DH).astype(np.float32)
        scores = jnp.where(vision_mask[:, None, None, :], scores, -jnp.inf)
        topv, topi = jax.lax.top_k(scores, K_TOP)
        probs = jax.nn.softmax(topv, axis=-1)
        bi = jnp.arange(Bb)[:, None, None, None]
        hi = jnp.arange(H)[None, :, None, None]
        ti = jnp.arange(Tt)[None, None, :, None]
        attn = jnp.zeros_like(scores).at[bi, hi, ti, topi].set(probs)
        attn_mean = attn.mean(axis=1)
        V = x_vision @ Wv
        c_t = jnp.einsum('btg,bgd->btd', attn_mean, V)
        c_t = c_t * text_mask[..., None]
        x = layernorm(x_text, g_norm_in, b_norm_in)
        scale_in, shift_in = jnp.split(c_t @ W_film_in + b_film_in, 2, axis=-1)
        x = x * (1.0 + mod_gate * scale_in) + mod_gate * shift_in
        y = s4d(x, log_dt, A_re, A_im, C_re, C_im, D_skip)
        scale_out, shift_out = jnp.split(c_t @ W_film_out + b_film_out, 2, axis=-1)
        y = y * (1.0 + mod_gate * scale_out) + mod_gate * shift_out
        xt = x_text + y
        h = layernorm(xt, g_ffn, b_ffn)
        h = jax.nn.gelu(h @ W1 + b1, approximate=False) @ W2 + b2
        xt = xt + h
        return layernorm(xt, g_norm_out, b_norm_out)

    def _L1_ffn_ref(x, router_W, router_b, gate_bias, exp_Wup, exp_bup, exp_Wg, exp_bg, exp_Wdown, exp_bdown, share_Wup, share_bup, share_Wg, share_bg, share_Wdown, share_bdown, norm_w):
        import jax, jax.numpy as jnp
        import numpy as np
        H, I, E, NS, C = (128, 128, 6, 2, 2)
        TOPK = 2
        TEMP = 1.0
        EPS = 1e-06
        B, S, Hd = x.shape
        xf = x.reshape(-1, Hd)
        for j in range(C):
            residual = xf
            gate = (xf @ router_W[j] + router_b[j]) / TEMP
            biased = gate + gate_bias[j]
            _, ids = jax.lax.top_k(biased, TOPK)
            sel = (ids[:, :, None] == jnp.arange(E)[None, None, :]).any(axis=1)
            weights = jax.nn.softmax(jnp.where(sel, gate, -jnp.inf), axis=-1)
            h = jnp.einsum('nh,ehi->eni', xf, exp_Wup) + exp_bup[:, None, :]
            h = jax.nn.silu(jnp.einsum('eni,eij->enj', h, exp_Wg) + exp_bg[:, None, :]) * h
            eo = jnp.einsum('eni,eih->enh', h, exp_Wdown) + exp_bdown[:, None, :]
            combined = jnp.einsum('ne,enh->nh', weights, eo)
            s = (xf @ share_Wup + share_bup).reshape(-1, NS, I)
            s = jax.nn.silu(s @ share_Wg + share_bg) * s
            share_out = (s @ share_Wdown + share_bdown).sum(axis=1)
            z = combined + share_out
            y = residual + z
            y = y * jax.lax.rsqrt(jnp.mean(y * y, axis=-1, keepdims=True) + EPS) * norm_w[j]
            xf = y
        return xf.reshape(B, S, Hd)
    x = _layernorm(x + _L0_attn_ref(x, L0_attn_W_in, L0_attn_W_out, L0_attn_dt_bias, L0_attn_B_bias, L0_attn_C_bias, L0_attn_B_norm_w, L0_attn_C_norm_w, L0_attn_D_param), axis=-1)
    x = _layernorm(x + _L0_xattn_ref(x, ctx_768, L0_xattn_Wq, L0_xattn_bq, L0_xattn_Wkv, L0_xattn_bkv, L0_xattn_Wo, L0_xattn_bo), axis=-1)
    x = _layernorm(x + _L0_ffn_ref(x, L0_ffn_gate_w, L0_ffn_w1, L0_ffn_b1, L0_ffn_w2, L0_ffn_b2), axis=-1)
    x = _layernorm(x + _L1_attn_ref(x, L1_attn_Wq, L1_attn_bq, L1_attn_Wk, L1_attn_bk, L1_attn_Wv, L1_attn_bv, L1_attn_Wo, L1_attn_bo, L1_attn_et_gate, L1_attn_is_gate, L1_attn_time_bias), axis=-1)
    x = _layernorm(x + _L1_xattn_ref(x, ctx_768, mask_BxS_bf1, mask_BxS2_bf1, L1_xattn_Wq, L1_xattn_Wk, L1_xattn_Wv, L1_xattn_W_film_in, L1_xattn_b_film_in, L1_xattn_W_film_out, L1_xattn_b_film_out, L1_xattn_g_norm_in, L1_xattn_b_norm_in, L1_xattn_g_norm_out, L1_xattn_b_norm_out, L1_xattn_g_ffn, L1_xattn_b_ffn, L1_xattn_W1, L1_xattn_b1, L1_xattn_W2, L1_xattn_b2, L1_xattn_log_dt, L1_xattn_A_re, L1_xattn_A_im, L1_xattn_C_re, L1_xattn_C_im, L1_xattn_D_skip, L1_xattn_mod_gate), axis=-1)
    x = _layernorm(x + _L1_ffn_ref(x, L1_ffn_router_W, L1_ffn_router_b, L1_ffn_gate_bias, L1_ffn_exp_Wup, L1_ffn_exp_bup, L1_ffn_exp_Wg, L1_ffn_exp_bg, L1_ffn_exp_Wdown, L1_ffn_exp_bdown, L1_ffn_share_Wup, L1_ffn_share_bup, L1_ffn_share_Wg, L1_ffn_share_bg, L1_ffn_share_Wdown, L1_ffn_share_bdown, L1_ffn_norm_w), axis=-1)
    return x

_drawn_inputs = setup_inputs


def setup_inputs(seed=0):
    import zlib

    import numpy as np

    out = dict(_drawn_inputs(seed))
    spreads = {'L0_attn_B_bias': (1.0, 0.6),
     'L0_attn_C_bias': (1.0, 0.6),
     'L0_attn_B_norm_w': (1.0, 0.6),
     'L0_attn_C_norm_w': (1.0, 0.6),
     'L0_attn_D_param': (1.0, 0.6),
     'L1_attn_bq': (0.0, 0.8),
     'L1_attn_bk': (0.0, 2.0),
     'L1_attn_bv': (0.0, 0.305),
     'L1_attn_bo': (0.0, 0.1),
     'L1_xattn_b_film_in': (0.0, 0.1),
     'L1_xattn_b_film_out': (0.0, 0.282),
     'L1_xattn_g_norm_in': (1.0, 0.2),
     'L1_xattn_b_norm_in': (0.0, 0.1),
     'L1_xattn_g_norm_out': (1.0, 0.2),
     'L1_xattn_b_norm_out': (0.0, 0.1),
     'L1_xattn_g_ffn': (1.0, 0.6),
     'L1_xattn_b_ffn': (0.0, 0.8),
     'L1_xattn_b1': (0.0, 0.8),
     'L1_xattn_b2': (0.0, 0.288),
     'L1_xattn_A_re': (-0.5, 0.2),
     'L1_ffn_exp_bup': (0.0, 0.8),
     'L1_ffn_exp_bg': (0.0, 0.8),
     'L1_ffn_exp_bdown': (0.0, 0.392),
     'L1_ffn_share_bup': (0.0, 0.8),
     'L1_ffn_share_bg': (0.0, 0.8),
     'L1_ffn_share_bdown': (0.0, 0.1),
     'L1_ffn_norm_w': (1.0, 0.2)}
    factors = {'L0_xattn_bq': 8.0,
     'L0_xattn_bkv': 4.698,
     'L0_xattn_bo': 5.61,
     'L0_ffn_b1': 4.253,
     'L0_ffn_b2': 2.819,
     'L1_attn_Wq': 8.0,
     'L1_attn_Wk': 8.0,
     'L1_attn_time_bias': 8.0,
     'L1_xattn_Wq': 8.0,
     'L1_xattn_Wk': 8.0,
     'L1_xattn_Wv': 5.071,
     'L1_xattn_W_film_in': 5.959,
     'L1_xattn_W_film_out': 8.0,
     'L1_xattn_W1': 3.621,
     'L1_xattn_W2': 3.377,
     'L1_ffn_router_b': 5.044,
     'L1_ffn_gate_bias': 4.08,
     'L1_ffn_exp_Wup': 8.0,
     'L1_ffn_exp_Wg': 8.0,
     'L1_ffn_exp_Wdown': 8.0,
     'L1_ffn_share_Wup': 8.0,
     'L1_ffn_share_Wg': 8.0,
     'L1_ffn_share_Wdown': 8.0}
    for name, (base, spread) in spreads.items():
        noise = np.random.default_rng([zlib.crc32(name.encode()), seed]).standard_normal(out[name].shape)
        drawn = base * np.exp(spread * noise) if base else spread * noise
        out[name] = jnp.asarray(drawn.astype(out[name].dtype))
    for name, factor in factors.items():
        out[name] = (out[name] * factor).astype(out[name].dtype)
    return out
```

```python
from contextlib import ExitStack

import numpy as np

import concourse.bass as bass
from concourse import mybir

F32 = mybir.dt.float32
U8 = mybir.dt.uint8
BF16 = mybir.dt.bfloat16
I32 = mybir.dt.int32
ALU = mybir.AluOpType
ACT = mybir.ActivationFunctionType
AX = mybir.AxisListType.X

B, S, D = 4, 512, 128
M, DC = 154, 96
P = 128
T = S // P
MT_, MR = P, M - P
RB = 32
MP = MT_ + RB
HM, PD, NS = 4, 64, 128
NA = 32
WIN = 2 * HM * PD + 2 * NS + 3 * HM + NA
NH, DH, HG = 16, 8, 4
E0, FF = 8, 512
FT = FF // P
EXPERT = FF + FT + FF
XH, XD, TOPK = 4, 32, 32
NST = 64
JL, IL = 32, 16
NF = 2 * S
E1, HOPS, NSH = 6, 2, 2
TBL = 500
RW = S + P * (T - 1)

EPS5, EPS6 = 1e-5, 1e-6
MAGIC = 12582912.0
INV2PI = float(1.0 / (2.0 * np.pi))
TURN = 6.283185
FAR = -1.0e30
TAKEN = -3.0e38
PI = float(np.pi)
LN2 = float(np.log(2.0))
LN2_HIGH = 0.693359375
LOG_LEAST, LOG_MOST = -87.0, 88.0
SERIES = [1.0, 1.0, 1 / 2, 1 / 6, 1 / 24, 1 / 120, 1 / 720, 1 / 5040]
EXP_BIAS, EXP_UNIT = 127.0, float(2 ** 23)


def columns():
    widths = [
        ("x0_bq", 1), ("x0_bk", 1), ("x0_bv", 1), ("x0_bo", 1),
        ("f0_b2", E0),
        ("a1_bq", 1), ("a1_bk", 1), ("a1_bv", 1), ("a1_bo", 1),
        ("x1_fin", 2), ("x1_fout", 2), ("x1_gin", 1), ("x1_bin", 1), ("x1_gout", 1), ("x1_bout", 1),
        ("x1_gffn", 1), ("x1_bffn", 1), ("x1_b1", FT), ("x1_b2", 1), ("x1_dskip", 1),
        ("f1_bup", E1), ("f1_bg", E1), ("f1_sup_b", NSH), ("f1_sg", 1), ("f1_sdown", 1),
        ("f1_norm", HOPS), ("m_dcol", 2), ("one", 1), ("sign", 1), ("phase", 1), ("phase2", 1),
        ("eps5", 1), ("eps6", 1), ("oneD", 1), ("half_pi", 1),
    ]
    at, out = 0, {}
    for name, w in widths:
        out[name] = (at, w)
        at += w
    return out, at


COL, NCOL = columns()


def rows():
    widths = [
        ("m_bias8", 2 * HM), ("m_bbias", HM * NS), ("m_cbias", HM * NS), ("m_bnw", NS), ("m_cnw", NS),
        ("et_gate", 1), ("is_gate", 1), ("mod_gate", 1), ("log_dt", D),
        ("f1_rb", HOPS * E1), ("f1_gb", HOPS * E1), ("jrow", JL), ("irow", IL),
    ]
    at, out = 0, {}
    for name, w in widths:
        out[name] = (at, w)
        at += w
    return out, at


ROW, NROW = rows()


def shape_constants():
    p = np.arange(P)
    ident = np.eye(P)
    centre = np.eye(P) - 1.0 / P
    upper = (p[:, None] <= p[None, :])
    ones = np.ones((P, P))
    shift = (p[:, None] == p[None, :] + 1)
    shift_last = np.zeros((P, P))
    shift_last[0, P - 1] = 1.0
    masked = np.where(upper, 0.0, FAR)
    headmask = ((p[:, None] % 32) // DH == np.arange(HG)[None, :])
    colmask = np.zeros((P, HG, P))
    colmask[:] = headmask.T[None]
    colmask_dj = colmask.reshape(P, HG, 4, HG, DH).transpose(0, 1, 2, 4, 3)
    restmask = colmask * (p[:, None, None] // RB == p[None, None, :] // 32)
    square = np.stack([ident, centre, upper, ones, shift, shift_last, masked], 1)
    small = np.concatenate([square.reshape(P, -1), headmask, colmask.reshape(P, -1),
                            restmask.reshape(P, -1), colmask_dj.reshape(P, -1)], 1).astype(np.float32)
    freq = (2 * np.arange(S) + 1)
    phi = (freq[:, None] * np.arange(S)[None, :]) % (4 * S)
    phi = phi * (np.pi / (2 * S))
    fwd = np.concatenate([np.cos(phi), -np.sin(phi)], 0)
    inv = fwd / S
    fwd = fwd.reshape(NF, T, P).transpose(2, 1, 0)
    inv = inv.reshape(NF // P, P, S).transpose(1, 0, 2)
    return small, np.ascontiguousarray(fwd, np.float32), np.ascontiguousarray(inv, np.float32)


NSMALL = 7 * P + HG + 3 * HG * P


def semaphores(nc, stack, prefix, names):
    return {n: stack.enter_context(nc.semaphore(f"{prefix}_{n}")) for n in names.split()}


def chained(eng, sem):
    count = [0]

    def link(ins):
        count[0] += 1
        ins.then_inc(sem, 1)
        eng.wait_ge(sem, count[0])

    return link


NORM_SEMS = "y tr st ag ready root rs ap back out"


def norm_names(*tags):
    return " ".join(f"{tag}_{n}" for tag in tags for n in NORM_SEMS.split())


LN_HALF = S // 2


def norm_tiles(nc, stack, tag):
    def sb(name, shape):
        return stack.enter_context(nc.sbuf_tensor(f"{tag}_{name}", shape, F32))
    return {"y": sb("norm_y", [P, S]), "yt": sb("norm_yt", [P, S]), "st": sb("norm_st", [P, T, 6]),
            "mv": sb("norm_mv", [P, T, 2]), "x": sb("norm_x", [P, T]), "h": sb("norm_h", [P, T]),
            "rs": sb("norm_rs", [P, T]), "nm": sb("norm_nm", [P, T]),
            "early": sb("norm_early", [P, 1])}


def norm_of(K, L, s, tag, there, back, out, centred=True, scale=None, shift=None, eps="eps5"):
    n = {name: s[f"{tag}_{name}"] for name in NORM_SEMS.split()}
    n.update(K=K, L=L, there=there, home=back, to=out, centred=centred, scale=scale, shift=shift, eps=eps)
    return n


def norm_tensor(eng, ps, n):
    L, ident = n["L"], n["K"]["ident"]
    for h in range(2):
        eng.wait_ge(n["y"], h + 1)
        for t in range(2):
            tok = h * LN_HALF + t * P
            mm = eng.transpose(ps[:, n["there"][h], t * P:(t + 1) * P], L["y"][:, tok:tok + P], ident)
        mm.then_inc(n["tr"], 1)
    for h in range(2):
        eng.wait_ge(n["ap"], 2 * h + 2)
        for t in range(2):
            tok = h * LN_HALF + t * P
            mm = eng.transpose(ps[:, n["home"][h], t * P:(t + 1) * P], L["yt"][:, tok:tok + P], ident)
        mm.then_inc(n["back"], 1)


def norm_scalar(eng, ps, n):
    L = n["L"]
    eng.activation(L["early"][:, :], n["K"]["one"], ACT.Sqrt)
    if n["centred"]:
        eng.wait_ge(n["ag"], T)
    else:
        eng.wait_ge(n["ready"], 2)
    eng.activation(L["h"][:, :], L["mv"][:, :, 1] if n["centred"] else L["x"][:, :], ACT.Sqrt,
                   bias=n["K"][n["eps"]]).then_inc(n["root"], 1)
    eng.wait_ge(n["rs"], 2 if n["centred"] else 1)
    eng.wait_ge(n["ap"], 2)
    for t in range(2):
        tok = LN_HALF + t * P
        src = ps[:, n["there"][1], t * P:(t + 1) * P]
        if n["centred"]:
            a = eng.activation(L["yt"][:, tok:tok + P], src, ACT.Identity, scale=L["rs"][:, 2 + t:3 + t],
                               bias=L["nm"][:, 2 + t:3 + t])
        else:
            a = eng.activation(L["yt"][:, tok:tok + P], src, ACT.Copy, scale=L["rs"][:, 2 + t:3 + t])
        a.then_inc(n["ap"], 1)
    eng.wait_ge(n["back"], 2)
    src, dst = ps[:, n["home"][1], 0:LN_HALF], n["to"][:, LN_HALF:S]
    if n["scale"] is None:
        a = eng.activation(dst, src, ACT.Copy)
    elif n["shift"] is None:
        a = eng.activation(dst, src, ACT.Copy, scale=n["scale"])
    else:
        a = eng.activation(dst, src, ACT.Identity, scale=n["scale"], bias=n["shift"])
    a.then_inc(n["out"], 1)


def norm_vector(eng, ps, n, put_y):
    L = n["L"]
    x, rs, mean, var = L["x"][:, :], L["rs"][:, :], L["mv"][:, :, 0], L["mv"][:, :, 1]
    for h in range(2):
        put_y(h).then_inc(n["y"], 1)
    for i in range(T):
        if i % 2 == 0:
            eng.wait_ge(n["tr"], i // 2 + 1)
        eng.bn_stats(L["st"][:, i, :], ps[:, n["there"][i // 2], (i % 2) * P:(i % 2 + 1) * P]).then_inc(n["st"], 1)
    for i in range(T):
        eng.wait_ge(n["st"], i + 1)
        eng.bn_aggr(L["mv"][:, i, :], L["st"][:, i, :]).then_inc(n["ag"], 1)
    eng.wait_ge(n["ag"], T)
    if not n["centred"]:
        eng.tensor_tensor(x, mean, mean, ALU.mult).then_inc(n["ready"], 1)
        eng.wait_ge(n["ready"], 1)
        eng.tensor_tensor(x, x, var, ALU.add).then_inc(n["ready"], 1)
    eng.wait_ge(n["root"], 1)
    eng.reciprocal(rs, L["h"][:, :]).then_inc(n["rs"], 1)
    eng.wait_ge(n["rs"], 1)
    if n["centred"]:
        eng.scalar_tensor_tensor(L["nm"][:, :], mean, -1.0, rs, ALU.mult, ALU.mult).then_inc(n["rs"], 1)
    for t in range(2):
        src = ps[:, n["there"][0], t * P:(t + 1) * P]
        if n["centred"]:
            i = eng.tensor_scalar(L["yt"][:, t * P:(t + 1) * P], src, L["mv"][:, t, 0:1], L["rs"][:, t:t + 1],
                                  ALU.subtract, ALU.mult)
        else:
            i = eng.tensor_scalar(L["yt"][:, t * P:(t + 1) * P], src, L["rs"][:, t:t + 1], None, ALU.mult)
        i.then_inc(n["ap"], 1)
    eng.wait_ge(n["back"], 1)
    src, dst = ps[:, n["home"][0], 0:LN_HALF], n["to"][:, 0:LN_HALF]
    if n["scale"] is None:
        i = eng.tensor_copy(dst, src)
    elif n["shift"] is None:
        i = eng.tensor_scalar(dst, src, n["scale"], None, ALU.mult)
    else:
        i = eng.tensor_scalar(dst, src, n["scale"], n["shift"], ALU.mult, ALU.add)
    i.then_inc(n["out"], 1)
    eng.wait_ge(n["out"], 2)



ROWS = 9 * DH
STACKED = 16 * 4
SPLIT_STEPS = 4
STACK_SEMS = "qf kf qs ks kept j0 j1 j2 j3 "


def split(eng, parts, x, sem):
    eng.tensor_copy(parts[:, 0, :], x[:, :]).then_inc(sem, 1)
    eng.wait_ge(sem, 1)
    eng.tensor_tensor(x[:, :], x[:, :], parts[:, 0, :], ALU.subtract).then_inc(sem, 1)
    eng.wait_ge(sem, 2)
    eng.tensor_copy(parts[:, 1, :], x[:, :]).then_inc(sem, 1)
    eng.wait_ge(sem, 3)
    eng.tensor_tensor(parts[:, 2, :], x[:, :], parts[:, 1, :], ALU.subtract).then_inc(sem, 1)


def split_scalar(eng, parts, x, sem):
    eng.activation(parts[:, 0, :], x[:, :], ACT.Copy).then_inc(sem, 1)
    eng.wait_ge(sem, 2)
    eng.activation(parts[:, 1, :], x[:, :], ACT.Copy).then_inc(sem, 1)


def split_vector(eng, parts, x, sem):
    eng.wait_ge(sem, 1)
    eng.tensor_tensor(x[:, :], x[:, :], parts[:, 0, :], ALU.subtract).then_inc(sem, 1)
    eng.wait_ge(sem, 3)
    eng.tensor_tensor(parts[:, 2, :], x[:, :], parts[:, 1, :], ALU.subtract).then_inc(sem, 1)


def stack_parts(eng, s, parts, stacks, dram):
    qs, ks = stacks
    for i, sem in enumerate(("qs", "ks")):
        eng.wait_ge(s[sem], SPLIT_STEPS)
        eng.dma_start(dram[i].rearrange("a p t -> p a t"), parts[i][:, :, :]).then_inc(s["kept"], 16)
    eng.wait_ge(s["kept"], 32)
    nq, nk = qs.shape[2], ks.shape[2]
    for j in range(HG):
        for b in range(3):
            eng.dma_start(ks[3 * DH * b:3 * DH * (b + 1), HG * j:HG * j + HG, :],
                          bass.AP(dram[1].tensor, HG * j * nk + b * P * nk, [[0, 3], [NH * nk, DH], [1, HG * nk]]))\
               .then_inc(s[f"j{j}"], 16)
        eng.dma_start(qs[:, HG * j:HG * j + HG, :],
                      bass.AP(dram[0].tensor, HG * j * nq, [[0, 3], [NH * nq, 3 * DH], [1, HG * nq]]))\
           .then_inc(s[f"j{j}"], 16)



A_SEMS = ("proj small xtok ssq bnsd rstd ne ex ln1 adt q ang qc w theta trig cosr bh ch hdec cumbc "
          "ltd ltm e1 le lw xw btr ctr bt ct cg cb mt y st hst zx zr tg out chain achain pchain " + norm_names("post"))


def mixer(nc, K, ps, X, s):
    with ExitStack() as stack:
        def sb(name, shape):
            return stack.enter_context(nc.sbuf_tensor(f"mix_{name}", shape, F32))
        L = norm_tiles(nc, stack, "mix")
        post = norm_of(K, L, s, "post", (7, 5), (3, 4), X)
        xtok = sb("xtok", [P, T, HM * PD])
        small = sb("small", [P, T, 3 * HM + NA])
        spx = sb("spx", [P, T, 2 * HM])
        ne = sb("ne", [P, T, 3 * HM])
        ex = sb("ex", [P, T, 3 * HM])
        ln1 = sb("ln1", [P, T, 2 * HM])
        spt = sb("spt", [P, T, 2 * HM])
        lam = sb("lam", [P, T, HM])
        adt = sb("adt", [P, T, HM])
        v = sb("v", [P, T, HM])
        q = sb("q", [P, T, HM])
        nqs = sb("nqs", [P, T, HM])
        w = sb("w", [P, T, HM])
        cum = sb("cum", [P, T, HM])
        fend = sb("fend", [P, T, HM])
        ssq = sb("ssq", [P, 2, T])
        rsd = sb("rsd", [P, 2, T])
        ang = sb("ang", [P, T, HM, NA])
        frac = sb("frac", [P, T * HM, NA])
        sn = sb("sn", [P, T * HM, NA])
        co = sb("co", [P, T * HM, NA])
        bn = sb("bn", [P, 2, T, NS])
        bh = sb("bh", [P, T, HM, NS])
        ch = sb("ch", [P, T, HM, NS])
        e1 = sb("e1", [P, T, HM, P])
        lw = sb("lw", [P, T, HM, P])
        dg = sb("dg", [P, T, HM, P])
        bt = sb("bt", [P, T, HM, P])
        ct = sb("ct", [P, T, HM, P])
        junk = bt[:, :, 0:2, :].rearrange("p t h n -> p t h n")
        tb = [lw[:, i, :, :].rearrange("p h (g a) -> p (h g) a", a=NA) for i in range(T)]
        tc = [ct[:, i, :, :].rearrange("p h (g a) -> p (h g) a", a=NA) for i in range(T)]
        cg = ch
        xw = sb("xw", [P, T, HM * PD])
        hst = sb("hst", [P, HM, PD])
        hdec = sb("hdec", [P, HM, PD])
        zr = sb("zr", [P, 2, S])
        xd = sb("xd", [P, 2, S])
        win, wout = K["m_win"], K["m_wout"]
        dt = spt[:, :, 0:HM]
        NB2 = 2 * HM * PD

        block = stack.enter_context(nc.Block(no_gpsimd_drain=True))

        @block.sync
        def _(eng):
            eng.wait_ge(*K["weights_in"])

        @block.tensor
        def _(eng):
            for t in range(T):
                eng.matmul(ps[:, t, :], X[:, t * P:(t + 1) * P], win[:, 256:768], start=True, stop=True)\
                   .then_inc(s["proj"], 1)
            for t in range(T):
                n = 3 * HM + NA
                mm = eng.matmul(ps[:, 4, t * n:(t + 1) * n], X[:, t * P:(t + 1) * P], win[:, 768:WIN],
                                start=True, stop=True)
            mm.then_inc(s["small"], 1)
            for k in range(2):
                eng.matmul(ps[:, 6 + k, :], win[:, k * P:(k + 1) * P], X[:, :], start=True, stop=True)\
                   .then_inc(s["zx"], 1)
            for k in range(2):
                eng.wait_ge(s["zr"], k + 1)
                eng.matmul(ps[:, 6 + k, :], win[:, (2 + k) * P:(3 + k) * P], X[:, :], start=True, stop=True)\
                   .then_inc(s["zx"], 1)
            eng.wait_ge(s["q"], 1)
            qf = q[:, :, :].rearrange("p t h -> p (t h)")
            nq = T * HM
            eng.matmul(ps[:, 4, 192:192 + nq], K["shift"], qf, start=True, stop=False)
            eng.matmul(ps[:, 4, 192:192 + nq - HM], K["shift_last"], qf[:, HM:nq], start=False, stop=True)
            eng.wait_ge(s["adt"], 1)
            eng.matmul(ps[:, 4, 208:208 + nq], K["upper"], adt[:, :, :].rearrange("p t h -> p (t h)"),
                       start=True, stop=True).then_inc(s["qc"], 1)
            eng.wait_ge(s["ang"], 1)
            af = ang[:, :, :, :].rearrange("p t h a -> p (t h a)")
            eng.matmul(ps[:, 5, :], K["upper"], af, start=True, stop=False)
            for back in range(1, T):
                mm = eng.matmul(ps[:, 5, back * P:S], K["ones"], af[:, 0:S - back * P], start=False,
                                stop=(back == T - 1))
            mm.then_inc(s["theta"], 1)

            def sums_and_transposes(c):
                if c == 0:
                    eng.wait_ge(s["trig"], 1)
                else:
                    eng.wait_ge(s["e1"], c)
                    eng.wait_ge(s["ltd"], c)
                for h in range(HM):
                    mm = eng.matmul(ps[:, 5, h * P:(h + 1) * P], adt[:, c, h:h + 1].to_broadcast([P, P]),
                                    K["upper"], start=True, stop=True)
                mm.then_inc(s["cumbc"], 1)
                if c == 0:
                    eng.wait_ge(s["bh"], T + 6)
                    eng.wait_ge(s["xtok"], T)
                else:
                    eng.wait_ge(s["bt"], c)
                for h in range(HM):
                    mm = eng.transpose(ps[:, 2, h * P:(h + 1) * P], bh[:, c, h, :], K["ident"])
                mm.then_inc(s["btr"], 1)
                if c == 0:
                    eng.wait_ge(s["ch"], T + 6)
                else:
                    eng.wait_ge(s["ct"], c)
                    eng.wait_ge(s["cg"], c)
                for h in range(HM):
                    mm = eng.transpose(ps[:, 3, h * P:(h + 1) * P], ch[:, c, h, :], K["ident"])
                mm.then_inc(s["ctr"], 1)

            def scores(c):
                eng.wait_ge(s["bt"], c + 1)
                eng.wait_ge(s["ct"], c + 1)
                if c == 0:
                    eng.wait_ge(s["zr"], 4)
                else:
                    eng.wait_ge(s["mt"], c)
                for h in range(HM):
                    mm = eng.matmul(ps[:, 6, h * P:(h + 1) * P], bt[:, c, h, :], ct[:, c, h, :],
                                    start=True, stop=True)
                mm.then_inc(s["cb"], 1)

            def outputs(c):
                eng.wait_ge(s["mt"], c + 1)
                if c > 0:
                    eng.wait_ge(s["cg"], c + 1)
                    eng.wait_ge(s["hst"], c)
                for h in range(HM):
                    o = ps[64 * (h % 2):64 * (h % 2) + 64, h // 2, c * P:(c + 1) * P]
                    mm = eng.matmul(o, xtok[:, c, h * PD:(h + 1) * PD], lw[:, c, h, :], start=True,
                                    stop=(c == 0))
                    if c > 0:
                        mm = eng.matmul(o, hst[:, h, :], cg[:, c, h, :], start=False, stop=True)
                mm.then_inc(s["y"], 1)
                if c < T - 1:
                    eng.wait_ge(s["xw"], c + 1)
                    for h in range(HM):
                        mm = eng.matmul(ps[:, 4, 256 + h * PD:256 + (h + 1) * PD], bh[:, c, h, :],
                                        xw[:, c, h * PD:(h + 1) * PD], start=True, stop=True)
                    mm.then_inc(s["st"], 1)

            for c in range(T):
                sums_and_transposes(c)
                if c > 0:
                    outputs(c - 1)
                scores(c)
            outputs(T - 1)
            for h in range(2):
                cols = slice(h * LN_HALF, (h + 1) * LN_HALF)
                eng.wait_ge(s["tg"], 2 * h + 2)
                for k in range(2):
                    mm = eng.matmul(ps[:, (2, 6)[h], 0:LN_HALF], wout[:, k, :], zr[:, k, cols], start=(k == 0),
                                    stop=(k == 1))
                mm.then_inc(s["out"], 1)
            norm_tensor(eng, ps, post)

        @block.scalar
        def _(eng):
            link = chained(eng, s["achain"])
            for t in range(T):
                eng.wait_ge(s["proj"], t + 1)
                eng.activation(xtok[:, t, :], ps[:, t, 0:256], ACT.Copy).then_inc(s["xtok"], 1)
                for k in range(2):
                    a = eng.activation(junk[:, t, k, :], ps[:, t, 256 + k * NS:256 + (k + 1) * NS],
                                       ACT.Square, accum_out=ssq[:, k, t:t + 1])
                    a.then_inc(s["ssq"], 1)
            eng.wait_ge(s["ssq"], 2 * T)
            link(eng.activation(ssq[:, :, :], ssq[:, :, :], ACT.Sqrt, bias=K["eps5"], scale=1.0 / NS))
            eng.wait_ge(s["zx"], 2)
            for k in range(2):
                eng.activation(zr[:, k, :], ps[:, 6 + k, :], ACT.Copy).then_inc(s["zr"], 1)
            eng.wait_ge(s["ne"], 1)
            eng.activation(ex[:, :, :], ne[:, :, :], ACT.Exp).then_inc(s["ex"], 1)
            eng.wait_ge(s["ex"], 1)
            eng.activation(ln1[:, :, :], ex[:, :, 0:2 * HM], ACT.Ln, bias=K["one"]).then_inc(s["ln1"], 1)
            for k in range(2):
                eng.wait_ge(s["zx"], 3 + k)
                eng.activation(xd[:, k, :], ps[:, 6 + k, :], ACT.Copy, scale=K["m_dcol"][:, k:k + 1])\
                   .then_inc(s["zr"], 1)
            eng.wait_ge(s["trig"], 1)
            eng.activation(sn[:, :, :], frac[:, :, :], ACT.Sin, scale=TURN).then_inc(s["cosr"], 1)
            eng.activation(co[:, :, :], frac[:, :, :], ACT.Sin, scale=TURN / 2).then_inc(s["cosr"], 1)
            for c in range(T):
                eng.wait_ge(s["cumbc"], c + 1)
                eng.activation(e1[:, c, :, :], ps[:, 5, :].rearrange("p (h t) -> p h t", h=HM), ACT.Exp)\
                   .then_inc(s["e1"], 1)
                eng.wait_ge(s["ltm"], c + 1)
                eng.activation(lw[:, c, :, :], lw[:, c, :, :], ACT.Exp).then_inc(s["le"], 1)
                eng.wait_ge(s["btr"], c + 1)
                eng.activation(bt[:, c, :, :], ps[:, 2, :].rearrange("p (h t) -> p h t", h=HM), ACT.Copy)\
                   .then_inc(s["bt"], 1)
                eng.wait_ge(s["ctr"], c + 1)
                eng.activation(ct[:, c, :, :], ps[:, 3, :].rearrange("p (h t) -> p h t", h=HM), ACT.Copy)\
                   .then_inc(s["ct"], 1)
            eng.wait_ge(s["zr"], 4)
            link(eng.activation(zr[:, :, :], zr[:, :, :], ACT.Silu))
            norm_scalar(eng, ps, post)

        @block.gpsimd
        def _(eng):
            link = chained(eng, s["pchain"])
            eng.wait_ge(s["w"], 1)
            for c in range(T):
                eng.tensor_tensor(dg[:, c, :, :], K["ident"].unsqueeze(1).to_broadcast([P, HM, P]),
                                  nqs[:, c, :].unsqueeze(2).to_broadcast([P, HM, P]), ALU.mult)\
                   .then_inc(s["pchain"], 1)
            eng.wait_ge(s["cosr"], 2)
            eng.tensor_tensor(co[:, :, :], co[:, :, :], co[:, :, :], ALU.mult).then_inc(s["cosr"], 1)
            eng.wait_ge(s["cosr"], 3)
            eng.tensor_scalar(co[:, :, :], co[:, :, :], -2.0, 1.0, ALU.mult, ALU.add).then_inc(s["cosr"], 1)
            eng.wait_ge(s["cosr"], 4)
            eng.wait_ge(s["ch"], T)
            rotate(eng, ch, tc, sn, co, s["ch"], T)
            for c in range(T):
                wb = w[:, c, :].unsqueeze(2)
                eng.wait_ge(s["ltd"], c + 1)
                eng.tensor_tensor(lw[:, c, :, :], lw[:, c, :, :],
                                  K["masked"].unsqueeze(1).to_broadcast([P, HM, P]), ALU.add)\
                   .then_inc(s["ltm"], 1)
                eng.wait_ge(s["le"], c + 1)
                eng.tensor_tensor(fend[:, c, :], lw[:, c, :, P - 1], w[:, c, :], ALU.mult)\
                   .then_inc(s["xw"], 1)
                eng.wait_ge(s["xw"], 2 * c + 1)
                eng.tensor_tensor(lw[:, c, :, :], lw[:, c, :, :], wb.to_broadcast([P, HM, P]), ALU.mult)\
                   .then_inc(s["lw"], 1)
                eng.tensor_tensor(xw[:, c, :].rearrange("p (h d) -> p h d", h=HM),
                                  xtok[:, c, :].rearrange("p (h d) -> p h d", h=HM),
                                  fend[:, c, :].unsqueeze(2).to_broadcast([P, HM, PD]), ALU.mult)\
                   .then_inc(s["xw"], 1)
                eng.wait_ge(s["lw"], 2 * c + 1)
                eng.wait_ge(s["pchain"], T)
                eng.tensor_tensor(lw[:, c, :, :], lw[:, c, :, :], dg[:, c, :, :], ALU.add)\
                   .then_inc(s["lw"], 1)

        @block.vector
        def _(eng):
            link = chained(eng, s["chain"])
            eng.wait_ge(s["small"], 1)
            link(eng.tensor_copy(small[:, :, :], ps[:, 4, 0:176].rearrange("p (t n) -> p t n", t=T)))
            link(eng.tensor_tensor(spx[:, :, :], small[:, :, 0:2 * HM],
                                   K["m_bias8"].unsqueeze(1).to_broadcast([P, T, 2 * HM]), ALU.add))
            link(eng.tensor_scalar(ne[:, :, 2 * HM:], small[:, :, 2 * HM:3 * HM], -1.0, None, ALU.mult))
            eng.scalar_tensor_tensor(ne[:, :, 0:2 * HM], spx[:, :, :], -1.0, spx[:, :, :], ALU.mult,
                                     ALU.min).then_inc(s["ne"], 1)
            eng.wait_ge(s["ln1"], 1)
            link(eng.scalar_tensor_tensor(spt[:, :, :], spx[:, :, :], 0.0, ln1[:, :, :], ALU.max, ALU.add))
            link(eng.tensor_scalar(lam[:, :, :], ex[:, :, 2 * HM:], 1.0, None, ALU.add))
            link(eng.reciprocal(lam[:, :, :], lam[:, :, :]))
            link(eng.tensor_scalar(adt[:, :, :], spt[:, :, HM:], 1e-4, -1.0, ALU.max, ALU.mult))
            eng.tensor_tensor(adt[:, :, :], adt[:, :, :], dt, ALU.mult).then_inc(s["adt"], 1)
            link(eng.tensor_tensor(v[:, :, :], dt, lam[:, :, :], ALU.mult))
            eng.tensor_tensor(q[:, :, :], dt, v[:, :, :], ALU.subtract).then_inc(s["q"], 1)
            eng.tensor_tensor(ang[:, :, :, :],
                              small[:, :, 3 * HM:].unsqueeze(2).to_broadcast([P, T, HM, NA]),
                              dt.unsqueeze(3).to_broadcast([P, T, HM, NA]), ALU.mult).then_inc(s["ang"], 1)
            eng.wait_ge(s["achain"], 1)
            eng.reciprocal(rsd[:, :, :], ssq[:, :, :]).then_inc(s["rstd"], 1)
            eng.wait_ge(s["rstd"], 1)
            for k, nw in ((0, "m_bnw"), (1, "m_cnw")):
                for t in range(T):
                    i = eng.scalar_tensor_tensor(bn[:, k, t, :], ps[:, t, 256 + k * NS:256 + (k + 1) * NS],
                                                 rsd[:, k, t:t + 1], K[nw], ALU.mult, ALU.mult)
                    i.then_inc(s["rstd"], 1)
            eng.wait_ge(s["rstd"], 1 + 2 * T)
            for k, (dst, bias, sem) in enumerate(((bh, "m_bbias", "bh"), (ch, "m_cbias", "ch"))):
                for t in range(T):
                    eng.tensor_tensor(dst[:, t, :, :], bn[:, k, t, :].unsqueeze(1).to_broadcast([P, HM, NS]),
                                      K[bias].rearrange("p (h n) -> p h n", h=HM), ALU.add)\
                       .then_inc(s[sem], 1)
            eng.wait_ge(s["qc"], 1)
            link(eng.tensor_scalar(nqs[:, :, :], ps[:, 4, 192:208].rearrange("p (t h) -> p t h", t=T), -1.0,
                                   None, ALU.mult))
            link(eng.tensor_copy(cum[:, :, :], ps[:, 4, 208:224].rearrange("p (t h) -> p t h", t=T)))
            eng.tensor_tensor(w[:, :, :], v[:, :, :], nqs[:, :, :], ALU.subtract).then_inc(s["w"], 1)
            eng.wait_ge(s["theta"], 1)
            th = ps[:, 5, :].rearrange("p (n a) -> p n a", a=NA)
            link(eng.tensor_scalar(frac[:, :, :], th, INV2PI, MAGIC, ALU.mult, ALU.add))
            link(eng.tensor_scalar(frac[:, :, :], frac[:, :, :], -MAGIC, None, ALU.add))
            eng.scalar_tensor_tensor(frac[:, :, :], th, INV2PI, frac[:, :, :], ALU.mult, ALU.subtract)\
               .then_inc(s["trig"], 1)
            eng.wait_ge(s["bh"], T)
            eng.wait_ge(s["cosr"], 4)
            rotate(eng, bh, tb, sn, co, s["bh"], T)
            for c in range(T):
                eng.wait_ge(s["e1"], c + 1)
                eng.tensor_tensor(lw[:, c, :, :], ps[:, 5, :].rearrange("p (h t) -> p h t", h=HM),
                                  cum[:, c, :].unsqueeze(2).to_broadcast([P, HM, P]), ALU.subtract)\
                   .then_inc(s["ltd"], 1)
                eng.wait_ge(s["ct"], c + 1)
                eng.tensor_tensor(cg[:, c, :, :], ps[:, 3, :].rearrange("p (h t) -> p h t", h=HM),
                                  e1[:, c, :, :], ALU.mult).then_inc(s["cg"], 1)
                if 0 < c:
                    state_update(eng, c - 1, s, ps, hst, hdec, e1)
                eng.wait_ge(s["lw"], 2 * c + 2)
                eng.wait_ge(s["cb"], c + 1)
                eng.tensor_tensor(lw[:, c, :, :], ps[:, 6, :].rearrange("p (h t) -> p h t", h=HM),
                                  lw[:, c, :, :], ALU.mult).then_inc(s["mt"], 1)
            eng.wait_ge(s["achain"], 2)
            for h in range(2):
                c = slice(h * LN_HALF, (h + 1) * LN_HALF)
                eng.wait_ge(s["y"], T)
                for k in range(2):
                    link(eng.tensor_tensor(xd[:, k, c], ps[:, k, c], xd[:, k, c], ALU.add))
                    eng.tensor_tensor(zr[:, k, c], xd[:, k, c], zr[:, k, c], ALU.mult).then_inc(s["tg"], 1)

            def sums(h):
                c = slice(h * LN_HALF, (h + 1) * LN_HALF)
                eng.wait_ge(s["out"], h + 1)
                return eng.tensor_tensor(L["y"][:, c], ps[:, (2, 6)[h], 0:LN_HALF], X[:, c], ALU.add)
            norm_vector(eng, ps, post, sums)


def state_update(eng, c, s, ps, hst, hdec, e1):
    new = ps[:, 4, 256:512].rearrange("p (h d) -> p h d", h=HM)
    eng.wait_ge(s["st"], c + 1)
    if c == 0:
        eng.tensor_copy(hst[:, :, :], new).then_inc(s["hst"], 1)
    else:
        eng.wait_ge(s["hst"], c)
        eng.tensor_tensor(hdec[:, :, :], hst[:, :, :],
                          e1[:, c, :, P - 1:P].to_broadcast([P, HM, PD]), ALU.mult).then_inc(s["hdec"], 1)
        eng.wait_ge(s["hdec"], c)
        eng.wait_ge(s["y"], c + 1)
        eng.tensor_tensor(hst[:, :, :], new, hdec[:, :, :], ALU.add).then_inc(s["hst"], 1)


def rotate(eng, vec, tmp, sn, co, sem, count):
    flat = vec[:, :, :, :].rearrange("p t h n -> p (t h) n")
    v1, v2 = flat[:, :, 0:NA], flat[:, :, NA:2 * NA]
    for out, a, b in ((tmp[0], v1, co), (tmp[1], v2, sn), (tmp[2], v1, sn), (tmp[3], v2, co)):
        eng.tensor_tensor(out, a, b[:, :, :], ALU.mult).then_inc(sem, 1)
    eng.wait_ge(sem, count + 4)
    eng.tensor_tensor(v1, tmp[0], tmp[1], ALU.subtract).then_inc(sem, 1)
    eng.tensor_tensor(v2, tmp[2], tmp[3], ALU.add).then_inc(sem, 1)
    eng.wait_ge(sem, count + 6)



B_SEMS = (STACK_SEMS + "proj vp bo pad sc mn p rest tm tr pt ptr pv rs rex rt rtb ot out chain achain "
          + norm_names("post"))


def cross0(nc, K, ps, X, s, parts_dram):
    with ExitStack() as stack:
        def sb(name, shape):
            return stack.enter_context(nc.sbuf_tensor(f"c0_{name}", shape, F32))
        L = norm_tiles(nc, stack, "c0")
        post = norm_of(K, L, s, "post", (2, 3), (5, 6), X)
        scale = float(DH) ** -0.5
        ctx = K["ctx"]

        def half(name, shape):
            return stack.enter_context(nc.sbuf_tensor(f"c0_{name}", shape, BF16))
        qf = sb("qf", [P, S])
        kf = sb("kf", [P, M])
        parts = [half("qparts", [P, 3, S]), half("kparts", [P, 3, M])]
        qs = half("qs", [ROWS, NH, S])
        ks = half("ks", [ROWS, NH, M])
        vp = sb("vp", [P, HG, P])
        vr = sb("vr", [P, HG, P])
        bo = sb("bo", [P, 1])
        mn = sb("mn", [P, 32, 2])
        p = sb("p", [P, 4, 2, MP])
        pr = sb("pr", [P, 2, 2, HG, RB])
        pt = sb("pt", [P, 2, HG, S])
        ptr = sb("ptr", [P, 2, S])
        rs = sb("rs", [P, T, NH])
        rex = sb("rex", [P, T, P])
        rt = sb("rt", [P, S])
        ot = sb("ot", [P, S])
        steps = [(j, qp, g) for j in range(HG) for qp in range(2) for g in range(4)]
        N = len(steps)
        block = stack.enter_context(nc.Block(no_gpsimd_drain=True))

        @block.tensor
        def _(eng):
            eng.matmul(ps[:, 0, :], K["x0_wq"][:, :], X[:, :], start=True, stop=True).then_inc(s["proj"], 1)
            eng.matmul(ps[:, 1, 0:M], K["x0_wk"][:, :], ctx[:, 0:M], start=True, stop=True)\
               .then_inc(s["proj"], 1)
            eng.matmul(ps[:, 2, 0:P], ctx[:, 0:P], K["x0_wv"][:, :], start=True, stop=True)\
               .then_inc(s["proj"], 1)
            for g in range(4):
                mm = eng.matmul(ps[32 * g:32 * g + 32, 3, 0:P], ctx[:, P:MP], K["x0_wv"][:, :],
                                start=True, stop=True)
            mm.then_inc(s["proj"], 1)
            eng.matmul(ps[:, 4, 0:1], K["x0_wo"][:, :], K["x0_bv"], start=True, stop=True)\
               .then_inc(s["proj"], 1)

            def scores(n):
                j, qp, g = steps[n]
                if n == 0:
                    eng.wait_ge(s["qf"], 1)
                    eng.wait_ge(s["kf"], 1)
                    eng.wait_ge(s["vp"], 2)
                if qp == 0 and g == 0:
                    eng.wait_ge(s[f"j{j}"], STACKED)
                if n >= 4:
                    eng.wait_ge(s["p"], n - 3)
                for i in range(2):
                    t = 2 * qp + i
                    mm = eng.matmul(ps[:, g, i * M:(i + 1) * M], qs[:, HG * j + g, t * P:(t + 1) * P],
                                    ks[:, HG * j + g, :], start=True, stop=True)
                mm.then_inc(s["sc"], 1)

            def turn(n):
                j, qp, g = steps[n]
                eng.wait_ge(s["p"], n + 1)
                if n == 0:
                    eng.wait_ge(s["bo"], 1)
                if n % 2 == 0 and n >= 4:
                    eng.wait_ge(s["pt"], n // 2 - 1)
                for i in range(2):
                    mm = eng.transpose(ps[:, 4 + (n // 2) % 2, (2 * (n % 2) + i) * P:(2 * (n % 2) + i + 1) * P],
                                       p[:, n % 4, i, 0:P], K["ident"])
                mm.then_inc(s["tm"], 1)
                if g == 3:
                    u = n // 4
                    eng.wait_ge(s["rest"], n + 1)
                    if u >= 1:
                        eng.wait_ge(s["ptr"], u)
                    for i in range(2):
                        mm = eng.transpose(ps[:, 6, i * P:(i + 1) * P],
                                           pr[:, u % 2, i, :, :].rearrange("p g m -> p (g m)"), K["ident"])
                    mm.then_inc(s["tr"], 1)

            def values(j):
                eng.wait_ge(s["pt"], 4 * j + 4)
                for g in range(4):
                    eng.matmul(ps[32 * g:32 * g + 32, 7, :], vp[:, j, 32 * g:32 * g + 32],
                               pt[:, j % 2, g, :], start=(j == 0), stop=False, skip_group_check=True)

            def values_rest(j):
                eng.wait_ge(s["ptr"], 2 * j + 2)
                eng.matmul(ps[:, 7, :], vr[:, j, :], ptr[:, j % 2, :], start=False, stop=(j == HG - 1),
                           skip_group_check=True).then_inc(s["pv"], 1)

            for n in range(4):
                scores(n)
            for n in range(N):
                if n + 4 < N:
                    scores(n + 4)
                turn(n)
                if n % 8 == 2 and n > 8:
                    values(n // 8 - 1)
                if n % 8 == 5 and n > 8:
                    values_rest(n // 8 - 1)
            values(HG - 1)
            values_rest(HG - 1)
            eng.wait_ge(s["rex"], 1)
            for t in range(T):
                mm = eng.transpose(ps[:, 4, t * P:(t + 1) * P], rex[:, t, :], K["ident"])
            mm.then_inc(s["rtb"], 1)
            for h in range(2):
                eng.wait_ge(s["ot"], h + 1)
                eng.matmul(ps[:, h, 0:LN_HALF], K["x0_wo"][:, :], ot[:, h * LN_HALF:(h + 1) * LN_HALF],
                           start=True, stop=True).then_inc(s["out"], 1)
            norm_tensor(eng, ps, post)

        @block.sync
        def _(eng):
            stack_parts(eng, s, parts, (qs, ks), parts_dram)

        @block.scalar
        def _(eng):
            eng.wait_ge(s["proj"], 2)
            eng.activation(kf[:, :], ps[:, 1, 0:M], ACT.Identity, bias=K["x0_bk"]).then_inc(s["kf"], 1)
            eng.wait_ge(s["kf"], 1)
            split_scalar(eng, parts[1], kf, s["ks"])

            def rest_back(u):
                j, qp, _ = steps[4 * u]
                eng.wait_ge(s["tr"], u + 1)
                if u >= 4:
                    eng.wait_ge(s["pv"], j - 1)
                eng.activation(ptr[:, j % 2, qp * 2 * P:(qp + 1) * 2 * P], ps[:, 6, 0:2 * P], ACT.Copy)\
                   .then_inc(s["ptr"], 1)

            for n, (j, qp, g) in enumerate(steps):
                eng.wait_ge(s["mn"], n + 1)
                if n == 0:
                    eng.wait_ge(s["pad"], 1)
                if n >= 4:
                    eng.wait_ge(s["tm"], n - 3)
                    eng.wait_ge(s["rest"], n - 3)
                for i in range(2):
                    t, h = 2 * qp + i, 4 * g + j
                    a = eng.activation(p[:, n % 4, i, 0:M], ps[:, g, i * M:(i + 1) * M], ACT.Exp,
                                       bias=mn[:, n, i:i + 1], scale=-1.0, accum_out=rs[:, t, h:h + 1])
                a.then_inc(s["p"], 1)
                if g == 1 and n > 4:
                    rest_back(n // 4 - 1)
            rest_back(N // 4 - 1)
            eng.wait_ge(s["rtb"], 1)
            eng.activation(rt[:, :], ps[:, 4, :], ACT.Copy).then_inc(s["rt"], 1)
            norm_scalar(eng, ps, post)

        @block.gpsimd
        def _(eng):
            eng.memset(p[:, :, :, M:MP], 0.0).then_inc(s["pad"], 1)
            eng.wait_ge(s["pad"], 1)
            for n, (j, qp, g) in enumerate(steps):
                u = n // 4
                eng.wait_ge(s["p"], n + 1)
                if g == 0 and u >= 2:
                    eng.wait_ge(s["tr"], u - 1)
                eng.tensor_copy(pr[:, u % 2, :, g, :], p[:, n % 4, :, P:MP]).then_inc(s["rest"], 1)

        @block.vector
        def _(eng):
            link = chained(eng, s["chain"])
            eng.wait_ge(s["proj"], 1)
            eng.tensor_scalar(qf[:, :], ps[:, 0, :], K["x0_bq"], -scale, ALU.add, ALU.mult).then_inc(s["qf"], 1)
            eng.wait_ge(s["qf"], 1)
            split(eng, parts[0], qf, s["qs"])
            eng.wait_ge(s["kf"], 1)
            split_vector(eng, parts[1], kf, s["ks"])
            for dst, bank, mask in ((vp, 2, "colmask"), (vr, 3, "restmask")):
                eng.wait_ge(s["proj"], bank + 1)
                eng.tensor_tensor(dst[:, :, :], ps[:, bank, 0:P].unsqueeze(1).to_broadcast([P, HG, P]),
                                  K[mask], ALU.mult).then_inc(s["vp"], 1)
            eng.wait_ge(s["proj"], 5)
            eng.tensor_tensor(bo[:, :], ps[:, 4, 0:1], K["x0_bo"], ALU.add).then_inc(s["bo"], 1)

            def minimum(n):
                j, qp, g = steps[n]
                eng.wait_ge(s["sc"], n + 1)
                eng.tensor_reduce(mn[:, n, :], ps[:, g, 0:2 * M].rearrange("p (i m) -> p i m", i=2), AX,
                                  ALU.min).then_inc(s["mn"], 1)

            def evacuate(k):
                j, qp, g = steps[2 * k]
                eng.wait_ge(s["tm"], 2 * k + 2)
                if j >= 2:
                    eng.wait_ge(s["pv"], j - 1)
                eng.tensor_copy(pt[:, j % 2, g:g + 2, qp * 2 * P:(qp + 1) * 2 * P],
                                ps[:, 4 + k % 2, :].rearrange("p (g q) -> p g q", g=2)).then_inc(s["pt"], 1)

            for n in range(N):
                minimum(n)
                if n % 2 == 1 and n >= 5:
                    evacuate((n - 5) // 2)
            evacuate(N // 2 - 2)
            evacuate(N // 2 - 1)
            eng.wait_ge(s["p"], N)
            link(eng.reciprocal(rs[:, :, :], rs[:, :, :]))
            eng.tensor_copy(rex[:, :, :].rearrange("p t (h d) -> p t h d", d=DH),
                            rs[:, :, :].unsqueeze(3).to_broadcast([P, T, NH, DH])).then_inc(s["rex"], 1)
            eng.wait_ge(s["rt"], 1)
            eng.wait_ge(s["pv"], HG)
            for h in range(2):
                c = slice(h * LN_HALF, (h + 1) * LN_HALF)
                eng.tensor_tensor(ot[:, c], ps[:, 7, c], rt[:, c], ALU.mult).then_inc(s["ot"], 1)

            def put_y(h):
                c = slice(h * LN_HALF, (h + 1) * LN_HALF)
                eng.wait_ge(s["out"], h + 1)
                return eng.scalar_tensor_tensor(L["y"][:, c], ps[:, h, 0:LN_HALF], bo[:, 0:1], X[:, c],
                                                ALU.add, ALU.add)
            norm_vector(eng, ps, post, put_y)



C_SEMS = ("mean logits pad m8 ee chosen w1 w2 hid g down acc chain " + norm_names("post"))


def experts0(nc, K, ps, X, s, experts):
    with ExitStack() as stack:
        def sb(name, shape):
            return stack.enter_context(nc.sbuf_tensor(f"e0_{name}", shape, F32))
        L = norm_tiles(nc, stack, "e0")
        post = norm_of(K, L, s, "post", (0, 1), (2, 3), X)
        xm = sb("xm", [P, 1])
        lg = sb("lg", [P, 2 * E0])
        m8 = sb("m8", [P, 8])
        rp = sb("rp", [P, 8])
        wk = sb("wk", [P, 2 * E0])
        nm = sb("nm", [P, 1])
        ee = sb("ee", [P, E0])
        cw = sb("cw", [P, E0])
        tot = sb("tot", [P, 1])
        be = sb("be", [P, 1])
        jk = sb("jk", [P, E0])
        sel = sb("sel", [P, E0])
        num = sb("num", [P, 2])
        numi = stack.enter_context(nc.sbuf_tensor("e0_numi", [P, 2], I32))
        cs = sb("cs", [P, 2])
        ew = sb("ew", [P, 2, EXPERT])
        g = sb("g", [P, 2 * FT, S])
        xb = sb("xb", [P, S])
        acc = sb("acc", [P, S])
        NU = 2 * FT
        block = stack.enter_context(nc.Block(no_gpsimd_drain=True))

        @block.sync
        def _(eng):
            eng.wait_ge(s["chosen"], 1)
            chosen = [eng.value_load(numi[0:1, i:i + 1], min_val=0, max_val=E0 - 1) for i in range(2)]
            for sem, part in (("w1", slice(0, FF + FT)), ("w2", slice(FF + FT, EXPERT))):
                for i in range(2):
                    eng.dma_start(ew[:, i, part], experts[chosen[i], :, part]).then_inc(s[sem], 16)

        @block.tensor
        def _(eng):
            eng.wait_ge(s["mean"], 1)
            eng.matmul(ps[:, 6, 0:E0], xm[:, 0:1].to_broadcast([P, P]), K["f0_gate"][:, :], start=True,
                       stop=True).then_inc(s["logits"], 1)
            eng.wait_ge(s["w1"], 32)

            def up(n):
                e, f = divmod(n, FT)
                if n >= 4:
                    eng.wait_ge(s["g"], n - 3)
                eng.matmul(ps[:, n % 4, :], ew[:, e, f * P:(f + 1) * P], X[:, :], start=True,
                           stop=True).then_inc(s["hid"], 1)

            def down(n):
                e, f = divmod(n, FT)
                if n == 0:
                    eng.wait_ge(s["w2"], 32)
                eng.wait_ge(s["g"], n + 1)
                at = FF + FT + f * P
                eng.matmul(ps[:, 4 + e, :], ew[:, e, at:at + P], g[:, n, :], start=(f == 0),
                           stop=(f == FT - 1)).then_inc(s["down"], 1)

            for n in range(4):
                up(n)
            for n in range(NU):
                down(n)
                if n + 4 < NU:
                    up(n + 4)
            norm_tensor(eng, ps, post)

        @block.scalar
        def _(eng):
            eng.wait_ge(s["m8"], 3)
            eng.activation(ee[:, :], lg[:, 0:E0], ACT.Exp, bias=nm[:, 0:1]).then_inc(s["ee"], 1)
            eng.wait_ge(s["w1"], 32)
            for n in range(NU):
                e, f = divmod(n, FT)
                eng.wait_ge(s["hid"], n + 1)
                eng.activation(g[:, n, :], ps[:, n % 4, :], ACT.Gelu, bias=ew[:, e, FF + f:FF + f + 1])\
                   .then_inc(s["g"], 1)
            norm_scalar(eng, ps, post)

        @block.gpsimd
        def _(eng):
            eng.memset(lg[:, E0:], FAR).then_inc(s["pad"], 1)
            eng.memset(rp[:, 2:], FAR).then_inc(s["pad"], 1)

        @block.vector
        def _(eng):
            link = chained(eng, s["chain"])
            eng.tensor_reduce(xm[:, :], X[:, :], AX, ALU.add).then_inc(s["mean"], 1)
            eng.wait_ge(s["logits"], 1)
            link(eng.tensor_scalar(lg[:, 0:E0], ps[:, 6, 0:E0], 1.0 / S, None, ALU.mult))
            eng.max(m8[:, :], lg[:, 0:E0]).then_inc(s["m8"], 1)
            eng.wait_ge(s["m8"], 1)
            eng.wait_ge(s["pad"], 2)
            eng.tensor_copy(rp[:, 0:2], m8[:, 0:2]).then_inc(s["m8"], 1)
            eng.tensor_scalar(nm[:, :], m8[:, 0:1], -1.0, None, ALU.mult).then_inc(s["m8"], 1)
            eng.wait_ge(s["m8"], 3)
            link(eng.match_replace(wk[:, :], rp[:, :], lg[:, :], TAKEN))
            numbers = K["jrow"][:, 0:E0]
            link(eng.scalar_tensor_tensor(sel[:, :], wk[:, 0:E0], TAKEN / 2, numbers, ALU.is_le, ALU.mult,
                                          accum_out=num[:, 0:1]))
            link(eng.tensor_reduce(num[:, 1:2], sel[:, :], AX, ALU.max))
            link(eng.tensor_tensor(num[:, 0:1], num[:, 0:1], num[:, 1:2], ALU.subtract))
            eng.tensor_copy(numi[:, :], num[:, :]).then_inc(s["chosen"], 1)
            eng.wait_ge(s["ee"], 1)
            link(eng.scalar_tensor_tensor(cw[:, :], wk[:, 0:E0], TAKEN / 2, ee[:, :], ALU.is_le, ALU.mult,
                                          accum_out=tot[:, :]))
            link(eng.reciprocal(tot[:, :], tot[:, :]))
            link(eng.tensor_scalar(cw[:, :], cw[:, :], tot[:, 0:1], None, ALU.mult))
            for i in range(2):
                link(eng.scalar_tensor_tensor(jk[:, :], numbers, num[:, i:i + 1], cw[:, :], ALU.is_equal, ALU.mult,
                                              accum_out=cs[:, i:i + 1]))
            link(eng.tensor_tensor_reduce(jk[:, :], K["f0_b2"], cw[:, :], 1.0, 0.0, ALU.mult, ALU.add,
                                          be[:, :]))
            link(eng.tensor_scalar(xb[:, :], X[:, :], be[:, 0:1], None, ALU.add))
            eng.wait_ge(s["down"], FT)
            link(eng.scalar_tensor_tensor(acc[:, :], ps[:, 4, :], cs[:, 0:1], xb[:, :], ALU.mult, ALU.add))
            eng.wait_ge(s["down"], NU)

            def put_y(h):
                c = slice(h * LN_HALF, (h + 1) * LN_HALF)
                return eng.scalar_tensor_tensor(L["y"][:, c], ps[:, 5, c], cs[:, 1:2], acc[:, c], ALU.mult,
                                                ALU.add)
            norm_vector(eng, ps, post, put_y)



D_SEMS = STACK_SEMS + "proj vp sc mn p tm pt pta pv rex rt rtb ot sent chain"
QL, QH = 16, 32


def attn1(nc, K, ps, X, s, b, contexts, parts_dram):
    with ExitStack() as stack:
        def sb(name, shape):
            return stack.enter_context(nc.sbuf_tensor(f"a1_{name}", shape, F32))

        def half(name, shape):
            return stack.enter_context(nc.sbuf_tensor(f"a1_{name}", shape, BF16))
        scale = float(DH) ** -0.5
        qf = sb("qf", [P, S])
        kf = sb("kf", [P, S])
        parts = [half(n, [P, 3, S]) for n in ("qparts", "kparts")]
        qs = half("qs", [ROWS, NH, S])
        ks = half("ks", [ROWS, NH, S])
        vp = sb("vp", [P, T, HG, P])
        steps = [(j, t, g) for j in range(HG) for t in range(T) for g in range(4)]
        N = len(steps)
        mn = sb("mn", [P, N])
        p = sb("p", [P, 8, S])
        pt = sb("pt", [P, 2, T, HG, 2 * P])
        rs = sb("rs", [P, T, NH])
        rex = sb("rex", [P, T, P])
        rt = sb("rt", [P, S])
        ot = sb("ot", [P, QL, QH])
        by_act = [n % 2 == 1 for n in range(N)]
        acts = [sum(by_act[:n + 1]) for n in range(N)]
        vecs = [n + 1 - acts[n] for n in range(N)]

        def emptied(eng, n):
            eng.wait_ge(s["pta"] if by_act[n] else s["pt"], acts[n] if by_act[n] else vecs[n])

        def empty(eng, copy, n, sem):
            j, t, g = steps[n]
            eng.wait_ge(s["tm"], n + 1)
            if n >= 16:
                eng.wait_ge(s["pv"], n // 8 - 1)
            copy(pt[:, (n // 8) % 2, :, g, (t % 2) * P:(t % 2 + 1) * P],
                 ps[:, 4 + n % 3, :].rearrange("p (k q) -> p k q", k=T)).then_inc(sem, 1)
        block = stack.enter_context(nc.Block(no_gpsimd_drain=True))

        @block.tensor
        def _(eng):
            eng.matmul(ps[:, 0, :], K["a1_wq"][:, :], X[:, :], start=True, stop=True).then_inc(s["proj"], 1)
            eng.matmul(ps[:, 1, :], K["a1_wk"][:, :], X[:, :], start=True, stop=True).then_inc(s["proj"], 1)
            for k in range(T):
                mm = eng.matmul(ps[:, 2, k * P:(k + 1) * P], X[:, k * P:(k + 1) * P], K["a1_wv"][:, :],
                                start=True, stop=True)
            mm.then_inc(s["proj"], 1)

            def scores(n):
                j, t, g = steps[n]
                if n == 0:
                    eng.wait_ge(s["qf"], 1)
                    eng.wait_ge(s["kf"], 1)
                if t == 0 and g == 0:
                    eng.wait_ge(s[f"j{j}"], STACKED)
                if n == 2:
                    eng.wait_ge(s["vp"], T)
                if n >= 4:
                    eng.wait_ge(s["mn"], n - 3)
                eng.matmul(ps[:, g, :], qs[:, HG * j + g, t * P:(t + 1) * P], ks[:, HG * j + g, :], start=True,
                           stop=True).then_inc(s["sc"], 1)

            def turn(n):
                eng.wait_ge(s["p"], n + 1)
                if n >= 3:
                    emptied(eng, n - 3)
                for k in range(T):
                    mm = eng.transpose(ps[:, 4 + n % 3, k * P:(k + 1) * P], p[:, n % 8, k * P:(k + 1) * P],
                                       K["ident"])
                mm.then_inc(s["tm"], 1)

            def values(u):
                j, t, _ = steps[8 * u]
                emptied(eng, 8 * u + 7)
                emptied(eng, 8 * u + 6)
                for k in range(T):
                    for g in range(4):
                        mm = eng.matmul(ps[32 * g:32 * g + 32, 7, t * P:(t + 2) * P],
                                        vp[:, k, j, 32 * g:32 * g + 32], pt[:, u % 2, k, g, :],
                                        start=(u == 0 and k == 0), stop=(j == HG - 1 and k == T - 1),
                                        skip_group_check=True)
                mm.then_inc(s["pv"], 1)

            for n in range(4):
                scores(n)
            for n in range(N):
                if n + 4 < N:
                    scores(n + 4)
                turn(n)
                if n % 8 == 3 and n > 8:
                    values(n // 8 - 1)
            values(N // 8 - 1)
            eng.wait_ge(s["rex"], 1)
            for t in range(T):
                mm = eng.transpose(ps[:, 4, t * P:(t + 1) * P], rex[:, t, :], K["ident"])
            mm.then_inc(s["rtb"], 1)

        @block.scalar
        def _(eng):
            eng.wait_ge(s["proj"], 2)
            eng.activation(kf[:, :], ps[:, 1, :], ACT.Identity, bias=K["a1_bk"]).then_inc(s["kf"], 1)
            eng.wait_ge(s["kf"], 1)
            split_scalar(eng, parts[1], kf, s["ks"])
            for n, (j, t, g) in enumerate(steps):
                eng.wait_ge(s["mn"], n + 1)
                h = 4 * g + j
                eng.activation(p[:, n % 8, :], p[:, n % 8, :], ACT.Exp, bias=mn[:, n:n + 1], scale=-1.0,
                               accum_out=rs[:, t, h:h + 1]).then_inc(s["p"], 1)
                if n >= 3 and by_act[n - 3]:
                    empty(eng, lambda o, i: eng.activation(o, i, ACT.Copy), n - 3, s["pta"])
            for n in range(N - 3, N):
                if by_act[n]:
                    empty(eng, lambda o, i: eng.activation(o, i, ACT.Copy), n, s["pta"])
            eng.wait_ge(s["rtb"], 1)
            eng.activation(rt[:, :], ps[:, 4, :], ACT.Copy).then_inc(s["rt"], 1)

        @block.vector
        def _(eng):
            link = chained(eng, s["chain"])
            eng.wait_ge(s["proj"], 1)
            eng.tensor_scalar(qf[:, :], ps[:, 0, :], K["a1_bq"], -scale, ALU.add, ALU.mult).then_inc(s["qf"], 1)
            eng.wait_ge(s["qf"], 1)
            split(eng, parts[0], qf, s["qs"])
            split_vector(eng, parts[1], kf, s["ks"])
            eng.wait_ge(s["proj"], 3)
            for k in range(T):
                eng.tensor_tensor(vp[:, k, :, :], ps[:, 2, k * P:(k + 1) * P].unsqueeze(1).to_broadcast([P, HG, P]),
                                  K["colmask_dj"], ALU.mult).then_inc(s["vp"], 1)

            def biased(n):
                j, t, g = steps[n]
                at = S - P - t * P
                eng.wait_ge(s["sc"], n + 1)
                if n >= 8:
                    eng.wait_ge(s["tm"], n - 7)
                eng.tensor_tensor_reduce(p[:, n % 8, :], ps[:, g, :], K["nbias"][:, at:at + S], 1.0, 3.0e38,
                                         ALU.add, ALU.min, mn[:, n:n + 1]).then_inc(s["mn"], 1)

            for n in range(N):
                biased(n)
                if n >= 4 and not by_act[n - 4]:
                    empty(eng, eng.tensor_copy, n - 4, s["pt"])
            for n in range(N - 4, N):
                if not by_act[n]:
                    empty(eng, eng.tensor_copy, n, s["pt"])
            eng.wait_ge(s["p"], N)
            link(eng.reciprocal(rs[:, :, :], rs[:, :, :]))
            eng.tensor_copy(rex[:, :, :].rearrange("p t (g d j) -> p (t g) d j", d=DH, j=HG),
                            rs[:, :, :].rearrange("p t (g j) -> p (t g) j", j=HG).unsqueeze(2)
                            .to_broadcast([P, T * 4, DH, HG])).then_inc(s["rex"], 1)
            eng.wait_ge(s["rt"], 1)
            eng.wait_ge(s["pv"], N // 8)
            link(eng.tensor_tensor(ot[:, :, :].rearrange("p a b -> p b a"),
                                   ps[:, 7, :].rearrange("p (b a) -> p b a", a=QL),
                                   rt[:, :].rearrange("p (b a) -> p b a", a=QL), ALU.mult))
            eng.tensor_scalar(ot[:, :, :], ot[:, :, :], K["a1_bv"], None, ALU.add).then_inc(s["ot"], 1)

        @block.sync
        def _(eng):
            stack_parts(eng, s, parts, (qs, ks), parts_dram)
            eng.wait_ge(s["ot"], 1)
            for g in range(4):
                eng.dma_start(bass.AP(contexts.tensor, g * P * S + b * QH, [[B * QH, DH * HG], [DH * S, QL], [1, QH]]),
                              ot[32 * g:32 * g + 32, :, :]).then_inc(s["sent"], 16)
            eng.wait_ge(s["sent"], 16 * 4)


O_SEMS = "out " + norm_names("post")


def attn1_out(nc, K, ps, X, s):
    with ExitStack() as stack:
        L = norm_tiles(nc, stack, "ao")
        post = norm_of(K, L, s, "post", (2, 3), (5, 6), X)
        block = stack.enter_context(nc.Block(no_gpsimd_drain=True))

        @block.tensor
        def _(eng):
            for h in range(2):
                eng.matmul(ps[:, h, 0:LN_HALF], K["a1_wo"][:, :], K["ot"][:, h * LN_HALF:(h + 1) * LN_HALF],
                           start=True, stop=True).then_inc(s["out"], 1)
            norm_tensor(eng, ps, post)

        @block.scalar
        def _(eng):
            norm_scalar(eng, ps, post)

        @block.vector
        def _(eng):
            def put_y(h):
                c = slice(h * LN_HALF, (h + 1) * LN_HALF)
                eng.wait_ge(s["out"], h + 1)
                return eng.scalar_tensor_tensor(L["y"][:, c], ps[:, h, 0:LN_HALF], K["a1_bo"], X[:, c],
                                                ALU.add, ALU.add)
            norm_vector(eng, ps, post, put_y)




F_SEMS = ("pad gates bg m8 rp wk sel gs ee wt wtt wts hid h gate sg h2 wx h3 down busy fb chain achain "
          + norm_names("r0", "r1", "post"))


def experts1(nc, K, ps, X, s):
    with ExitStack() as stack:
        def sb(name, shape):
            return stack.enter_context(nc.sbuf_tensor(f"e1_{name}", shape, F32))
        L = norm_tiles(nc, stack, "e1")
        gt = sb("gt", [P, HOPS, T, E1])
        bg = sb("bg", [P, HOPS, T, 16])
        m8 = sb("m8", [P, HOPS, T, 8])
        rp = sb("rp", [P, HOPS, T, 8])
        wk = sb("wk", [P, HOPS, T, 16])
        sel = sb("sel", [P, HOPS, T, E1])
        gs = sb("gs", [P, HOPS, T, E1])
        mx = sb("mx", [P, HOPS, T])
        ee = sb("ee", [P, HOPS, T, E1])
        tot = sb("tot", [P, HOPS, T])
        wt = sb("wt", [P, HOPS, T, E1])
        wtt = sb("wtt", [E1, HOPS, S])
        xf = [X, sb("xf0", [P, S]), sb("xf1", [P, S])]
        h = sb("h", [P, 2, S])
        g = sb("g", [P, 2, S])
        h2 = sb("h2", [P, 2, S])
        h3 = sb("h3", [P, 2, S])
        sdown2 = sb("sdown2", [P, 1])
        hop = [norm_of(K, L, s, f"r{j}", (0, 1), (2, 3), xf[j + 1], centred=False,
                       scale=K["f1_norm"][:, j:j + 1], eps="eps6") for j in range(HOPS)]
        post = norm_of(K, L, s, "post", (4, 5), (0, 1), X)
        NU = E1 + NSH
        block = stack.enter_context(nc.Block(no_gpsimd_drain=True))

        def weights(u):
            if u < E1:
                return (K["f1_up"][:, u, :], K["f1_g"][:, u, :], K["f1_down"][:, u, :],
                        K["f1_bup"][:, u:u + 1], K["f1_bg"][:, u:u + 1])
            n = u - E1
            return (K["f1_sup"][:, n * P:(n + 1) * P], K["f1_swg"][:, :], K["f1_swdown"][:, :],
                    K["f1_sup_b"][:, n:n + 1], K["f1_sg"])
        ORDER = list(range(E1, NU)) + list(range(E1))

        @block.tensor
        def _(eng):
            for j in range(HOPS):
                base = j * NU
                if j:
                    eng.wait_ge(s[f"r{j - 1}_out"], 2)
                for t in range(T):
                    mm = eng.matmul(ps[:, 7, t * E1:(t + 1) * E1], xf[j][:, t * P:(t + 1) * P],
                                    K["f1_router"][:, j, :], start=True, stop=True)
                mm.then_inc(s["gates"], 1)

                def up(i):
                    n = base + i
                    if n >= 2:
                        eng.wait_ge(s["h"], n - 1)
                    eng.matmul(ps[:, n % 2, :], weights(ORDER[i])[0], xf[j][:, :], start=True, stop=True)\
                       .then_inc(s["hid"], 1)

                def gate(i):
                    n = base + i
                    eng.wait_ge(s["h"], n + 1)
                    if n >= 2:
                        eng.wait_ge(s["sg"], n - 1)
                    eng.matmul(ps[:, 2 + n % 2, :], weights(ORDER[i])[1], h[:, n % 2, :], start=True,
                               stop=True).then_inc(s["gate"], 1)

                def spread(i):
                    e = ORDER[i]
                    if e >= E1:
                        return
                    n = j * E1 + e
                    if e == 0:
                        eng.wait_ge(s["wts"], j + 1)
                    if n >= 2:
                        eng.wait_ge(s["h3"], n - 1)
                    eng.matmul(ps[:, 4 + n % 2, :], K["esel"][:, e, :], wtt[:, j, :], start=True, stop=True)\
                       .then_inc(s["wx"], 1)

                def down(i):
                    n, e = base + i, ORDER[i]
                    if e < E1:
                        eng.wait_ge(s["h3"], j * E1 + e + 1)
                        src = h3[:, (j * E1 + e) % 2, :]
                    else:
                        eng.wait_ge(s["h2"], n + 1)
                        src = h2[:, n % 2, :]
                    if n % NU == 0 and j:
                        eng.wait_ge(s["r0_y"], 2)
                    eng.matmul(ps[:, 6, :], weights(e)[2], src, start=(i == 0), stop=False,
                               skip_group_check=True).then_inc(s["down"], 1)

                def routing():
                    eng.wait_ge(s["wt"], j + 1)
                    eng.wait_ge(s["bg"], j + 1)
                    for t in range(T):
                        mm = eng.transpose(ps[0:E1, 7, t * P:(t + 1) * P], wt[:, j, t, :], K["ident"])
                    mm.then_inc(s["wtt"], 1)

                up(0)
                up(1)
                gate(0)
                for i in range(NU):
                    if i + 2 < NU:
                        up(i + 2)
                    if i + 1 < NU:
                        gate(i + 1)
                    if i == NSH - 1:
                        routing()
                        spread(NSH)
                    if i >= NSH and i + 1 < NU:
                        spread(i + 1)
                    down(i)
                eng.matmul(ps[:, 6, :], K["f1_bdown"][:, :], wtt[:, j, :], start=False, stop=True,
                           skip_group_check=True).then_inc(s["fb"], 1)
                norm_tensor(eng, ps, hop[j])
            norm_tensor(eng, ps, post)

        @block.scalar
        def _(eng):
            for j in range(HOPS):
                def hidden(i):
                    n = j * NU + i
                    eng.wait_ge(s["hid"], n + 1)
                    if n >= 2:
                        eng.wait_ge(s["h2"], n - 1)
                    eng.activation(h[:, n % 2, :], ps[:, n % 2, :], ACT.Identity, bias=weights(ORDER[i])[3])\
                       .then_inc(s["h"], 1)

                def silu(i):
                    n = j * NU + i
                    eng.wait_ge(s["gate"], n + 1)
                    eng.activation(g[:, n % 2, :], ps[:, 2 + n % 2, :], ACT.Silu, bias=weights(ORDER[i])[4])\
                       .then_inc(s["sg"], 1)
                hidden(0)
                hidden(1)
                eng.wait_ge(s["gs"], j + 1)
                eng.activation(ee[:, j, :, :], gs[:, j, :, :], ACT.Exp).then_inc(s["ee"], 1)
                for i in range(NU):
                    silu(i)
                    if i == 1:
                        eng.wait_ge(s["wtt"], j + 1)
                        eng.activation(wtt[:, j, :], ps[0:E1, 7, :], ACT.Copy).then_inc(s["wts"], 1)
                    if i + 2 < NU:
                        hidden(i + 2)
                norm_scalar(eng, ps, hop[j])
            norm_scalar(eng, ps, post)

        @block.gpsimd
        def _(eng):
            eng.memset(bg[:, :, :, E1:], FAR).then_inc(s["pad"], 1)
            eng.memset(rp[:, :, :, 2:], FAR).then_inc(s["pad"], 1)

        @block.vector
        def _(eng):
            link = chained(eng, s["chain"])
            link(eng.tensor_scalar(sdown2[:, :], K["f1_sdown"], float(NSH), None, ALU.mult))
            for j in range(HOPS):
                def route():
                    eng.wait_ge(s["gates"], j + 1)
                    link(eng.tensor_tensor(gt[:, j, :, :], ps[:, 7, 0:T * E1].rearrange("p (t e) -> p t e", t=T),
                                           K["f1_rb"][:, j * E1:(j + 1) * E1].unsqueeze(1).to_broadcast([P, T, E1]),
                                           ALU.add))
                    eng.wait_ge(s["pad"], 2)
                    eng.tensor_tensor(bg[:, j, :, 0:E1], gt[:, j, :, :],
                                      K["f1_gb"][:, j * E1:(j + 1) * E1].unsqueeze(1).to_broadcast([P, T, E1]),
                                      ALU.add).then_inc(s["bg"], 1)
                    eng.wait_ge(s["bg"], j + 1)
                    for t in range(T):
                        i = eng.max(m8[:, j, t, :], bg[:, j, t, :])
                        i.then_inc(s["m8"], 1)
                    eng.wait_ge(s["m8"], T * (j + 1))
                    link(eng.tensor_copy(rp[:, j, :, 0:2], m8[:, j, :, 0:2]))
                    for t in range(T):
                        eng.match_replace(wk[:, j, t, :], rp[:, j, t, :], bg[:, j, t, :], TAKEN)\
                           .then_inc(s["wk"], 1)
                    eng.wait_ge(s["wk"], T * (j + 1))
                    link(eng.tensor_scalar(sel[:, j, :, :], wk[:, j, :, 0:E1], TAKEN / 2, None, ALU.is_le))
                    link(eng.tensor_scalar(gs[:, j, :, :], sel[:, j, :, :], -FAR, FAR, ALU.mult, ALU.add))
                    link(eng.tensor_tensor(gs[:, j, :, :], gs[:, j, :, :], gt[:, j, :, :], ALU.add))
                    link(eng.tensor_reduce(mx[:, j, :], gs[:, j, :, :], AX, ALU.max))
                    eng.tensor_tensor(gs[:, j, :, :], gs[:, j, :, :],
                                      mx[:, j, :].unsqueeze(2).to_broadcast([P, T, E1]), ALU.subtract)\
                       .then_inc(s["gs"], 1)
                    eng.wait_ge(s["ee"], j + 1)
                    link(eng.tensor_reduce(tot[:, j, :], ee[:, j, :, :], AX, ALU.add))
                    link(eng.reciprocal(tot[:, j, :], tot[:, j, :]))
                    eng.tensor_tensor(wt[:, j, :, :], ee[:, j, :, :],
                                      tot[:, j, :].unsqueeze(2).to_broadcast([P, T, E1]), ALU.mult)\
                       .then_inc(s["wt"], 1)
                route()
                for i in range(NU):
                    n, e = j * NU + i, ORDER[i]
                    eng.wait_ge(s["sg"], n + 1)
                    if n >= 2:
                        eng.wait_ge(s["down"], n - 1)
                    eng.tensor_tensor(h2[:, n % 2, :], h[:, n % 2, :], g[:, n % 2, :], ALU.mult)\
                       .then_inc(s["h2"], 1)
                    if e < E1:
                        m = j * E1 + e
                        eng.wait_ge(s["h2"], n + 1)
                        eng.wait_ge(s["wx"], m + 1)
                        eng.tensor_tensor(h3[:, m % 2, :], h2[:, n % 2, :], ps[:, 4 + m % 2, :], ALU.mult)\
                           .then_inc(s["h3"], 1)

                def put_y(hf, j=j):
                    c = slice(hf * LN_HALF, (hf + 1) * LN_HALF)
                    eng.wait_ge(s["fb"], j + 1)
                    return eng.scalar_tensor_tensor(L["y"][:, c], ps[:, 6, c], sdown2[:, 0:1], xf[j][:, c],
                                                    ALU.add, ALU.add)
                norm_vector(eng, ps, hop[j], put_y)

            def put_y(hf):
                c = slice(hf * LN_HALF, (hf + 1) * LN_HALF)
                return eng.tensor_tensor(L["y"][:, c], xf[2][:, c], X[:, c], ALU.add)
            norm_vector(eng, ps, post, put_y)


def bias_table(nc, stack, K, s):
    nbias = stack.enter_context(nc.sbuf_tensor("k_nbias", [P, RW], F32))
    sg = stack.enter_context(nc.sbuf_tensor("k_sg", [P, 1], F32))
    with nc.Block(no_gpsimd_drain=True) as block:
        @block.scalar
        def _(eng):
            eng.activation(sg[:, :], K["et_gate"], ACT.Exp, scale=-1.0).then_inc(s["bc"], 1)

        @block.vector
        def _(eng):
            link = chained(eng, s["chain"])
            eng.wait_ge(s["bc"], 1)
            link(eng.tensor_scalar(sg[:, :], sg[:, :], 1.0, None, ALU.add))
            link(eng.reciprocal(sg[:, :], sg[:, :]))
            link(eng.tensor_scalar(nbias[:, :], K["skew"][:, :], sg[:, 0:1], K["is_gate"], ALU.mult, ALU.add))
            link(eng.tensor_scalar(nbias[:, :], nbias[:, :], -1.0, None, ALU.mult))
    K["nbias"] = nbias
    nc.gpsimd.sem_clear(s["chain"])
    nc.gpsimd.sem_clear(s["bc"])
    nc.all_engine_barrier()



def kernel_spectrum(nc, stack, I, K, ps):
    kf = stack.enter_context(nc.sbuf_tensor("k_kf", [P, NF // P, P], F32))
    K["kf"] = kf
    with ExitStack() as tmp:
        s = semaphores(nc, tmp, "kf", "s4 dt chain args small targs iargs trig tab prod ks ksc kf")
        def sb(name, shape):
            return tmp.enter_context(nc.sbuf_tensor(f"kf_{name}", shape, F32))
        s4 = sb("s4", [P, 4, P])
        dt = sb("dt", [P, P])
        near = sb("near", [P, P])
        power = tmp.enter_context(nc.sbuf_tensor("kf_power", [P, P], I32))
        r = sb("r", [P, P])
        turns = sb("turns", [P, P])
        arg = sb("arg", [P, 3, P])
        whole = sb("whole", [P, P * JL])
        trig = sb("trig", [P, 3, P])
        er = sb("er", [P, P])
        th = sb("th", [P, P])
        a = sb("a", [P, P])
        b = sb("b", [P, P])
        c = sb("c", [P, P])
        e = sb("e", [P, P])
        alpha = sb("alpha", [P, P])
        beta = sb("beta", [P, P])
        tj = sb("tj", [P, P, JL])
        ej = sb("ej", [P, P, JL])
        uv = sb("uv", [P, 2, P, IL])
        ei = sb("ei", [P, P, IL])
        ti = uv[:, 0, :, :]
        ks = whole[:, 0:T * P].rearrange("p (k d) -> p k d", k=T)
        block = tmp.enter_context(nc.Block(no_gpsimd_drain=True))

        @block.sync
        def _(eng):
            eng.dma_start(s4[:, :, :], I["s4"]).then_inc(s["s4"], 16)

        @block.tensor
        def _(eng):
            eng.wait_ge(s["prod"], 2)
            for d in range(P):
                for g in range(T):
                    mm = eng.matmul(ps[JL * g:JL * g + JL, 0, d:3 * P + d + 1:P], tj[:, d, :], ti[:, d, g::T],
                                    start=True, stop=True, skip_group_check=True)
            mm.then_inc(s["ks"], 1)
            eng.wait_ge(s["ksc"], 1)
            for f in range(NF // P):
                for k in range(T):
                    mm = eng.matmul(ps[:, 1 + f // T, (f % T) * P:(f % T + 1) * P],
                                    K["fwd"][:, k, f * P:(f + 1) * P], ks[:, k, :],
                                    start=(k == 0), stop=(k == T - 1))
            mm.then_inc(s["kf"], 1)

        @block.scalar
        def _(eng):
            eng.wait_ge(s["args"], 1)
            eng.activation(er[:, :], r[:, :], ACT.Exp).then_inc(s["small"], 1)
            eng.activation(th[:, :], r[:, :], ACT.Tanh, scale=0.5).then_inc(s["small"], 1)
            eng.wait_ge(s["targs"], 1)
            eng.activation(ej[:, :, :], ej[:, :, :], ACT.Exp).then_inc(s["tab"], 1)
            eng.activation(ei[:, :, :], ei[:, :, :], ACT.Exp).then_inc(s["tab"], 1)
            eng.wait_ge(s["args"], 2)
            eng.activation(trig[:, :, :], arg[:, :, :], ACT.Sin, scale=TURN).then_inc(s["trig"], 1)
            eng.wait_ge(s["iargs"], 1)
            eng.activation(uv[:, :, :, :], uv[:, :, :, :], ACT.Sin, scale=TURN).then_inc(s["tab"], 1)
            eng.wait_ge(s["iargs"], 2)
            eng.activation(tj[:, :, :], tj[:, :, :], ACT.Sin, scale=TURN).then_inc(s["tab"], 1)

        @block.vector
        def _(eng):
            link = chained(eng, s["chain"])

            def fraction(x, w):
                link(eng.tensor_scalar(w, x, MAGIC, None, ALU.add))
                link(eng.tensor_scalar(w, w, -MAGIC, None, ALU.add))
                return eng.tensor_tensor(x, x, w, ALU.subtract)

            def wide(v, n):
                return v.unsqueeze(2).to_broadcast([P, P, n])

            def steps(name, n):
                return K[name].unsqueeze(1).to_broadcast([P, P, n])
            link(eng.tensor_scalar(r[:, :], K["log_dt"], LOG_LEAST, LOG_MOST, ALU.max, ALU.min))
            link(eng.tensor_scalar(near[:, :], r[:, :], 1.0 / LN2, None, ALU.mult))
            link(eng.tensor_scalar(near[:, :], near[:, :], MAGIC, None, ALU.add))
            link(eng.tensor_scalar(near[:, :], near[:, :], -MAGIC, None, ALU.add))
            link(eng.scalar_tensor_tensor(r[:, :], near[:, :], -LN2_HIGH, r[:, :], ALU.mult, ALU.add))
            link(eng.scalar_tensor_tensor(r[:, :], near[:, :], LN2_HIGH - LN2, r[:, :], ALU.mult, ALU.add))
            link(eng.tensor_scalar(dt[:, :], r[:, :], SERIES[-1], None, ALU.mult))
            for term in SERIES[-2:0:-1]:
                link(eng.scalar_tensor_tensor(dt[:, :], dt[:, :], term, r[:, :], ALU.add, ALU.mult))
            link(eng.tensor_scalar(power[:, :], near[:, :], EXP_BIAS, EXP_UNIT, ALU.add, ALU.mult))
            link(eng.scalar_tensor_tensor(dt[:, :], dt[:, :], 1.0, power[:, :].bitcast(F32), ALU.add, ALU.mult))
            eng.wait_ge(s["s4"], 16)
            eng.tensor_tensor(r[:, :], dt[:, :], s4[:, 0, :], ALU.mult).then_inc(s["args"], 1)
            eng.wait_ge(s["args"], 1)
            link(eng.scalar_tensor_tensor(turns[:, :], s4[:, 1, :], INV2PI, dt[:, :], ALU.mult, ALU.mult))
            link(eng.tensor_tensor(ej[:, :, :], wide(r[:, :], JL), steps("jrow", JL), ALU.mult))
            eng.tensor_tensor(ei[:, :, :], wide(r[:, :], IL), steps("irow", IL), ALU.mult)\
               .then_inc(s["targs"], 1)
            link(eng.tensor_copy(arg[:, 0, :], turns[:, :]))
            link(eng.tensor_scalar(arg[:, 1, :], turns[:, :], 0.25, None, ALU.add))
            link(eng.tensor_scalar(arg[:, 2, :], turns[:, :], 0.5, None, ALU.mult))
            fraction(arg[:, :, :], whole[:, 0:3 * P].rearrange("p (a b) -> p a b", a=3)).then_inc(s["args"], 1)
            eng.wait_ge(s["args"], 2)
            link(eng.tensor_tensor(uv[:, 0, :, :], wide(turns[:, :], IL), steps("irow", IL), ALU.mult))
            link(eng.tensor_scalar(uv[:, 1, :, :], uv[:, 0, :, :], K["phase2"], None, ALU.add))
            link(eng.tensor_scalar(uv[:, 0, :, :], uv[:, 0, :, :], K["phase"], None, ALU.add))
            fraction(uv[:, :, :, :], whole[:, :].rearrange("p (c d i) -> p c d i", c=2, d=P))\
                .then_inc(s["iargs"], 1)
            eng.wait_ge(s["iargs"], 1)
            link(eng.tensor_tensor(tj[:, :, :], wide(turns[:, :], JL), steps("jrow", JL), ALU.mult))
            link(eng.tensor_scalar(tj[:, :, :], tj[:, :, :], K["phase"], None, ALU.add))
            fraction(tj[:, :, :], whole[:, :].rearrange("p (d j) -> p d j", d=P)).then_inc(s["iargs"], 1)
            eng.wait_ge(s["small"], 2)
            eng.wait_ge(s["trig"], 1)
            link(eng.scalar_tensor_tensor(th[:, :], er[:, :], 1.0, th[:, :], ALU.add, ALU.mult))
            link(eng.tensor_tensor(th[:, :], th[:, :], trig[:, 1, :], ALU.mult))
            link(eng.scalar_tensor_tensor(a[:, :], trig[:, 2, :], -2.0, trig[:, 2, :], ALU.mult, ALU.mult))
            link(eng.tensor_tensor(a[:, :], a[:, :], th[:, :], ALU.add))
            link(eng.tensor_tensor(b[:, :], er[:, :], trig[:, 0, :], ALU.mult))
            link(eng.tensor_tensor(c[:, :], s4[:, 2, :], a[:, :], ALU.mult))
            link(eng.tensor_tensor(e[:, :], s4[:, 3, :], b[:, :], ALU.mult))
            link(eng.tensor_tensor(c[:, :], c[:, :], e[:, :], ALU.subtract))
            link(eng.tensor_tensor(b[:, :], s4[:, 2, :], b[:, :], ALU.mult))
            link(eng.tensor_tensor(e[:, :], s4[:, 3, :], a[:, :], ALU.mult))
            link(eng.tensor_tensor(e[:, :], e[:, :], b[:, :], ALU.add))
            link(eng.tensor_tensor(a[:, :], s4[:, 0, :], s4[:, 0, :], ALU.mult))
            link(eng.tensor_tensor(b[:, :], s4[:, 1, :], s4[:, 1, :], ALU.mult))
            link(eng.tensor_tensor(a[:, :], a[:, :], b[:, :], ALU.add))
            link(eng.reciprocal(er[:, :], a[:, :]))
            link(eng.tensor_tensor(a[:, :], c[:, :], s4[:, 0, :], ALU.mult))
            link(eng.tensor_tensor(b[:, :], e[:, :], s4[:, 1, :], ALU.mult))
            link(eng.tensor_tensor(a[:, :], a[:, :], b[:, :], ALU.add))
            link(eng.scalar_tensor_tensor(alpha[:, :], a[:, :], K["sign"], er[:, :], ALU.mult, ALU.mult))
            link(eng.tensor_tensor(a[:, :], c[:, :], s4[:, 1, :], ALU.mult))
            link(eng.tensor_tensor(b[:, :], e[:, :], s4[:, 0, :], ALU.mult))
            link(eng.tensor_tensor(a[:, :], a[:, :], b[:, :], ALU.subtract))
            link(eng.tensor_tensor(beta[:, :], a[:, :], er[:, :], ALU.mult))
            eng.wait_ge(s["tab"], 3)
            link(eng.tensor_tensor(uv[:, 0, :, :], uv[:, 0, :, :], wide(alpha[:, :], IL), ALU.mult))
            link(eng.tensor_tensor(uv[:, 1, :, :], uv[:, 1, :, :], wide(beta[:, :], IL), ALU.mult))
            link(eng.tensor_tensor(uv[:, 0, :, :], uv[:, 0, :, :], uv[:, 1, :, :], ALU.add))
            eng.scalar_tensor_tensor(ti[:, :, :], uv[:, 0, :, :], 2.0, ei[:, :, :], ALU.mult, ALU.mult)\
               .then_inc(s["prod"], 1)
            eng.wait_ge(s["tab"], 4)
            eng.tensor_tensor(tj[:, :, :], tj[:, :, :], ej[:, :, :], ALU.mult).then_inc(s["prod"], 1)
            eng.wait_ge(s["ks"], 1)
            eng.tensor_copy(ks[:, :, :], ps[:, 0, :].rearrange("p (k d) -> p k d", k=T)).then_inc(s["ksc"], 1)
            eng.wait_ge(s["kf"], 1)
            eng.tensor_copy(kf[:, :, :], ps[:, 1:3, :].rearrange("p b (f d) -> p (b f) d", d=P))
    for sem in s.values():
        nc.gpsimd.sem_clear(sem)
    nc.all_engine_barrier()



E_SEMS = ("proj qk v mask sc scr mx mr neg e a rs r dg at atc ct ctc film filmc xi xit xitc dft y inv "
          "h1 hg h2 chain " + norm_names("nin", "nffn", "nout", "post"))
ROUNDS = TOPK // 8


def cross1(nc, K, ps, X, s):
    with ExitStack() as stack:
        def sb(name, shape):
            return stack.enter_context(nc.sbuf_tensor(f"c1_{name}", shape, F32))
        L = norm_tiles(nc, stack, "c1")
        ctx = K["ctx"]
        qt = sb("qt", [P, S])
        kt = sb("kt", [P, M])
        v = sb("v", [P, P])
        vr = sb("vr", [MR, P])
        vm = sb("vm", [P, M])
        tm = sb("tm", [P, T])
        xn = sb("xn", [P, S])
        sc = sb("sc", [P, 2, XH, M])
        wk = sb("wk", [P, XH, M])
        m8 = sb("m8", [P, ROUNDS, XH, 8])
        neg = sb("neg", [P, 2, XH])
        e = sb("e", [P, 2, XH, M])
        a = sb("a", [P, 2, XH, M])
        rs = sb("rs", [P, 2, XH])
        r = sb("r", [P, 2, XH])
        dg = sb("dg", [P, 2, XH, P])
        at = sb("at", [P, S])
        atr = sb("atr", [MR, S])
        ct = sb("ct", [P, S])
        fb = sb("fb", [P, 4])
        film = sb("film", [P, 4, S])
        xi = sb("xi", [P, S])
        xit = sb("xit", [P, T, P])
        kf = K["kf"]
        y = sb("y", [P, NF // P, P])
        m = sb("m", [P, 4, T, P])
        hn = sb("hn", [P, S])
        hg = sb("hg", [P, FT, S])
        z = sb("z", [P, S])
        nin = norm_of(K, L, s, "nin", (4, 5), (6, 7), xn, scale=K["x1_gin"], shift=K["x1_bin"])
        nffn = norm_of(K, L, s, "nffn", (4, 5), (0, 1), hn, scale=K["x1_gffn"], shift=K["x1_bffn"])
        nout = norm_of(K, L, s, "nout", (4, 5), (2, 3), z, scale=K["x1_gout"], shift=K["x1_bout"])
        post = norm_of(K, L, s, "post", (4, 5), (0, 1), X)
        block = stack.enter_context(nc.Block(no_gpsimd_drain=True))

        @block.tensor
        def _(eng):
            eng.matmul(ps[:, 0, :], K["x1_wq"][:, :], X[:, :], start=True, stop=True).then_inc(s["proj"], 1)
            eng.matmul(ps[:, 1, 0:M], K["x1_wk"][:, :], ctx[:, 0:M], start=True, stop=True)\
               .then_inc(s["proj"], 1)
            eng.matmul(ps[:, 2, 0:P], ctx[:, 0:P], K["x1_wv"][:, :], start=True, stop=True)\
               .then_inc(s["proj"], 1)
            eng.matmul(ps[0:MR, 3, 0:P], ctx[:, P:M], K["x1_wv"][:, :], start=True, stop=True)\
               .then_inc(s["proj"], 1)

            def scores(t):
                if t == 0:
                    eng.wait_ge(s["qk"], 2)
                    eng.wait_ge(s["v"], 2)
                else:
                    eng.wait_ge(s["scr"], t)
                for h in range(XH):
                    mm = eng.matmul(ps[:, h, 0:M], qt[XD * h:XD * h + XD, t * P:(t + 1) * P],
                                    kt[XD * h:XD * h + XD, :], start=True, stop=True)
                mm.then_inc(s["sc"], 1)
            scores(0)
            norm_tensor(eng, ps, nin)
            for t in range(T):
                if t + 1 < T:
                    scores(t + 1)
                eng.wait_ge(s["a"], XH * (t + 1))
                eng.wait_ge(s["dg"], XH * (t + 1))
                for bank, cols, rows in ((4, slice(0, P), P), (5, slice(P, M), MR)):
                    for h in range(XH):
                        mm = eng.matmul(ps[0:rows, bank, t * P:(t + 1) * P], a[:, t % 2, h, cols],
                                        dg[:, t % 2, h, :], start=(h == 0), stop=(h == XH - 1))
                mm.then_inc(s["at"], 1)
            eng.wait_ge(s["atc"], 2)
            eng.matmul(ps[:, 6, :], v[:, :], at[:, :], start=True, stop=False)
            eng.matmul(ps[:, 6, :], vr[:, :], atr[:, :], start=False, stop=True).then_inc(s["ct"], 1)
            eng.wait_ge(s["ctc"], 1)
            for n, w in enumerate(("x1_win", "x1_win", "x1_wout", "x1_wout")):
                eng.matmul(ps[:, n, :], K[w][:, (n % 2) * P:(n % 2 + 1) * P], ct[:, :], start=True, stop=True)\
                   .then_inc(s["film"], 1)
            eng.wait_ge(s["xi"], 1)
            for t in range(T):
                mm = eng.transpose(ps[:, 4, t * P:(t + 1) * P], xi[:, t * P:(t + 1) * P], K["ident"])
            mm.then_inc(s["xit"], 1)
            eng.wait_ge(s["xitc"], 1)
            for f in range(NF // P):
                for t in range(T):
                    mm = eng.matmul(ps[:, 5 + f // T, (f % T) * P:(f % T + 1) * P],
                                    K["fwd"][:, t, f * P:(f + 1) * P], xit[:, t, :],
                                    start=(t == 0), stop=(t == T - 1))
                if f % T == T - 1:
                    mm.then_inc(s["dft"], 1)
            eng.wait_ge(s["y"], 1)
            for f in range(NF // P):
                if f == T:
                    eng.wait_ge(s["y"], 2)
                mm = eng.matmul(ps[:, 7, :], y[:, f, :], K["inv"][:, f, :], start=(f == 0),
                                stop=(f == NF // P - 1))
            mm.then_inc(s["inv"], 1)
            norm_tensor(eng, ps, nffn)
            eng.wait_ge(nffn["out"], 2)
            for f in range(FT):
                eng.matmul(ps[:, f, :], K["x1_w1"][:, f * P:(f + 1) * P], hn[:, :], start=True, stop=True)\
                   .then_inc(s["h1"], 1)
            for f in range(FT):
                eng.wait_ge(s["hg"], f + 1)
                mm = eng.matmul(ps[:, 6, :], K["x1_w2"][:, f, :], hg[:, f, :], start=(f == 0), stop=(f == FT - 1))
            mm.then_inc(s["h2"], 1)
            norm_tensor(eng, ps, nout)
            norm_tensor(eng, ps, post)

        @block.scalar
        def _(eng):
            norm_scalar(eng, ps, nin)
            for t in range(T):
                eng.wait_ge(s["neg"], t + 1)
                if t >= 2:
                    eng.wait_ge(s["a"], XH * (t - 1))
                for h in range(XH):
                    eng.activation(e[:, t % 2, h, :], sc[:, t % 2, h, :], ACT.Exp, bias=neg[:, t % 2, h:h + 1])\
                       .then_inc(s["e"], 1)
            eng.wait_ge(s["at"], T)
            eng.activation(at[:, :], ps[:, 4, :], ACT.Copy).then_inc(s["atc"], 1)
            eng.activation(atr[:, :], ps[0:MR, 5, :], ACT.Copy).then_inc(s["atc"], 1)
            eng.wait_ge(s["ct"], 1)
            eng.activation(ct[:, :], ps[:, 6, :], ACT.Copy).then_inc(s["ctc"], 1)
            eng.wait_ge(s["mask"], 1)
            for n in range(4):
                eng.wait_ge(s["film"], n + 1)
                eng.activation(film[:, n, :], ps[:, n, :], ACT.Identity, bias=fb[:, n:n + 1],
                               scale=K["mod_gate"]).then_inc(s["filmc"], 1)
            eng.wait_ge(s["xit"], 1)
            eng.activation(xit[:, :, :], ps[:, 4, :].rearrange("p (t d) -> p t d", t=T), ACT.Copy)\
               .then_inc(s["xitc"], 1)
            norm_scalar(eng, ps, nffn)
            for f in range(FT):
                eng.wait_ge(s["h1"], f + 1)
                eng.activation(hg[:, f, :], ps[:, f, :], ACT.Gelu, bias=K["x1_b1"][:, f:f + 1])\
                   .then_inc(s["hg"], 1)
            norm_scalar(eng, ps, nout)
            norm_scalar(eng, ps, post)

        @block.gpsimd
        def _(eng):
            for t in range(T):
                eng.wait_ge(s["r"], t + 1)
                if t >= 2:
                    eng.wait_ge(s["at"], t - 1)
                for h in range(XH):
                    eng.tensor_scalar(dg[:, t % 2, h, :], K["ident"], r[:, t % 2, h:h + 1], None, ALU.mult)\
                       .then_inc(s["dg"], 1)

        @block.vector
        def _(eng):
            link = chained(eng, s["chain"])
            eng.wait_ge(s["proj"], 1)
            eng.tensor_scalar(qt[:, :], ps[:, 0, :], float(XD) ** -0.5, None, ALU.mult).then_inc(s["qk"], 1)
            eng.wait_ge(s["proj"], 2)
            eng.tensor_copy(kt[:, :], ps[:, 1, 0:M]).then_inc(s["qk"], 1)
            eng.wait_ge(s["proj"], 3)
            eng.tensor_copy(v[:, :], ps[:, 2, 0:P]).then_inc(s["v"], 1)
            eng.wait_ge(s["proj"], 4)
            eng.tensor_copy(vr[:, :], ps[0:MR, 3, 0:P]).then_inc(s["v"], 1)
            link(eng.tensor_scalar(vm[:, :], K["vmask"][:, :], -FAR, FAR, ALU.mult, ALU.add))
            link(eng.tensor_scalar(tm[:, :], K["tmask"][:, :], 1.0 / XH, None, ALU.mult))
            for n, name in enumerate(("x1_fin", "x1_fout")):
                link(eng.tensor_scalar(fb[:, 2 * n:2 * n + 2], K[name], K["mod_gate"], None, ALU.mult))
            for n in (0, 2):
                i = eng.tensor_scalar(fb[:, n:n + 1], fb[:, n:n + 1], 1.0, None, ALU.add)
                if n == 0:
                    link(i)
            i.then_inc(s["mask"], 1)

            def put_x(h):
                c = slice(h * LN_HALF, (h + 1) * LN_HALF)
                return eng.tensor_copy(L["y"][:, c], X[:, c])
            norm_vector(eng, ps, nin, put_x)

            n_mr = 0
            for t in range(T):
                eng.wait_ge(s["sc"], t + 1)
                if t >= 2:
                    eng.wait_ge(s["e"], XH * (t - 1))
                eng.tensor_tensor(sc[:, t % 2, :, :], ps[:, 0:XH, 0:M],
                                  vm[:, :].unsqueeze(1).to_broadcast([P, XH, M]), ALU.add).then_inc(s["scr"], 1)
                eng.wait_ge(s["scr"], t + 1)
                for k in range(ROUNDS):
                    for h in range(XH):
                        src = sc[:, t % 2, h, :] if k == 0 else wk[:, h, :]
                        if k:
                            eng.wait_ge(s["mr"], n_mr + h + 1 - XH)
                        eng.max(m8[:, k, h, :], src).then_inc(s["mx"], 1)
                    if k == 0:
                        eng.wait_ge(s["mx"], t * ROUNDS * XH + XH)
                        eng.tensor_scalar(neg[:, t % 2, :], m8[:, 0, :, 0], -1.0, None, ALU.mult)\
                           .then_inc(s["neg"], 1)
                    for h in range(XH):
                        src = sc[:, t % 2, h, :] if k == 0 else wk[:, h, :]
                        eng.wait_ge(s["mx"], n_mr + h + 1)
                        eng.match_replace(wk[:, h, :], m8[:, k, h, :], src, TAKEN).then_inc(s["mr"], 1)
                    n_mr += XH
                for h in range(XH):
                    eng.wait_ge(s["mr"], n_mr - XH + h + 1)
                    eng.wait_ge(s["e"], XH * t + h + 1)
                    if t >= 2 and h == 0:
                        eng.wait_ge(s["at"], t - 1)
                    eng.scalar_tensor_tensor(a[:, t % 2, h, :], wk[:, h, :], TAKEN / 2, e[:, t % 2, h, :],
                                             ALU.is_le, ALU.mult, accum_out=rs[:, t % 2, h:h + 1])\
                       .then_inc(s["a"], 1)
                eng.wait_ge(s["a"], XH * (t + 1))
                link(eng.reciprocal(rs[:, t % 2, :], rs[:, t % 2, :]))
                eng.tensor_scalar(r[:, t % 2, :], rs[:, t % 2, :], tm[:, t:t + 1], None, ALU.mult)\
                   .then_inc(s["r"], 1)
            eng.wait_ge(s["filmc"], 2)
            link(eng.tensor_tensor(xi[:, :], xn[:, :], film[:, 0, :], ALU.mult))
            eng.tensor_tensor(xi[:, :], xi[:, :], film[:, 1, :], ALU.add).then_inc(s["xi"], 1)
            re, im = ps[:, 5, :].rearrange("p (f d) -> p f d", f=T), ps[:, 6, :].rearrange("p (f d) -> p f d", f=T)
            eng.wait_ge(s["dft"], 1)
            link(eng.tensor_tensor(m[:, 0, :, :], re, kf[:, 0:T, :], ALU.mult))
            link(eng.tensor_tensor(m[:, 2, :, :], re, kf[:, T:, :], ALU.mult))
            eng.wait_ge(s["dft"], 2)
            link(eng.tensor_tensor(m[:, 1, :, :], im, kf[:, T:, :], ALU.mult))
            link(eng.tensor_tensor(m[:, 3, :, :], im, kf[:, 0:T, :], ALU.mult))
            eng.tensor_tensor(y[:, 0:T, :], m[:, 0, :, :], m[:, 1, :, :], ALU.subtract).then_inc(s["y"], 1)
            eng.tensor_tensor(y[:, T:, :], m[:, 2, :, :], m[:, 3, :, :], ALU.add).then_inc(s["y"], 1)

            eng.wait_ge(s["filmc"], 4)
            eng.wait_ge(s["inv"], 1)

            def put_text(h):
                c = slice(h * LN_HALF, (h + 1) * LN_HALF)
                link(eng.scalar_tensor_tensor(z[:, c], xi[:, c], K["x1_dskip"], ps[:, 7, c], ALU.mult, ALU.add))
                link(eng.tensor_tensor(z[:, c], z[:, c], film[:, 2, c], ALU.mult))
                link(eng.tensor_tensor(z[:, c], z[:, c], film[:, 3, c], ALU.add))
                return eng.tensor_tensor(L["y"][:, c], z[:, c], X[:, c], ALU.add)
            norm_vector(eng, ps, nffn, put_text)
            eng.wait_ge(s["h2"], 1)

            def put_fed(h):
                c = slice(h * LN_HALF, (h + 1) * LN_HALF)
                return eng.scalar_tensor_tensor(L["y"][:, c], ps[:, 6, c], K["x1_b2"], L["y"][:, c],
                                                ALU.add, ALU.add)
            norm_vector(eng, ps, nout, put_fed)

            def put_sum(h):
                c = slice(h * LN_HALF, (h + 1) * LN_HALF)
                return eng.tensor_tensor(L["y"][:, c], X[:, c], z[:, c], ALU.add)
            norm_vector(eng, ps, post, put_sum)



WEIGHTS = {
    "m_win": [P, WIN], "m_wout": [P, 2, P],
    "x0_wq": [P, P], "x0_wk": [DC, P], "x0_wv": [DC, P], "x0_wo": [P, P],
    "f0_gate": [P, E0],
    "a1_wq": [P, P], "a1_wk": [P, P], "a1_wv": [P, P], "a1_wo": [P, P],
    "x1_wq": [P, P], "x1_wk": [DC, P], "x1_wv": [DC, P], "x1_win": [P, 2 * P], "x1_wout": [P, 2 * P],
    "x1_w1": [P, FF], "x1_w2": [P, FT, P],
    "f1_router": [P, HOPS, E1], "f1_up": [P, E1, P], "f1_g": [P, E1, P], "f1_down": [P, E1, P],
    "f1_bdown": [E1, P], "f1_sup": [P, NSH * P], "f1_swg": [P, P], "f1_swdown": [P, P],
    "esel": [E1, E1, P], "fwd": [P, T, NF], "inv": [P, NF // P, S],
}
WEIGHT_SOURCE = {
    "m_wout": "(k p) n -> p k n", 
    "x1_w2": "(k p) n -> p k n", "f1_router": "c p e -> p c e", "f1_up": "e p n -> p e n",
    "f1_g": "e p n -> p e n", "f1_down": "e p n -> p e n",
}
NEEDED_FIRST = ("m_win", "m_wout")
SETUP_SEMS = "first weights chain bc"


def setup(nc, stack, I, K, s):
    def keep(name, shape, dt=F32):
        return stack.enter_context(nc.sbuf_tensor(f"k_{name}", shape, dt))
    cols = keep("cols", [P, NCOL])
    rows_ = keep("rows", [P, NROW])
    small = keep("small", [P, NSMALL])
    skew = keep("skew", [P, RW])
    tiles = {n: keep(n, shape) for n, shape in WEIGHTS.items()}
    for n, (a, w) in COL.items():
        K[n] = cols[:, a:a + w]
    for n, (a, w) in ROW.items():
        K[n] = rows_[:, a:a + w]
    for i, n in enumerate(("ident", "centre", "upper", "ones", "shift", "shift_last", "masked")):
        K[n] = small[:, i * P:(i + 1) * P]
    at = 7 * P
    K["headmask"] = small[:, at:at + HG]
    at += HG
    K["colmask"] = small[:, at:at + HG * P].rearrange("p (j n) -> p j n", j=HG)
    at += HG * P
    K["restmask"] = small[:, at:at + HG * P].rearrange("p (j n) -> p j n", j=HG)
    at += HG * P
    K["colmask_dj"] = small[:, at:at + HG * P].rearrange("p (j n) -> p j n", j=HG)
    K.update(tiles)
    K["skew"] = skew
    with nc.Block(no_gpsimd_drain=True) as block:
        n_loads = {"first": 0, "weights": 0}

        @block.sync
        def _(eng):
            def load(dst, src, sem="first"):
                eng.dma_start(dst, src).then_inc(s[sem], 16)
                n_loads[sem] += 1
            load(cols[:, :], I["cols"])
            load(rows_[:, :], bass.AP(I["rows"].tensor, 0, [[0, P], [1, NROW]]))
            load(small[:, :], I["small"])
            load(skew[:, :], I["skew"])
            for n, tile in tiles.items():
                src = I[n]
                if n in WEIGHT_SOURCE:
                    pat = WEIGHT_SOURCE[n]
                    src = src.rearrange(pat, p=P)
                full = tuple(slice(None) for _ in tile.shape)
                load(tile[full], src, "first" if n in NEEDED_FIRST else "weights")
            eng.wait_ge(s["first"], 16 * n_loads["first"])
    return 16 * n_loads["weights"]


FIRST = ("mixer", "cross0", "experts0", "attn1")
SECOND = ("attn1_out", "cross1", "experts1")


def decoder(nc, I, out, first=FIRST, second=SECOND, batches=B):
    with ExitStack() as stack:
        K = {}
        ps = stack.enter_context(nc.psum_tensor("ps", [P, 8, S], F32))
        X = stack.enter_context(nc.sbuf_tensor("x", [P, S], F32))
        ot = stack.enter_context(nc.sbuf_tensor("ot", [P, S], F32))
        ctx = stack.enter_context(nc.sbuf_tensor("ctx", [DC, MP], F32))
        vmask = stack.enter_context(nc.sbuf_tensor("vmask", [P, M], U8))
        tmask = stack.enter_context(nc.sbuf_tensor("tmask", [P, T], U8))
        middle = nc.dram_tensor("middle", (B, P, S), F32, kind="Internal").ap()
        contexts = nc.dram_tensor("contexts", (B, P, S), F32, kind="Internal").ap()
        parts_dram = [nc.dram_tensor(n, (3, P, S), BF16, kind="Internal").ap() for n in ("q_parts", "k_parts")]
        cross_dram = [parts_dram[0], nc.dram_tensor("cross_k_parts", (3, P, M), BF16, kind="Internal").ap()]
        s_set = semaphores(nc, stack, "set", SETUP_SEMS)
        s_io = semaphores(nc, stack, "io", "in out")
        names = {"mixer": A_SEMS, "cross0": B_SEMS, "experts0": C_SEMS, "attn1": D_SEMS, "attn1_out": O_SEMS,
                 "cross1": E_SEMS, "experts1": F_SEMS}
        code = {"mixer": mixer, "cross0": cross0, "experts0": experts0, "attn1_out": attn1_out,
                "cross1": cross1, "experts1": experts1}
        weights_in = setup(nc, stack, I, K, s_set)
        bias_table(nc, stack, K, s_set)
        K["weights_in"] = (s_set["weights"], weights_in)
        K["ctx"], K["vmask"], K["tmask"], K["ot"] = ctx, vmask, tmask, ot

        def layers(which, b):
            last = stack.enter_context(ExitStack())
            for n in which:
                own = stack.enter_context(ExitStack())
                s = semaphores(nc, own, n, names[n])
                if n == "attn1":
                    attn1(nc, K, ps, X, s, b, contexts, parts_dram)
                elif n == "cross0":
                    cross0(nc, K, ps, X, s, cross_dram)
                elif n == "experts0":
                    experts0(nc, K, ps, X, s, I["experts"])
                else:
                    code[n](nc, K, ps, X, s)
                for sem in s.values():
                    nc.gpsimd.sem_clear(sem)
                last.close()
                last = own
            last.close()

        def store(b, to):
            with nc.Block(no_gpsimd_drain=True) as block:
                @block.sync
                def _(eng):
                    eng.dma_start(to[b], X[:, :]).then_inc(s_io["out"], 16)
                    eng.wait_ge(s_io["out"], 16)
            nc.gpsimd.sem_clear(s_io["out"])

        if first:
            with nc.Fori(0, batches) as b:
                with nc.Block(no_gpsimd_drain=True) as block:
                    @block.sync
                    def _(eng):
                        eng.dma_start(X[:, :], I["x"][b]).then_inc(s_io["in"], 16)
                        eng.dma_start(ctx[:, :], I["ctx"][b]).then_inc(s_io["in"], 16)
                        eng.wait_ge(s_io["in"], 32)
                        if "mixer" not in first:
                            eng.wait_ge(s_set["weights"], weights_in)
                nc.gpsimd.sem_clear(s_io["in"])
                layers(first, b)
                store(b, middle if second else out)
        if not first:
            nc.sync.wait_ge(s_set["weights"], weights_in)
            nc.all_engine_barrier()
        if "cross1" in second:
            kernel_spectrum(nc, stack, I, K, ps)
        if second:
            with nc.Fori(0, batches) as b:
                with nc.Block(no_gpsimd_drain=True) as block:
                    @block.sync
                    def _(eng):
                        eng.dma_start(X[:, :], (middle if first else I["x"])[b]).then_inc(s_io["in"], 16)
                        if "attn1" in first:
                            eng.dma_start(ot[:, :], contexts[b]).then_inc(s_io["in"], 16)
                        else:
                            eng.dma_start(ot[:, :], I["x"][b]).then_inc(s_io["in"], 16)
                        eng.dma_start(ctx[:, :], I["ctx"][b]).then_inc(s_io["in"], 16)
                        eng.dma_start(vmask[:, :], bass.AP(I["vmask"].tensor, b * M, [[0, P], [1, M]]))\
                           .then_inc(s_io["in"], 16)
                        eng.dma_start(tmask[:, :], I["tmask"][b]).then_inc(s_io["in"], 16)
                        eng.wait_ge(s_io["in"], 80)
                nc.gpsimd.sem_clear(s_io["in"])
                layers(second, b)
                store(b, out)


def laid_out(inputs):
    a = {k: np.asarray(v) for k, v in inputs.items()}
    f = np.float32
    by_width = np.arange(P).reshape(4, HG, DH).transpose(2, 1, 0).reshape(-1)
    by_group = np.arange(P).reshape(4, HG, DH).transpose(0, 2, 1).reshape(-1)
    cols = {
        "x0_bq": a["L0_xattn_bq"][by_width],
        "x0_bk": a["L0_xattn_bkv"].reshape(NH, 2, DH)[:, 0].reshape(-1)[by_width],
        "x0_bv": a["L0_xattn_bkv"].reshape(NH, 2, DH)[:, 1].reshape(-1), "x0_bo": a["L0_xattn_bo"],
        "f0_b2": a["L0_ffn_b2"].T,
        "a1_bq": a["L1_attn_bq"][by_width], "a1_bk": a["L1_attn_bk"][by_width], "a1_bv": a["L1_attn_bv"][by_group], "a1_bo": a["L1_attn_bo"],
        "x1_fin": a["L1_xattn_b_film_in"].reshape(2, P).T, "x1_fout": a["L1_xattn_b_film_out"].reshape(2, P).T,
        "x1_gin": a["L1_xattn_g_norm_in"], "x1_bin": a["L1_xattn_b_norm_in"],
        "x1_gout": a["L1_xattn_g_norm_out"], "x1_bout": a["L1_xattn_b_norm_out"],
        "x1_gffn": a["L1_xattn_g_ffn"], "x1_bffn": a["L1_xattn_b_ffn"],
        "x1_b1": a["L1_xattn_b1"].reshape(FT, P).T, "x1_b2": a["L1_xattn_b2"], "x1_dskip": a["L1_xattn_D_skip"],
        "f1_bup": a["L1_ffn_exp_bup"].T, "f1_bg": a["L1_ffn_exp_bg"].T,
        "f1_sup_b": a["L1_ffn_share_bup"].reshape(NSH, P).T, "f1_sg": a["L1_ffn_share_bg"],
        "f1_sdown": a["L1_ffn_share_bdown"], "f1_norm": a["L1_ffn_norm_w"].T,
        "m_dcol": np.repeat(a["L0_attn_D_param"], PD).reshape(2, P).T,
        "one": np.ones(P, f), "sign": np.repeat(np.array([1.0, -1.0], f), P // 2),
        "phase": np.repeat(np.array([0.25, 0.0], f), P // 2), "phase2": np.repeat(np.array([0.0, 0.25], f), P // 2),
        "eps5": np.full(P, EPS5, f), "eps6": np.full(P, EPS6, f), "oneD": np.full(P, 1.0 / D, f),
        "half_pi": np.full(P, PI / 2, f),
    }
    packed_cols = np.concatenate([cols[n].reshape(P, w) for n, (_, w) in COL.items()], 1)
    rws = {
        "m_bias8": np.concatenate([a["L0_attn_dt_bias"], np.zeros(HM, f)]),
        "m_bbias": a["L0_attn_B_bias"], "m_cbias": a["L0_attn_C_bias"],
        "m_bnw": a["L0_attn_B_norm_w"], "m_cnw": a["L0_attn_C_norm_w"],
        "et_gate": a["L1_attn_et_gate"], "is_gate": a["L1_attn_is_gate"], "mod_gate": a["L1_xattn_mod_gate"],
        "log_dt": a["L1_xattn_log_dt"], "f1_rb": a["L1_ffn_router_b"], "f1_gb": a["L1_ffn_gate_bias"],
        "jrow": np.arange(JL, dtype=f), "irow": JL * np.arange(IL, dtype=f),
    }
    packed_rows = np.concatenate([rws[n].reshape(-1) for n in ROW])
    at = np.clip(np.arange(RW)[None, :] - np.arange(P)[:, None] - (S - P) + TBL // 2, 0, TBL - 1)
    small, fwd, inv = shape_constants()
    wkv = a["L0_xattn_Wkv"].reshape(NH, 2, DH, DC)
    ctx = np.concatenate([a["ctx_768"].transpose(0, 2, 1), np.zeros((B, DC, MP - M), f)], 2)

    experts = np.concatenate([a["L0_ffn_w1"], a["L0_ffn_b1"].reshape(E0, FT, P).transpose(0, 2, 1),
                              a["L0_ffn_w2"].reshape(E0, FT, P, P).transpose(0, 2, 1, 3).reshape(E0, P, FF)], 2)

    def twice(m):
        return np.concatenate([m.T, m.T], 0)
    arrays = {
        "x": a["x"].transpose(0, 2, 1), "ctx": ctx,
        "vmask": a["mask_BxS2_bf1"], "tmask": a["mask_BxS_bf1"].reshape(B, T, P).transpose(0, 2, 1),
        "cols": packed_cols, "rows": packed_rows, "small": small, "fwd": fwd, "inv": inv,
        "skew": a["L1_attn_time_bias"].reshape(-1)[at],
        "m_win": a["L0_attn_W_in"].T, "m_wout": a["L0_attn_W_out"].T,
        "x0_wq": a["L0_xattn_Wq"].T[:, by_width], "x0_wk": wkv[:, 0].reshape(P, DC).T[:, by_width], "x0_wv": wkv[:, 1].reshape(P, DC).T,
        "x0_wo": a["L0_xattn_Wo"].T,
        "f0_gate": a["L0_ffn_gate_w"], "experts": experts,
        "a1_wq": a["L1_attn_Wq"].T[:, by_width], "a1_wk": a["L1_attn_Wk"].T[:, by_width], "a1_wv": a["L1_attn_Wv"].T[:, by_group],
        "a1_wo": a["L1_attn_Wo"].T,
        "x1_wq": a["L1_xattn_Wq"], "x1_wk": a["L1_xattn_Wk"], "x1_wv": a["L1_xattn_Wv"],
        "x1_win": a["L1_xattn_W_film_in"], "x1_wout": a["L1_xattn_W_film_out"],
        "x1_w1": a["L1_xattn_W1"], "x1_w2": a["L1_xattn_W2"],
        "f1_router": a["L1_ffn_router_W"], "f1_up": a["L1_ffn_exp_Wup"], "f1_g": a["L1_ffn_exp_Wg"],
        "esel": np.repeat(np.eye(E1, dtype=f)[:, :, None], P, 2), "f1_down": a["L1_ffn_exp_Wdown"], "f1_bdown": a["L1_ffn_exp_bdown"],
        "f1_sup": a["L1_ffn_share_Wup"], "f1_swg": a["L1_ffn_share_Wg"], "f1_swdown": a["L1_ffn_share_Wdown"],
        "s4": np.stack([twice(a["L1_xattn_A_re"]), twice(a["L1_xattn_A_im"]), twice(a["L1_xattn_C_re"]),
                        twice(a["L1_xattn_C_im"])], 1),
    }
    return {n: np.ascontiguousarray(v) for n, v in arrays.items()}


def kernel(**inputs):
    import concourse.bacc as bacc
    from concourse.bass_utils import run_bass_kernel_spmd

    arrays = laid_out(inputs)
    nc = bacc.Bacc("TRN2", target_bir_lowering=False, num_devices=1)
    I = {n: nc.dram_tensor(f"in_{n}", a.shape, mybir.dt.from_np(a.dtype), kind="ExternalInput").ap()
         for n, a in arrays.items()}
    out = nc.dram_tensor("out_y", (B, D, S), F32, kind="ExternalOutput").ap()
    decoder(nc, I, out)
    r = run_bass_kernel_spmd(nc, [{f"in_{n}": a for n, a in arrays.items()}], core_ids=[0])
    return np.ascontiguousarray(r.results[0]["out_y"].transpose(0, 2, 1))
```

```python
from contextlib import ExitStack

import numpy as np

import concourse.bass as bass
from concourse import mybir

F32 = mybir.dt.float32
U8 = mybir.dt.uint8
BF16 = mybir.dt.bfloat16
I32 = mybir.dt.int32
ALU = mybir.AluOpType
ACT = mybir.ActivationFunctionType
AX = mybir.AxisListType.X

B, S, D = 4, 512, 128
M, DC = 154, 96
P = 128
T = S // P
MT_, MR = P, M - P
RB = 32
MP = MT_ + RB
HM, PD, NS = 4, 64, 128
NA = 32
WIN = 2 * HM * PD + 2 * NS + 3 * HM + NA
NH, DH, HG = 16, 8, 4
E0, FF = 8, 512
FT = FF // P
EXPERT = FF + FT + FF
XH, XD, TOPK = 4, 32, 32
NST = 64
JL, IL = 32, 16
HD = P // 4
NF = 2 * S
E1, HOPS, NSH = 6, 2, 2
TBL = 500
RW = S + P * (T - 1)

EPS5, EPS6 = 1e-5, 1e-6
MAGIC = 12582912.0
INV2PI = float(1.0 / (2.0 * np.pi))
TURN = 6.283185
FAR = -1.0e30
TAKEN = -3.0e38
PI = float(np.pi)
LN2 = float(np.log(2.0))
LN2_HIGH = 0.693359375
LOG_LEAST, LOG_MOST = -87.0, 88.0
SERIES = [1.0, 1.0, 1 / 2, 1 / 6, 1 / 24, 1 / 120, 1 / 720, 1 / 5040]
EXP_BIAS, EXP_UNIT = 127.0, float(2 ** 23)


def columns():
    widths = [
        ("x0_bq", 1), ("x0_bk", 1), ("x0_bv", 1), ("x0_bo", 1),
        ("f0_b2", E0),
        ("a1_bq", 1), ("a1_bk", 1), ("a1_bv", 1), ("a1_bo", 1),
        ("x1_fin", 2), ("x1_fout", 2), ("x1_gin", 1), ("x1_bin", 1), ("x1_gout", 1), ("x1_bout", 1),
        ("x1_gffn", 1), ("x1_bffn", 1), ("x1_b1", FT), ("x1_b2", 1), ("x1_dskip", 1),
        ("f1_bup", E1), ("f1_bg", E1), ("f1_sup_b", NSH), ("f1_sg", 1), ("f1_sdown", 1),
        ("f1_norm", HOPS), ("m_dcol", 2), ("one", 1), ("sign", 1), ("phase", 1), ("phase2", 1),
        ("eps5", 1), ("eps6", 1), ("oneD", 1), ("half_pi", 1),
    ]
    at, out = 0, {}
    for name, w in widths:
        out[name] = (at, w)
        at += w
    return out, at


COL, NCOL = columns()


def rows():
    widths = [
        ("m_bias8", 2 * HM), ("m_bbias", HM * NS), ("m_cbias", HM * NS), ("m_bnw", NS), ("m_cnw", NS),
        ("et_gate", 1), ("is_gate", 1), ("mod_gate", 1), ("log_dt", D),
        ("f1_rb", HOPS * E1), ("f1_gb", HOPS * E1), ("jrow", JL), ("irow", IL),
    ]
    at, out = 0, {}
    for name, w in widths:
        out[name] = (at, w)
        at += w
    return out, at


ROW, NROW = rows()


def shape_constants():
    p = np.arange(P)
    ident = np.eye(P)
    centre = np.eye(P) - 1.0 / P
    upper = (p[:, None] <= p[None, :])
    ones = np.ones((P, P))
    shift = (p[:, None] == p[None, :] + 1)
    shift_last = np.zeros((P, P))
    shift_last[0, P - 1] = 1.0
    masked = np.where(upper, 0.0, FAR)
    headmask = ((p[:, None] % 32) // DH == np.arange(HG)[None, :])
    colmask = np.zeros((P, HG, P))
    colmask[:] = headmask.T[None]
    colmask_dj = colmask.reshape(P, HG, 4, HG, DH).transpose(0, 1, 2, 4, 3)
    restmask = colmask * (p[:, None, None] // RB == p[None, None, :] // 32)
    square = np.stack([ident, centre, upper, ones, shift, shift_last, masked], 1)
    small = np.concatenate([square.reshape(P, -1), headmask, colmask.reshape(P, -1),
                            restmask.reshape(P, -1), colmask_dj.reshape(P, -1)], 1).astype(np.float32)
    freq = (2 * np.arange(S) + 1)
    phi = (freq[:, None] * np.arange(S)[None, :]) % (4 * S)
    phi = phi * (np.pi / (2 * S))
    fwd = np.concatenate([np.cos(phi), -np.sin(phi)], 0)
    inv = fwd / S
    fwd = fwd.reshape(NF, T, P).transpose(2, 1, 0)
    inv = inv.reshape(NF // P, P, S).transpose(1, 0, 2)
    return small, np.ascontiguousarray(fwd, np.float32), np.ascontiguousarray(inv, np.float32)


NSMALL = 7 * P + HG + 3 * HG * P


def semaphores(nc, stack, prefix, names):
    return {n: stack.enter_context(nc.semaphore(f"{prefix}_{n}")) for n in names.split()}


def chained(eng, sem):
    count = [0]

    def link(ins):
        count[0] += 1
        ins.then_inc(sem, 1)
        eng.wait_ge(sem, count[0])

    return link


NORM_SEMS = "y tr st ag ready root rs ap back out"


def norm_names(*tags):
    return " ".join(f"{tag}_{n}" for tag in tags for n in NORM_SEMS.split())


LN_HALF = S // 2


def norm_tiles(nc, stack, tag):
    def sb(name, shape):
        return stack.enter_context(nc.sbuf_tensor(f"{tag}_{name}", shape, F32))
    return {"y": sb("norm_y", [P, S]), "yt": sb("norm_yt", [P, S]), "st": sb("norm_st", [P, T, 6]),
            "mv": sb("norm_mv", [P, T, 2]), "x": sb("norm_x", [P, T]), "h": sb("norm_h", [P, T]),
            "rs": sb("norm_rs", [P, T]), "nm": sb("norm_nm", [P, T]),
            "early": sb("norm_early", [P, 1])}


def norm_of(K, L, s, tag, there, back, out, centred=True, scale=None, shift=None, eps="eps5"):
    n = {name: s[f"{tag}_{name}"] for name in NORM_SEMS.split()}
    n.update(K=K, L=L, there=there, home=back, to=out, centred=centred, scale=scale, shift=shift, eps=eps)
    return n


def norm_tensor(eng, ps, n):
    L, ident = n["L"], n["K"]["ident"]
    for h in range(2):
        eng.wait_ge(n["y"], h + 1)
        for t in range(2):
            tok = h * LN_HALF + t * P
            mm = eng.transpose(ps[:, n["there"][h], t * P:(t + 1) * P], L["y"][:, tok:tok + P], ident)
        mm.then_inc(n["tr"], 1)
    for h in range(2):
        eng.wait_ge(n["ap"], 2 * h + 2)
        for t in range(2):
            tok = h * LN_HALF + t * P
            mm = eng.transpose(ps[:, n["home"][h], t * P:(t + 1) * P], L["yt"][:, tok:tok + P], ident)
        mm.then_inc(n["back"], 1)


def norm_scalar(eng, ps, n):
    L = n["L"]
    eng.activation(L["early"][:, :], n["K"]["one"], ACT.Sqrt)
    if n["centred"]:
        eng.wait_ge(n["ag"], T)
    else:
        eng.wait_ge(n["ready"], 2)
    eng.activation(L["h"][:, :], L["mv"][:, :, 1] if n["centred"] else L["x"][:, :], ACT.Sqrt,
                   bias=n["K"][n["eps"]]).then_inc(n["root"], 1)
    eng.wait_ge(n["rs"], 2 if n["centred"] else 1)
    eng.wait_ge(n["ap"], 2)
    for t in range(2):
        tok = LN_HALF + t * P
        src = ps[:, n["there"][1], t * P:(t + 1) * P]
        if n["centred"]:
            a = eng.activation(L["yt"][:, tok:tok + P], src, ACT.Identity, scale=L["rs"][:, 2 + t:3 + t],
                               bias=L["nm"][:, 2 + t:3 + t])
        else:
            a = eng.activation(L["yt"][:, tok:tok + P], src, ACT.Copy, scale=L["rs"][:, 2 + t:3 + t])
        a.then_inc(n["ap"], 1)
    eng.wait_ge(n["back"], 2)
    src, dst = ps[:, n["home"][1], 0:LN_HALF], n["to"][:, LN_HALF:S]
    if n["scale"] is None:
        a = eng.activation(dst, src, ACT.Copy)
    elif n["shift"] is None:
        a = eng.activation(dst, src, ACT.Copy, scale=n["scale"])
    else:
        a = eng.activation(dst, src, ACT.Identity, scale=n["scale"], bias=n["shift"])
    a.then_inc(n["out"], 1)


def norm_vector(eng, ps, n, put_y):
    norm_input(eng, n, put_y)
    norm_statistics(eng, ps, n)
    norm_factors(eng, ps, n)
    norm_output(eng, ps, n)


def norm_input(eng, n, put_y):
    for h in range(2):
        put_y(h).then_inc(n["y"], 1)


def norm_statistics(eng, ps, n):
    L = n["L"]
    x, mean, var = L["x"][:, :], L["mv"][:, :, 0], L["mv"][:, :, 1]
    for i in range(T):
        if i % 2 == 0:
            eng.wait_ge(n["tr"], i // 2 + 1)
        eng.bn_stats(L["st"][:, i, :], ps[:, n["there"][i // 2], (i % 2) * P:(i % 2 + 1) * P]).then_inc(n["st"], 1)
    for i in range(T):
        eng.wait_ge(n["st"], i + 1)
        eng.bn_aggr(L["mv"][:, i, :], L["st"][:, i, :]).then_inc(n["ag"], 1)
    eng.wait_ge(n["ag"], T)
    if not n["centred"]:
        eng.tensor_tensor(x, mean, mean, ALU.mult).then_inc(n["ready"], 1)
        eng.wait_ge(n["ready"], 1)
        eng.tensor_tensor(x, x, var, ALU.add).then_inc(n["ready"], 1)


def norm_factors(eng, ps, n):
    L = n["L"]
    rs, mean = L["rs"][:, :], L["mv"][:, :, 0]
    eng.wait_ge(n["root"], 1)
    eng.reciprocal(rs, L["h"][:, :]).then_inc(n["rs"], 1)
    eng.wait_ge(n["rs"], 1)
    if n["centred"]:
        eng.scalar_tensor_tensor(L["nm"][:, :], mean, -1.0, rs, ALU.mult, ALU.mult).then_inc(n["rs"], 1)
    for t in range(2):
        src = ps[:, n["there"][0], t * P:(t + 1) * P]
        if n["centred"]:
            i = eng.tensor_scalar(L["yt"][:, t * P:(t + 1) * P], src, L["mv"][:, t, 0:1], L["rs"][:, t:t + 1],
                                  ALU.subtract, ALU.mult)
        else:
            i = eng.tensor_scalar(L["yt"][:, t * P:(t + 1) * P], src, L["rs"][:, t:t + 1], None, ALU.mult)
        i.then_inc(n["ap"], 1)


def norm_output(eng, ps, n):
    eng.wait_ge(n["back"], 1)
    src, dst = ps[:, n["home"][0], 0:LN_HALF], n["to"][:, 0:LN_HALF]
    if n["scale"] is None:
        i = eng.tensor_copy(dst, src)
    elif n["shift"] is None:
        i = eng.tensor_scalar(dst, src, n["scale"], None, ALU.mult)
    else:
        i = eng.tensor_scalar(dst, src, n["scale"], n["shift"], ALU.mult, ALU.add)
    i.then_inc(n["out"], 1)
    eng.wait_ge(n["out"], 2)



ROWS = 9 * DH
STACKED = 16 * 4
SPLIT_STEPS = 4
STACK_SEMS = "qf kf qs ks kept j0 j1 j2 j3 "


def split(eng, parts, x, sem):
    eng.tensor_copy(parts[:, 0, :], x[:, :]).then_inc(sem, 1)
    eng.wait_ge(sem, 1)
    eng.tensor_tensor(x[:, :], x[:, :], parts[:, 0, :], ALU.subtract).then_inc(sem, 1)
    eng.wait_ge(sem, 2)
    eng.tensor_copy(parts[:, 1, :], x[:, :]).then_inc(sem, 1)
    eng.wait_ge(sem, 3)
    eng.tensor_tensor(parts[:, 2, :], x[:, :], parts[:, 1, :], ALU.subtract).then_inc(sem, 1)


def split_scalar(eng, parts, x, sem):
    eng.activation(parts[:, 0, :], x[:, :], ACT.Copy).then_inc(sem, 1)
    eng.wait_ge(sem, 2)
    eng.activation(parts[:, 1, :], x[:, :], ACT.Copy).then_inc(sem, 1)


def split_vector(eng, parts, x, sem):
    eng.wait_ge(sem, 1)
    eng.tensor_tensor(x[:, :], x[:, :], parts[:, 0, :], ALU.subtract).then_inc(sem, 1)
    eng.wait_ge(sem, 3)
    eng.tensor_tensor(parts[:, 2, :], x[:, :], parts[:, 1, :], ALU.subtract).then_inc(sem, 1)


def stack_parts(eng, s, parts, stacks, dram):
    qs, ks = stacks
    for i, sem in enumerate(("qs", "ks")):
        eng.wait_ge(s[sem], SPLIT_STEPS)
        eng.dma_start(dram[i].rearrange("a p t -> p a t"), parts[i][:, :, :]).then_inc(s["kept"], 16)
    eng.wait_ge(s["kept"], 32)
    nq, nk = qs.shape[2], ks.shape[2]
    for j in range(HG):
        for b in range(3):
            eng.dma_start(ks[3 * DH * b:3 * DH * (b + 1), HG * j:HG * j + HG, :],
                          bass.AP(dram[1].tensor, HG * j * nk + b * P * nk, [[0, 3], [NH * nk, DH], [1, HG * nk]]))\
               .then_inc(s[f"j{j}"], 16)
        eng.dma_start(qs[:, HG * j:HG * j + HG, :],
                      bass.AP(dram[0].tensor, HG * j * nq, [[0, 3], [NH * nq, 3 * DH], [1, HG * nq]]))\
           .then_inc(s[f"j{j}"], 16)



A_SEMS = ("proj small xtok ssq bnsd rstd ne ex ln1 adt q ang qc w theta trig cosr bh ch hdec cumbc "
          "ltd ltm e1 le lw xw btr ctr bt ct cg cb mt y st hst zx zr tg out dg ch2 chain achain " + norm_names("post"))


def mixer(nc, K, ps, xin, X, s):
    with ExitStack() as stack:
        def sb(name, shape):
            return stack.enter_context(nc.sbuf_tensor(f"mix_{name}", shape, F32))
        L = norm_tiles(nc, stack, "mix")
        post = norm_of(K, L, s, "post", (7, 5), (3, 4), X)
        early = sb("early", [P, 1])
        xtok = sb("xtok", [P, T, HM * PD])
        small = sb("small", [P, T, 3 * HM + NA])
        spx = sb("spx", [P, T, 2 * HM])
        ne = sb("ne", [P, T, 3 * HM])
        ex = sb("ex", [P, T, 3 * HM])
        ln1 = sb("ln1", [P, T, 2 * HM])
        spt = sb("spt", [P, T, 2 * HM])
        lam = sb("lam", [P, T, HM])
        adt = sb("adt", [P, T, HM])
        v = sb("v", [P, T, HM])
        q = sb("q", [P, T, HM])
        nqs = sb("nqs", [P, T, HM])
        w = sb("w", [P, T, HM])
        cum = sb("cum", [P, T, HM])
        fend = sb("fend", [P, T, HM])
        ssq = sb("ssq", [P, 2, T])
        rsd = sb("rsd", [P, 2, T])
        ang = sb("ang", [P, T, HM, NA])
        frac = sb("frac", [P, T * HM, NA])
        sn = sb("sn", [P, T * HM, NA])
        co = sb("co", [P, T * HM, NA])
        bn = sb("bn", [P, 2, T, NS])
        bh = sb("bh", [P, T, HM, NS])
        ch = sb("ch", [P, T, HM, NS])
        e1 = sb("e1", [P, T, HM, P])
        lw = sb("lw", [P, T, HM, P])
        dg = sb("dg", [P, T, HM, P])
        bt = sb("bt", [P, T, HM, P])
        ct = sb("ct", [P, T, HM, P])
        junk = bt[:, :, 0:2, :].rearrange("p t h n -> p t h n")
        tb = [lw[:, i, :, :].rearrange("p h (g a) -> p (h g) a", a=NA) for i in range(T)]
        tc = [ct[:, i, :, :].rearrange("p h (g a) -> p (h g) a", a=NA) for i in range(T)]
        cg = ch
        xw = sb("xw", [P, T, HM * PD])
        hst = sb("hst", [P, HM, PD])
        hdec = sb("hdec", [P, HM, PD])
        zr = sb("zr", [P, 2, S])
        xd = sb("xd", [P, 2, S])
        win, wout = K["m_win"], K["m_wout"]
        dt = spt[:, :, 0:HM]
        NB2 = 2 * HM * PD

        block = stack.enter_context(nc.Block(no_gpsimd_drain=True))

        @block.sync
        def _(eng):
            eng.wait_ge(*K["weights_in"])

        @block.tensor
        def _(eng):
            for t in range(T):
                n = 3 * HM + NA
                mm = eng.matmul(ps[:, 4, t * n:(t + 1) * n], xin[:, t * P:(t + 1) * P], win[:, 768:WIN],
                                start=True, stop=True)
            mm.then_inc(s["small"], 1)
            for t in range(T):
                eng.matmul(ps[:, t, :], xin[:, t * P:(t + 1) * P], win[:, 256:768], start=True, stop=True)\
                   .then_inc(s["proj"], 1)
            eng.wait_ge(s["q"], 1)
            qf = q[:, :, :].rearrange("p t h -> p (t h)")
            nq = T * HM
            eng.matmul(ps[:, 4, 192:192 + nq], K["shift"], qf, start=True, stop=False)
            eng.matmul(ps[:, 4, 192:192 + nq - HM], K["shift_last"], qf[:, HM:nq], start=False, stop=True)
            eng.wait_ge(s["adt"], 1)
            eng.matmul(ps[:, 4, 208:208 + nq], K["upper"], adt[:, :, :].rearrange("p t h -> p (t h)"),
                       start=True, stop=True).then_inc(s["qc"], 1)
            eng.wait_ge(s["ang"], 1)
            af = ang[:, :, :, :].rearrange("p t h a -> p (t h a)")
            eng.matmul(ps[:, 5, :], K["upper"], af, start=True, stop=False)
            for back in range(1, T):
                mm = eng.matmul(ps[:, 5, back * P:S], K["ones"], af[:, 0:S - back * P], start=False,
                                stop=(back == T - 1))
            mm.then_inc(s["theta"], 1)
            for k in range(2):
                eng.matmul(ps[:, 6 + k, :], win[:, k * P:(k + 1) * P], xin[:, :], start=True, stop=True)\
                   .then_inc(s["zx"], 1)
            for k in range(2):
                eng.wait_ge(s["zr"], k + 1)
                eng.matmul(ps[:, 6 + k, :], win[:, (2 + k) * P:(3 + k) * P], xin[:, :], start=True, stop=True)\
                   .then_inc(s["zx"], 1)

            def sums(c):
                if c == 0:
                    eng.wait_ge(s["trig"], 1)
                else:
                    eng.wait_ge(s["e1"], c)
                    eng.wait_ge(s["ltd"], c)
                for h in range(HM):
                    mm = eng.matmul(ps[:, 5, h * P:(h + 1) * P], adt[:, c, h:h + 1].to_broadcast([P, P]),
                                    K["upper"], start=True, stop=True)
                mm.then_inc(s["cumbc"], 1)

            def turns(c):
                if c == 0:
                    eng.wait_ge(s["bh"], T + 6)
                    eng.wait_ge(s["xtok"], T)
                else:
                    eng.wait_ge(s["bt"], c)
                for h in range(HM):
                    mm = eng.transpose(ps[:, 2, h * P:(h + 1) * P], bh[:, c, h, :], K["ident"])
                mm.then_inc(s["btr"], 1)
                if c == 0:
                    eng.wait_ge(s["ch"], T + 4)
                else:
                    eng.wait_ge(s["ct"], c)
                    eng.wait_ge(s["cg"], c)
                for h in range(HM):
                    mm = eng.transpose(ps[:, 3, h * P:(h + 1) * P], ch[:, c, h, :], K["ident"])
                mm.then_inc(s["ctr"], 1)

            def scores(c):
                eng.wait_ge(s["bt"], c + 1)
                eng.wait_ge(s["ct"], c + 1)
                if c == 0:
                    eng.wait_ge(s["zr"], 4)
                else:
                    eng.wait_ge(s["mt"], c)
                for h in range(HM):
                    mm = eng.matmul(ps[:, 6, h * P:(h + 1) * P], bt[:, c, h, :], ct[:, c, h, :],
                                    start=True, stop=True)
                mm.then_inc(s["cb"], 1)

            def outputs(c):
                eng.wait_ge(s["mt"], c + 1)
                if c > 0:
                    eng.wait_ge(s["cg"], c + 1)
                    eng.wait_ge(s["hst"], c)
                for h in range(HM):
                    o = ps[64 * (h % 2):64 * (h % 2) + 64, h // 2, c * P:(c + 1) * P]
                    mm = eng.matmul(o, xtok[:, c, h * PD:(h + 1) * PD], lw[:, c, h, :], start=True,
                                    stop=(c == 0))
                    if c > 0:
                        mm = eng.matmul(o, hst[:, h, :], cg[:, c, h, :], start=False, stop=True)
                mm.then_inc(s["y"], 1)
                if c < T - 1:
                    eng.wait_ge(s["xw"], 2 * c + 2)
                    for h in range(HM):
                        mm = eng.matmul(ps[:, 4, 256 + h * PD:256 + (h + 1) * PD], bh[:, c, h, :],
                                        xw[:, c, h * PD:(h + 1) * PD], start=True, stop=True)
                    mm.then_inc(s["st"], 1)

            sums(0)
            sums(1)
            for c in range(T):
                turns(c)
                if c + 2 < T:
                    sums(c + 2)
                if c > 0:
                    outputs(c - 1)
                scores(c)
            outputs(T - 1)
            for h in range(2):
                cols = slice(h * LN_HALF, (h + 1) * LN_HALF)
                eng.wait_ge(s["tg"], 2 * h + 2)
                for k in range(2):
                    mm = eng.matmul(ps[:, (2, 6)[h], 0:LN_HALF], wout[:, k, :], zr[:, k, cols], start=(k == 0),
                                    stop=(k == 1))
                mm.then_inc(s["out"], 1)
            norm_tensor(eng, ps, post)

        @block.scalar
        def _(eng):
            link = chained(eng, s["achain"])
            eng.wait_ge(s["ne"], 1)
            eng.activation(ex[:, :, :], ne[:, :, :], ACT.Exp).then_inc(s["ex"], 1)
            eng.wait_ge(s["ex"], 1)
            eng.activation(ln1[:, :, :], ex[:, :, 0:2 * HM], ACT.Ln, bias=K["one"]).then_inc(s["ln1"], 1)
            for t in range(T):
                eng.wait_ge(s["proj"], t + 1)
                eng.activation(xtok[:, t, :], ps[:, t, 0:256], ACT.Copy).then_inc(s["xtok"], 1)
                for k in range(2):
                    a = eng.activation(junk[:, t, k, :], ps[:, t, 256 + k * NS:256 + (k + 1) * NS],
                                       ACT.Square, accum_out=ssq[:, k, t:t + 1])
                    a.then_inc(s["ssq"], 1)
            eng.wait_ge(s["ssq"], 2 * T)
            link(eng.activation(ssq[:, :, :], ssq[:, :, :], ACT.Sqrt, bias=K["eps5"], scale=1.0 / NS))
            def gates():
                for k in range(2):
                    eng.wait_ge(s["zx"], 1 + k)
                    eng.activation(zr[:, k, :], ps[:, 6 + k, :], ACT.Copy).then_inc(s["zr"], 1)

            def skips():
                for k in range(2):
                    eng.wait_ge(s["zx"], 3 + k)
                    eng.activation(xd[:, k, :], ps[:, 6 + k, :], ACT.Copy, scale=K["m_dcol"][:, k:k + 1])\
                       .then_inc(s["zr"], 1)

            def decays(c):
                eng.wait_ge(s["cumbc"], c + 1)
                eng.activation(e1[:, c, :, :], ps[:, 5, :].rearrange("p (h t) -> p h t", h=HM), ACT.Exp)\
                   .then_inc(s["e1"], 1)
                eng.wait_ge(s["ltm"], c + 1)
                eng.activation(lw[:, c, :, :], lw[:, c, :, :], ACT.Exp).then_inc(s["le"], 1)

            eng.activation(early[:, :], K["one"], ACT.Sin)
            eng.wait_ge(s["trig"], 1)
            eng.activation(sn[:, :, :], frac[:, :, :], ACT.Sin, scale=TURN).then_inc(s["cosr"], 1)
            eng.activation(co[:, :, :], frac[:, :, :], ACT.Sin, scale=TURN / 2).then_inc(s["cosr"], 1)
            gates()
            decays(0)
            skips()
            decays(1)
            for c in range(T):
                eng.wait_ge(s["btr"], c + 1)
                eng.activation(bt[:, c, :, :], ps[:, 2, :].rearrange("p (h t) -> p h t", h=HM), ACT.Copy)\
                   .then_inc(s["bt"], 1)
                eng.wait_ge(s["ctr"], c + 1)
                eng.activation(ct[:, c, :, :], ps[:, 3, :].rearrange("p (h t) -> p h t", h=HM), ACT.Copy)\
                   .then_inc(s["ct"], 1)
                if c + 2 < T:
                    decays(c + 2)
            eng.wait_ge(s["zr"], 4)
            link(eng.activation(zr[:, :, :], zr[:, :, :], ACT.Silu))
            norm_scalar(eng, ps, post)

        @block.gpsimd
        def _(eng):
            eng.wait_ge(s["rstd"], 1 + 2 * T)
            for c in range(T):
                eng.tensor_tensor(ch[:, c, :, :], bn[:, 1, c, :].unsqueeze(1).to_broadcast([P, HM, NS]),
                                  K["m_cbias"].rearrange("p (h n) -> p h n", h=HM), ALU.add)\
                   .then_inc(s["ch"], 1)
            eng.wait_ge(s["ch"], T)
            eng.wait_ge(s["cosr"], 4)
            products(eng, ch, tc, sn, co, s["ch"], (0, 1))
            for c in range(T):
                eng.wait_ge(s["ltd"], c + 1)
                eng.tensor_tensor(lw[:, c, :, :], lw[:, c, :, :],
                                  K["masked"].unsqueeze(1).to_broadcast([P, HM, P]), ALU.add)\
                   .then_inc(s["ltm"], 1)
                eng.wait_ge(s["w"], 1)
                eng.tensor_tensor(dg[:, c, :, :], K["ident"].unsqueeze(1).to_broadcast([P, HM, P]),
                                  nqs[:, c, :].unsqueeze(2).to_broadcast([P, HM, P]), ALU.mult)\
                   .then_inc(s["dg"], 1)
                if c == T - 1:
                    break
                eng.wait_ge(s["le"], c + 1)
                eng.tensor_tensor(fend[:, c, :], lw[:, c, :, P - 1], w[:, c, :], ALU.mult)\
                   .then_inc(s["xw"], 1)
                eng.wait_ge(s["xw"], 2 * c + 1)
                eng.tensor_tensor(xw[:, c, :].rearrange("p (h d) -> p h d", h=HM),
                                  xtok[:, c, :].rearrange("p (h d) -> p h d", h=HM),
                                  fend[:, c, :].unsqueeze(2).to_broadcast([P, HM, PD]), ALU.mult)\
                   .then_inc(s["xw"], 1)

        @block.vector
        def _(eng):
            link = chained(eng, s["chain"])
            eng.wait_ge(s["small"], 1)
            link(eng.tensor_copy(small[:, :, :], ps[:, 4, 0:176].rearrange("p (t n) -> p t n", t=T)))
            link(eng.tensor_tensor(spx[:, :, :], small[:, :, 0:2 * HM],
                                   K["m_bias8"].unsqueeze(1).to_broadcast([P, T, 2 * HM]), ALU.add))
            link(eng.tensor_scalar(ne[:, :, 2 * HM:], small[:, :, 2 * HM:3 * HM], -1.0, None, ALU.mult))
            eng.scalar_tensor_tensor(ne[:, :, 0:2 * HM], spx[:, :, :], -1.0, spx[:, :, :], ALU.mult,
                                     ALU.min).then_inc(s["ne"], 1)
            eng.wait_ge(s["ln1"], 1)
            link(eng.scalar_tensor_tensor(spt[:, :, :], spx[:, :, :], 0.0, ln1[:, :, :], ALU.max, ALU.add))
            link(eng.tensor_scalar(lam[:, :, :], ex[:, :, 2 * HM:], 1.0, None, ALU.add))
            link(eng.reciprocal(lam[:, :, :], lam[:, :, :]))
            link(eng.tensor_scalar(adt[:, :, :], spt[:, :, HM:], 1e-4, -1.0, ALU.max, ALU.mult))
            eng.tensor_tensor(adt[:, :, :], adt[:, :, :], dt, ALU.mult).then_inc(s["adt"], 1)
            link(eng.tensor_tensor(v[:, :, :], dt, lam[:, :, :], ALU.mult))
            eng.tensor_tensor(q[:, :, :], dt, v[:, :, :], ALU.subtract).then_inc(s["q"], 1)
            eng.tensor_tensor(ang[:, :, :, :],
                              small[:, :, 3 * HM:].unsqueeze(2).to_broadcast([P, T, HM, NA]),
                              dt.unsqueeze(3).to_broadcast([P, T, HM, NA]), ALU.mult).then_inc(s["ang"], 1)
            eng.wait_ge(s["achain"], 1)
            eng.reciprocal(rsd[:, :, :], ssq[:, :, :]).then_inc(s["rstd"], 1)
            eng.wait_ge(s["rstd"], 1)
            for k, nw in ((0, "m_bnw"), (1, "m_cnw")):
                for t in range(T):
                    i = eng.scalar_tensor_tensor(bn[:, k, t, :], ps[:, t, 256 + k * NS:256 + (k + 1) * NS],
                                                 rsd[:, k, t:t + 1], K[nw], ALU.mult, ALU.mult)
                    i.then_inc(s["rstd"], 1)
            eng.wait_ge(s["rstd"], 1 + 2 * T)
            eng.wait_ge(s["qc"], 1)
            link(eng.tensor_scalar(nqs[:, :, :], ps[:, 4, 192:208].rearrange("p (t h) -> p t h", t=T), -1.0,
                                   None, ALU.mult))
            link(eng.tensor_copy(cum[:, :, :], ps[:, 4, 208:224].rearrange("p (t h) -> p t h", t=T)))
            eng.tensor_tensor(w[:, :, :], v[:, :, :], nqs[:, :, :], ALU.subtract).then_inc(s["w"], 1)
            eng.wait_ge(s["theta"], 1)
            th = ps[:, 5, :].rearrange("p (n a) -> p n a", a=NA)
            link(eng.tensor_scalar(frac[:, :, :], th, INV2PI, MAGIC, ALU.mult, ALU.add))
            link(eng.tensor_scalar(frac[:, :, :], frac[:, :, :], -MAGIC, None, ALU.add))
            eng.scalar_tensor_tensor(frac[:, :, :], th, INV2PI, frac[:, :, :], ALU.mult, ALU.subtract)\
               .then_inc(s["trig"], 1)
            for c in range(T):
                eng.tensor_tensor(bh[:, c, :, :], bn[:, 0, c, :].unsqueeze(1).to_broadcast([P, HM, NS]),
                                  K["m_bbias"].rearrange("p (h n) -> p h n", h=HM), ALU.add)\
                   .then_inc(s["bh"], 1)
            eng.wait_ge(s["cosr"], 2)
            eng.tensor_tensor(co[:, :, :], co[:, :, :], co[:, :, :], ALU.mult).then_inc(s["cosr"], 1)
            eng.wait_ge(s["cosr"], 3)
            eng.tensor_scalar(co[:, :, :], co[:, :, :], -2.0, 1.0, ALU.mult, ALU.add).then_inc(s["cosr"], 1)

            def differences(c):
                eng.wait_ge(s["e1"], c + 1)
                eng.tensor_tensor(lw[:, c, :, :], ps[:, 5, :].rearrange("p (h t) -> p h t", h=HM),
                                  cum[:, c, :].unsqueeze(2).to_broadcast([P, HM, P]), ALU.subtract)\
                   .then_inc(s["ltd"], 1)

            def weigh(c):
                eng.wait_ge(s["dg"], c + 1)
                if c < T - 1:
                    eng.wait_ge(s["xw"], 2 * c + 1)
                else:
                    eng.wait_ge(s["le"], T)
                for h in range(HM):
                    eng.scalar_tensor_tensor(lw[:, c, h, :], lw[:, c, h, :], w[:, c, h:h + 1], dg[:, c, h, :],
                                             ALU.mult, ALU.add).then_inc(s["lw"], 1)
            eng.wait_ge(s["bh"], T)
            eng.wait_ge(s["cosr"], 4)
            products(eng, bh, tb, sn, co, s["bh"], range(4))
            combine(eng, bh, tb, s["bh"], T)
            eng.wait_ge(s["bh"], T + 6)
            differences(0)
            eng.wait_ge(s["ch"], T + 2)
            products(eng, ch, tc, sn, co, s["ch2"], (2, 3))
            eng.wait_ge(s["ch2"], 2)
            combine(eng, ch, tc, s["ch"], T - 2)
            differences(1)
            weigh(0)
            for c in range(T):
                eng.wait_ge(s["ct"], c + 1)
                eng.tensor_tensor(cg[:, c, :, :], ps[:, 3, :].rearrange("p (h t) -> p h t", h=HM),
                                  e1[:, c, :, :], ALU.mult).then_inc(s["cg"], 1)
                if c + 2 < T:
                    differences(c + 2)
                if 0 < c:
                    state_update(eng, c - 1, s, ps, hst, hdec, e1)
                eng.wait_ge(s["lw"], HM * (c + 1))
                eng.wait_ge(s["cb"], c + 1)
                eng.tensor_tensor(lw[:, c, :, :], ps[:, 6, :].rearrange("p (h t) -> p h t", h=HM),
                                  lw[:, c, :, :], ALU.mult).then_inc(s["mt"], 1)
                if c + 1 < T:
                    weigh(c + 1)
            eng.wait_ge(s["achain"], 2)
            for h in range(2):
                c = slice(h * LN_HALF, (h + 1) * LN_HALF)
                eng.wait_ge(s["y"], T)
                for k in range(2):
                    link(eng.tensor_tensor(xd[:, k, c], ps[:, k, c], xd[:, k, c], ALU.add))
                    eng.tensor_tensor(zr[:, k, c], xd[:, k, c], zr[:, k, c], ALU.mult).then_inc(s["tg"], 1)

            def sums(h):
                c = slice(h * LN_HALF, (h + 1) * LN_HALF)
                eng.wait_ge(s["out"], h + 1)
                return eng.tensor_tensor(L["y"][:, c], ps[:, (2, 6)[h], 0:LN_HALF], xin[:, c], ALU.add)
            norm_vector(eng, ps, post, sums)


def state_update(eng, c, s, ps, hst, hdec, e1):
    new = ps[:, 4, 256:512].rearrange("p (h d) -> p h d", h=HM)
    eng.wait_ge(s["st"], c + 1)
    if c == 0:
        eng.tensor_copy(hst[:, :, :], new).then_inc(s["hst"], 1)
    else:
        eng.wait_ge(s["hst"], c)
        eng.tensor_tensor(hdec[:, :, :], hst[:, :, :],
                          e1[:, c, :, P - 1:P].to_broadcast([P, HM, PD]), ALU.mult).then_inc(s["hdec"], 1)
        eng.wait_ge(s["hdec"], c)
        eng.wait_ge(s["y"], c + 1)
        eng.tensor_tensor(hst[:, :, :], new, hdec[:, :, :], ALU.add).then_inc(s["hst"], 1)


def halves(vec):
    flat = vec[:, :, :, :].rearrange("p t h n -> p (t h) n")
    return flat[:, :, 0:NA], flat[:, :, NA:2 * NA]


def products(eng, vec, tmp, sn, co, sem, which):
    v1, v2 = halves(vec)
    four = ((v1, co), (v2, sn), (v1, sn), (v2, co))
    for i in which:
        eng.tensor_tensor(tmp[i], four[i][0], four[i][1][:, :, :], ALU.mult).then_inc(sem, 1)


def combine(eng, vec, tmp, sem, count):
    v1, v2 = halves(vec)
    eng.wait_ge(sem, count + 4)
    eng.tensor_tensor(v1, tmp[0], tmp[1], ALU.subtract).then_inc(sem, 1)
    eng.tensor_tensor(v2, tmp[2], tmp[3], ALU.add).then_inc(sem, 1)



B_SEMS = (STACK_SEMS + "proj vp bo pad sc mn p rest tm tr pt ptr pv rs rex rt rtb ot out chain achain "
          + norm_names("post"))


def cross0(nc, K, ps, X, s, parts_dram):
    with ExitStack() as stack:
        def sb(name, shape):
            return stack.enter_context(nc.sbuf_tensor(f"c0_{name}", shape, F32))
        L = norm_tiles(nc, stack, "c0")
        post = norm_of(K, L, s, "post", (2, 3), (5, 6), X)
        scale = float(DH) ** -0.5
        ctx = K["ctx"]

        def half(name, shape):
            return stack.enter_context(nc.sbuf_tensor(f"c0_{name}", shape, BF16))
        qf = sb("qf", [P, S])
        kf = sb("kf", [P, M])
        parts = [half("qparts", [P, 3, S]), half("kparts", [P, 3, M])]
        qs = half("qs", [ROWS, NH, S])
        ks = half("ks", [ROWS, NH, M])
        vp = sb("vp", [P, HG, P])
        vr = sb("vr", [P, HG, P])
        bo = sb("bo", [P, 1])
        mn = sb("mn", [P, 32, 2])
        p = sb("p", [P, 4, 2, MP])
        pr = sb("pr", [P, 2, 2, HG, RB])
        pt = sb("pt", [P, 2, HG, S])
        ptr = sb("ptr", [P, 2, S])
        rs = sb("rs", [P, T, NH])
        rex = sb("rex", [P, T, P])
        rt = sb("rt", [P, S])
        ot = sb("ot", [P, S])
        steps = [(j, qp, g) for j in range(HG) for qp in range(2) for g in range(4)]
        N = len(steps)
        block = stack.enter_context(nc.Block(no_gpsimd_drain=True))

        @block.tensor
        def _(eng):
            eng.matmul(ps[:, 0, :], K["x0_wq"][:, :], X[:, :], start=True, stop=True).then_inc(s["proj"], 1)
            eng.matmul(ps[:, 1, 0:M], K["x0_wk"][:, :], ctx[:, 0:M], start=True, stop=True)\
               .then_inc(s["proj"], 1)
            eng.matmul(ps[:, 2, 0:P], ctx[:, 0:P], K["x0_wv"][:, :], start=True, stop=True)\
               .then_inc(s["proj"], 1)
            for g in range(4):
                mm = eng.matmul(ps[32 * g:32 * g + 32, 3, 0:P], ctx[:, P:MP], K["x0_wv"][:, :],
                                start=True, stop=True)
            mm.then_inc(s["proj"], 1)
            eng.matmul(ps[:, 4, 0:1], K["x0_wo"][:, :], K["x0_bv"], start=True, stop=True)\
               .then_inc(s["proj"], 1)

            def scores(n):
                j, qp, g = steps[n]
                if n == 0:
                    eng.wait_ge(s["qf"], 1)
                    eng.wait_ge(s["kf"], 1)
                    eng.wait_ge(s["vp"], 2)
                if qp == 0 and g == 0:
                    eng.wait_ge(s[f"j{j}"], STACKED)
                if n >= 4:
                    eng.wait_ge(s["p"], n - 3)
                for i in range(2):
                    t = 2 * qp + i
                    mm = eng.matmul(ps[:, g, i * M:(i + 1) * M], qs[:, HG * j + g, t * P:(t + 1) * P],
                                    ks[:, HG * j + g, :], start=True, stop=True)
                mm.then_inc(s["sc"], 1)

            def turn(n):
                j, qp, g = steps[n]
                eng.wait_ge(s["p"], n + 1)
                if n == 0:
                    eng.wait_ge(s["bo"], 1)
                if n % 2 == 0 and n >= 4:
                    eng.wait_ge(s["pt"], n // 2 - 1)
                for i in range(2):
                    mm = eng.transpose(ps[:, 4 + (n // 2) % 2, (2 * (n % 2) + i) * P:(2 * (n % 2) + i + 1) * P],
                                       p[:, n % 4, i, 0:P], K["ident"])
                mm.then_inc(s["tm"], 1)
                if g == 3:
                    u = n // 4
                    eng.wait_ge(s["rest"], n + 1)
                    if u >= 1:
                        eng.wait_ge(s["ptr"], u)
                    for i in range(2):
                        mm = eng.transpose(ps[:, 6, i * P:(i + 1) * P],
                                           pr[:, u % 2, i, :, :].rearrange("p g m -> p (g m)"), K["ident"])
                    mm.then_inc(s["tr"], 1)

            def values(j):
                eng.wait_ge(s["pt"], 4 * j + 4)
                for g in range(4):
                    eng.matmul(ps[32 * g:32 * g + 32, 7, :], vp[:, j, 32 * g:32 * g + 32],
                               pt[:, j % 2, g, :], start=(j == 0), stop=False, skip_group_check=True)

            def values_rest(j):
                eng.wait_ge(s["ptr"], 2 * j + 2)
                eng.matmul(ps[:, 7, :], vr[:, j, :], ptr[:, j % 2, :], start=False, stop=(j == HG - 1),
                           skip_group_check=True).then_inc(s["pv"], 1)

            for n in range(4):
                scores(n)
            for n in range(N):
                if n + 4 < N:
                    scores(n + 4)
                turn(n)
                if n % 8 == 2 and n > 8:
                    values(n // 8 - 1)
                if n % 8 == 5 and n > 8:
                    values_rest(n // 8 - 1)
            values(HG - 1)
            values_rest(HG - 1)
            eng.wait_ge(s["rex"], 1)
            for t in range(T):
                mm = eng.transpose(ps[:, 4, t * P:(t + 1) * P], rex[:, t, :], K["ident"])
            mm.then_inc(s["rtb"], 1)
            for h in range(2):
                eng.wait_ge(s["ot"], h + 1)
                eng.matmul(ps[:, h, 0:LN_HALF], K["x0_wo"][:, :], ot[:, h * LN_HALF:(h + 1) * LN_HALF],
                           start=True, stop=True).then_inc(s["out"], 1)
            norm_tensor(eng, ps, post)

        @block.sync
        def _(eng):
            stack_parts(eng, s, parts, (qs, ks), parts_dram)

        @block.scalar
        def _(eng):
            eng.wait_ge(s["proj"], 2)
            eng.activation(kf[:, :], ps[:, 1, 0:M], ACT.Identity, bias=K["x0_bk"]).then_inc(s["kf"], 1)
            eng.wait_ge(s["kf"], 1)
            split_scalar(eng, parts[1], kf, s["ks"])

            def rest_back(u):
                j, qp, _ = steps[4 * u]
                eng.wait_ge(s["tr"], u + 1)
                if u >= 4:
                    eng.wait_ge(s["pv"], j - 1)
                eng.activation(ptr[:, j % 2, qp * 2 * P:(qp + 1) * 2 * P], ps[:, 6, 0:2 * P], ACT.Copy)\
                   .then_inc(s["ptr"], 1)

            for n, (j, qp, g) in enumerate(steps):
                eng.wait_ge(s["mn"], n + 1)
                if n == 0:
                    eng.wait_ge(s["pad"], 1)
                if n >= 4:
                    eng.wait_ge(s["tm"], n - 3)
                    eng.wait_ge(s["rest"], n - 3)
                for i in range(2):
                    t, h = 2 * qp + i, 4 * g + j
                    a = eng.activation(p[:, n % 4, i, 0:M], ps[:, g, i * M:(i + 1) * M], ACT.Exp,
                                       bias=mn[:, n, i:i + 1], scale=-1.0, accum_out=rs[:, t, h:h + 1])
                a.then_inc(s["p"], 1)
                if g == 1 and n > 4:
                    rest_back(n // 4 - 1)
            rest_back(N // 4 - 1)
            eng.wait_ge(s["rtb"], 1)
            eng.activation(rt[:, :], ps[:, 4, :], ACT.Copy).then_inc(s["rt"], 1)
            norm_scalar(eng, ps, post)

        @block.gpsimd
        def _(eng):
            eng.memset(p[:, :, :, M:MP], 0.0).then_inc(s["pad"], 1)
            eng.wait_ge(s["pad"], 1)
            for n, (j, qp, g) in enumerate(steps):
                u = n // 4
                eng.wait_ge(s["p"], n + 1)
                if g == 0 and u >= 2:
                    eng.wait_ge(s["tr"], u - 1)
                eng.tensor_copy(pr[:, u % 2, :, g, :], p[:, n % 4, :, P:MP]).then_inc(s["rest"], 1)

        @block.vector
        def _(eng):
            link = chained(eng, s["chain"])
            eng.wait_ge(s["proj"], 1)
            eng.tensor_scalar(qf[:, :], ps[:, 0, :], K["x0_bq"], -scale, ALU.add, ALU.mult).then_inc(s["qf"], 1)
            eng.wait_ge(s["qf"], 1)
            split(eng, parts[0], qf, s["qs"])
            eng.wait_ge(s["kf"], 1)
            split_vector(eng, parts[1], kf, s["ks"])
            for dst, bank, mask in ((vp, 2, "colmask"), (vr, 3, "restmask")):
                eng.wait_ge(s["proj"], bank + 1)
                eng.tensor_tensor(dst[:, :, :], ps[:, bank, 0:P].unsqueeze(1).to_broadcast([P, HG, P]),
                                  K[mask], ALU.mult).then_inc(s["vp"], 1)
            eng.wait_ge(s["proj"], 5)
            eng.tensor_tensor(bo[:, :], ps[:, 4, 0:1], K["x0_bo"], ALU.add).then_inc(s["bo"], 1)

            def minimum(n):
                j, qp, g = steps[n]
                eng.wait_ge(s["sc"], n + 1)
                eng.tensor_reduce(mn[:, n, :], ps[:, g, 0:2 * M].rearrange("p (i m) -> p i m", i=2), AX,
                                  ALU.min).then_inc(s["mn"], 1)

            def evacuate(k):
                j, qp, g = steps[2 * k]
                eng.wait_ge(s["tm"], 2 * k + 2)
                if j >= 2:
                    eng.wait_ge(s["pv"], j - 1)
                eng.tensor_copy(pt[:, j % 2, g:g + 2, qp * 2 * P:(qp + 1) * 2 * P],
                                ps[:, 4 + k % 2, :].rearrange("p (g q) -> p g q", g=2)).then_inc(s["pt"], 1)

            for n in range(N):
                minimum(n)
                if n % 2 == 1 and n >= 5:
                    evacuate((n - 5) // 2)
            evacuate(N // 2 - 2)
            evacuate(N // 2 - 1)
            eng.wait_ge(s["p"], N)
            link(eng.reciprocal(rs[:, :, :], rs[:, :, :]))
            eng.tensor_copy(rex[:, :, :].rearrange("p t (h d) -> p t h d", d=DH),
                            rs[:, :, :].unsqueeze(3).to_broadcast([P, T, NH, DH])).then_inc(s["rex"], 1)
            eng.wait_ge(s["rt"], 1)
            eng.wait_ge(s["pv"], HG)
            for h in range(2):
                c = slice(h * LN_HALF, (h + 1) * LN_HALF)
                eng.tensor_tensor(ot[:, c], ps[:, 7, c], rt[:, c], ALU.mult).then_inc(s["ot"], 1)

            def put_y(h):
                c = slice(h * LN_HALF, (h + 1) * LN_HALF)
                eng.wait_ge(s["out"], h + 1)
                return eng.scalar_tensor_tensor(L["y"][:, c], ps[:, h, 0:LN_HALF], bo[:, 0:1], X[:, c],
                                                ALU.add, ALU.add)
            norm_vector(eng, ps, post, put_y)



C_SEMS = ("mean logits pad m8 ee chosen w1 w2 hid g down acc chain " + norm_names("post"))


def experts0(nc, K, ps, X, s, experts, fetch_next):
    with ExitStack() as stack:
        def sb(name, shape):
            return stack.enter_context(nc.sbuf_tensor(f"e0_{name}", shape, F32))
        L = norm_tiles(nc, stack, "e0")
        post = norm_of(K, L, s, "post", (0, 1), (2, 3), X)
        xm = sb("xm", [P, 1])
        lg = sb("lg", [P, 2 * E0])
        m8 = sb("m8", [P, 8])
        rp = sb("rp", [P, 8])
        wk = sb("wk", [P, 2 * E0])
        nm = sb("nm", [P, 1])
        ee = sb("ee", [P, E0])
        cw = sb("cw", [P, E0])
        tot = sb("tot", [P, 1])
        be = sb("be", [P, 1])
        jk = sb("jk", [P, E0])
        sel = sb("sel", [P, E0])
        num = sb("num", [P, 2])
        numi = stack.enter_context(nc.sbuf_tensor("e0_numi", [P, 2], I32))
        cs = sb("cs", [P, 2])
        ew = sb("ew", [P, 2, EXPERT])
        g = sb("g", [P, 2 * FT, S])
        xb = sb("xb", [P, S])
        early = sb("early", [P, 1])
        acc = sb("acc", [P, S])
        NU = 2 * FT
        block = stack.enter_context(nc.Block(no_gpsimd_drain=True))

        @block.sync
        def _(eng):
            eng.wait_ge(s["chosen"], 1)
            chosen = [eng.value_load(numi[0:1, i:i + 1], min_val=0, max_val=E0 - 1) for i in range(2)]
            for sem, part in (("w1", slice(0, FF + FT)), ("w2", slice(FF + FT, EXPERT))):
                for i in range(2):
                    eng.dma_start(ew[:, i, part], experts[chosen[i], :, part]).then_inc(s[sem], 16)
            fetch_next(eng)

        @block.tensor
        def _(eng):
            eng.wait_ge(s["mean"], 1)
            eng.matmul(ps[:, 6, 0:E0], xm[:, 0:1].to_broadcast([P, P]), K["f0_gate"][:, :], start=True,
                       stop=True).then_inc(s["logits"], 1)
            eng.wait_ge(s["w1"], 32)

            def up(n):
                e, f = divmod(n, FT)
                if n >= 4:
                    eng.wait_ge(s["g"], n - 3)
                eng.matmul(ps[:, n % 4, :], ew[:, e, f * P:(f + 1) * P], X[:, :], start=True,
                           stop=True).then_inc(s["hid"], 1)

            def down(n):
                e, f = divmod(n, FT)
                if n == 0:
                    eng.wait_ge(s["w2"], 32)
                eng.wait_ge(s["g"], n + 1)
                at = FF + FT + f * P
                eng.matmul(ps[:, 4 + e, :], ew[:, e, at:at + P], g[:, n, :], start=(f == 0),
                           stop=(f == FT - 1)).then_inc(s["down"], 1)

            for n in range(4):
                up(n)
            for n in range(NU):
                down(n)
                if n + 4 < NU:
                    up(n + 4)
            norm_tensor(eng, ps, post)

        @block.scalar
        def _(eng):
            eng.wait_ge(s["m8"], 3)
            eng.activation(ee[:, :], lg[:, 0:E0], ACT.Exp, bias=nm[:, 0:1]).then_inc(s["ee"], 1)
            eng.activation(early[:, :], K["one"], ACT.Gelu)
            eng.wait_ge(s["w1"], 32)
            for n in range(NU):
                e, f = divmod(n, FT)
                eng.wait_ge(s["hid"], n + 1)
                eng.activation(g[:, n, :], ps[:, n % 4, :], ACT.Gelu, bias=ew[:, e, FF + f:FF + f + 1])\
                   .then_inc(s["g"], 1)
            norm_scalar(eng, ps, post)

        @block.gpsimd
        def _(eng):
            eng.memset(lg[:, E0:], FAR).then_inc(s["pad"], 1)
            eng.memset(rp[:, 2:], FAR).then_inc(s["pad"], 1)

        @block.vector
        def _(eng):
            link = chained(eng, s["chain"])
            eng.tensor_reduce(xm[:, :], X[:, :], AX, ALU.add).then_inc(s["mean"], 1)
            eng.wait_ge(s["logits"], 1)
            link(eng.tensor_scalar(lg[:, 0:E0], ps[:, 6, 0:E0], 1.0 / S, None, ALU.mult))
            eng.max(m8[:, :], lg[:, 0:E0]).then_inc(s["m8"], 1)
            eng.wait_ge(s["m8"], 1)
            eng.wait_ge(s["pad"], 2)
            eng.tensor_copy(rp[:, 0:2], m8[:, 0:2]).then_inc(s["m8"], 1)
            eng.tensor_scalar(nm[:, :], m8[:, 0:1], -1.0, None, ALU.mult).then_inc(s["m8"], 1)
            eng.wait_ge(s["m8"], 3)
            link(eng.match_replace(wk[:, :], rp[:, :], lg[:, :], TAKEN))
            numbers = K["jrow"][:, 0:E0]
            link(eng.scalar_tensor_tensor(sel[:, :], wk[:, 0:E0], TAKEN / 2, numbers, ALU.is_le, ALU.mult,
                                          accum_out=num[:, 0:1]))
            link(eng.tensor_reduce(num[:, 1:2], sel[:, :], AX, ALU.max))
            link(eng.tensor_tensor(num[:, 0:1], num[:, 0:1], num[:, 1:2], ALU.subtract))
            eng.tensor_copy(numi[:, :], num[:, :]).then_inc(s["chosen"], 1)
            eng.wait_ge(s["ee"], 1)
            link(eng.scalar_tensor_tensor(cw[:, :], wk[:, 0:E0], TAKEN / 2, ee[:, :], ALU.is_le, ALU.mult,
                                          accum_out=tot[:, :]))
            link(eng.reciprocal(tot[:, :], tot[:, :]))
            link(eng.tensor_scalar(cw[:, :], cw[:, :], tot[:, 0:1], None, ALU.mult))
            for i in range(2):
                link(eng.scalar_tensor_tensor(jk[:, :], numbers, num[:, i:i + 1], cw[:, :], ALU.is_equal, ALU.mult,
                                              accum_out=cs[:, i:i + 1]))
            link(eng.tensor_tensor_reduce(jk[:, :], K["f0_b2"], cw[:, :], 1.0, 0.0, ALU.mult, ALU.add,
                                          be[:, :]))
            link(eng.tensor_scalar(xb[:, :], X[:, :], be[:, 0:1], None, ALU.add))
            eng.wait_ge(s["down"], FT)
            link(eng.scalar_tensor_tensor(acc[:, :], ps[:, 4, :], cs[:, 0:1], xb[:, :], ALU.mult, ALU.add))
            eng.wait_ge(s["down"], NU)

            def put_y(h):
                c = slice(h * LN_HALF, (h + 1) * LN_HALF)
                return eng.scalar_tensor_tensor(L["y"][:, c], ps[:, 5, c], cs[:, 1:2], acc[:, c], ALU.mult,
                                                ALU.add)
            norm_vector(eng, ps, post, put_y)



D_SEMS = STACK_SEMS + "kept_x proj vp sc mn p tm pt pta pv rex rt rtb ot sent chain"
QL, QH = 16, 32


def attn1(nc, K, ps, X, s, b, contexts, parts_dram, middle):
    with ExitStack() as stack:
        def sb(name, shape):
            return stack.enter_context(nc.sbuf_tensor(f"a1_{name}", shape, F32))

        def half(name, shape):
            return stack.enter_context(nc.sbuf_tensor(f"a1_{name}", shape, BF16))
        scale = float(DH) ** -0.5
        qf = sb("qf", [P, S])
        kf = sb("kf", [P, S])
        parts = [half(n, [P, 3, S]) for n in ("qparts", "kparts")]
        qs = half("qs", [ROWS, NH, S])
        ks = half("ks", [ROWS, NH, S])
        vp = sb("vp", [P, T, HG, P])
        steps = [(j, t, g) for j in range(HG) for t in range(T) for g in range(4)]
        N = len(steps)
        mn = sb("mn", [P, N])
        p = sb("p", [P, 8, S])
        pt = sb("pt", [P, 2, T, HG, 2 * P])
        rs = sb("rs", [P, T, NH])
        rex = sb("rex", [P, T, P])
        rt = sb("rt", [P, S])
        ot = sb("ot", [P, QL, QH])
        by_act = [n % 2 == 1 for n in range(N)]
        acts = [sum(by_act[:n + 1]) for n in range(N)]
        vecs = [n + 1 - acts[n] for n in range(N)]

        def emptied(eng, n):
            eng.wait_ge(s["pta"] if by_act[n] else s["pt"], acts[n] if by_act[n] else vecs[n])

        def empty(eng, copy, n, sem):
            j, t, g = steps[n]
            eng.wait_ge(s["tm"], n + 1)
            if n >= 16:
                eng.wait_ge(s["pv"], n // 8 - 1)
            copy(pt[:, (n // 8) % 2, :, g, (t % 2) * P:(t % 2 + 1) * P],
                 ps[:, 4 + n % 3, :].rearrange("p (k q) -> p k q", k=T)).then_inc(sem, 1)
        block = stack.enter_context(nc.Block(no_gpsimd_drain=True))

        @block.tensor
        def _(eng):
            eng.matmul(ps[:, 0, :], K["a1_wq"][:, :], X[:, :], start=True, stop=True).then_inc(s["proj"], 1)
            eng.matmul(ps[:, 1, :], K["a1_wk"][:, :], X[:, :], start=True, stop=True).then_inc(s["proj"], 1)
            for k in range(T):
                mm = eng.matmul(ps[:, 2, k * P:(k + 1) * P], X[:, k * P:(k + 1) * P], K["a1_wv"][:, :],
                                start=True, stop=True)
            mm.then_inc(s["proj"], 1)

            def scores(n):
                j, t, g = steps[n]
                if n == 0:
                    eng.wait_ge(s["qf"], 1)
                    eng.wait_ge(s["kf"], 1)
                if t == 0 and g == 0:
                    eng.wait_ge(s[f"j{j}"], STACKED)
                if n == 2:
                    eng.wait_ge(s["vp"], T)
                if n >= 4:
                    eng.wait_ge(s["mn"], n - 3)
                eng.matmul(ps[:, g, :], qs[:, HG * j + g, t * P:(t + 1) * P], ks[:, HG * j + g, :], start=True,
                           stop=True).then_inc(s["sc"], 1)

            def turn(n):
                eng.wait_ge(s["p"], n + 1)
                if n >= 3:
                    emptied(eng, n - 3)
                for k in range(T):
                    mm = eng.transpose(ps[:, 4 + n % 3, k * P:(k + 1) * P], p[:, n % 8, k * P:(k + 1) * P],
                                       K["ident"])
                mm.then_inc(s["tm"], 1)

            def values(u):
                j, t, _ = steps[8 * u]
                emptied(eng, 8 * u + 7)
                emptied(eng, 8 * u + 6)
                for k in range(T):
                    for g in range(4):
                        mm = eng.matmul(ps[32 * g:32 * g + 32, 7, t * P:(t + 2) * P],
                                        vp[:, k, j, 32 * g:32 * g + 32], pt[:, u % 2, k, g, :],
                                        start=(u == 0 and k == 0), stop=(j == HG - 1 and k == T - 1),
                                        skip_group_check=True)
                mm.then_inc(s["pv"], 1)

            for n in range(4):
                scores(n)
            for n in range(N):
                if n + 4 < N:
                    scores(n + 4)
                turn(n)
                if n % 8 == 3 and n > 8:
                    values(n // 8 - 1)
            values(N // 8 - 1)
            eng.wait_ge(s["rex"], 1)
            for t in range(T):
                mm = eng.transpose(ps[:, 4, t * P:(t + 1) * P], rex[:, t, :], K["ident"])
            mm.then_inc(s["rtb"], 1)

        @block.scalar
        def _(eng):
            eng.wait_ge(s["proj"], 2)
            eng.activation(kf[:, :], ps[:, 1, :], ACT.Identity, bias=K["a1_bk"]).then_inc(s["kf"], 1)
            eng.wait_ge(s["kf"], 1)
            split_scalar(eng, parts[1], kf, s["ks"])
            for n, (j, t, g) in enumerate(steps):
                eng.wait_ge(s["mn"], n + 1)
                h = 4 * g + j
                eng.activation(p[:, n % 8, :], p[:, n % 8, :], ACT.Exp, bias=mn[:, n:n + 1], scale=-1.0,
                               accum_out=rs[:, t, h:h + 1]).then_inc(s["p"], 1)
                if n >= 3 and by_act[n - 3]:
                    empty(eng, lambda o, i: eng.activation(o, i, ACT.Copy), n - 3, s["pta"])
            for n in range(N - 3, N):
                if by_act[n]:
                    empty(eng, lambda o, i: eng.activation(o, i, ACT.Copy), n, s["pta"])
            eng.wait_ge(s["rtb"], 1)
            eng.activation(rt[:, :], ps[:, 4, :], ACT.Copy).then_inc(s["rt"], 1)

        @block.vector
        def _(eng):
            link = chained(eng, s["chain"])
            eng.wait_ge(s["proj"], 1)
            eng.tensor_scalar(qf[:, :], ps[:, 0, :], K["a1_bq"], -scale, ALU.add, ALU.mult).then_inc(s["qf"], 1)
            eng.wait_ge(s["qf"], 1)
            split(eng, parts[0], qf, s["qs"])
            split_vector(eng, parts[1], kf, s["ks"])
            eng.wait_ge(s["proj"], 3)
            for k in range(T):
                eng.tensor_tensor(vp[:, k, :, :], ps[:, 2, k * P:(k + 1) * P].unsqueeze(1).to_broadcast([P, HG, P]),
                                  K["colmask_dj"], ALU.mult).then_inc(s["vp"], 1)

            def biased(n):
                j, t, g = steps[n]
                at = S - P - t * P
                eng.wait_ge(s["sc"], n + 1)
                if n >= 8:
                    eng.wait_ge(s["tm"], n - 7)
                eng.tensor_tensor_reduce(p[:, n % 8, :], ps[:, g, :], K["nbias"][:, at:at + S], 1.0, 3.0e38,
                                         ALU.add, ALU.min, mn[:, n:n + 1]).then_inc(s["mn"], 1)

            for n in range(N):
                biased(n)
                if n >= 4 and not by_act[n - 4]:
                    empty(eng, eng.tensor_copy, n - 4, s["pt"])
            for n in range(N - 4, N):
                if not by_act[n]:
                    empty(eng, eng.tensor_copy, n, s["pt"])
            eng.wait_ge(s["p"], N)
            link(eng.reciprocal(rs[:, :, :], rs[:, :, :]))
            eng.tensor_copy(rex[:, :, :].rearrange("p t (g d j) -> p (t g) d j", d=DH, j=HG),
                            rs[:, :, :].rearrange("p t (g j) -> p (t g) j", j=HG).unsqueeze(2)
                            .to_broadcast([P, T * 4, DH, HG])).then_inc(s["rex"], 1)
            eng.wait_ge(s["rt"], 1)
            eng.wait_ge(s["pv"], N // 8)
            link(eng.tensor_tensor(ot[:, :, :].rearrange("p a b -> p b a"),
                                   ps[:, 7, :].rearrange("p (b a) -> p b a", a=QL),
                                   rt[:, :].rearrange("p (b a) -> p b a", a=QL), ALU.mult))
            eng.tensor_scalar(ot[:, :, :], ot[:, :, :], K["a1_bv"], None, ALU.add).then_inc(s["ot"], 1)

        @block.sync
        def _(eng):
            eng.dma_start(middle[b], X[:, :]).then_inc(s["kept_x"], 16)
            stack_parts(eng, s, parts, (qs, ks), parts_dram)
            eng.wait_ge(s["kept_x"], 16)
            eng.wait_ge(s["ot"], 1)
            for g in range(4):
                eng.dma_start(bass.AP(contexts.tensor, g * P * S + b * QH, [[B * QH, DH * HG], [DH * S, QL], [1, QH]]),
                              ot[32 * g:32 * g + 32, :, :]).then_inc(s["sent"], 16)
            eng.wait_ge(s["sent"], 16 * 4)


O_SEMS = "out " + norm_names("post")


def attn1_out(nc, K, ps, xin, X, s):
    with ExitStack() as stack:
        L = norm_tiles(nc, stack, "ao")
        post = norm_of(K, L, s, "post", (2, 3), (5, 6), X)
        block = stack.enter_context(nc.Block(no_gpsimd_drain=True))

        @block.tensor
        def _(eng):
            for h in range(2):
                eng.matmul(ps[:, h, 0:LN_HALF], K["a1_wo"][:, :], K["ot"][:, h * LN_HALF:(h + 1) * LN_HALF],
                           start=True, stop=True).then_inc(s["out"], 1)
            norm_tensor(eng, ps, post)

        @block.scalar
        def _(eng):
            norm_scalar(eng, ps, post)

        @block.vector
        def _(eng):
            def put_y(h):
                c = slice(h * LN_HALF, (h + 1) * LN_HALF)
                eng.wait_ge(s["out"], h + 1)
                return eng.scalar_tensor_tensor(L["y"][:, c], ps[:, h, 0:LN_HALF], K["a1_bo"], xin[:, c],
                                                ALU.add, ALU.add)
            norm_vector(eng, ps, post, put_y)




def kernel_spectrum(nc, stack, K, s4, ps, load_rest):
    kf = K["kf"]
    with ExitStack() as tmp:
        s = semaphores(nc, tmp, "kf", "gate chain args small pchain targs iargs trig tab prod ks ksc kf")
        def sb(name, shape):
            return tmp.enter_context(nc.sbuf_tensor(f"kf_{name}", shape, F32))
        dt = sb("dt", [P, P])
        gate = sb("gate", [P, 1])
        near = sb("near", [P, P])
        power = tmp.enter_context(nc.sbuf_tensor("kf_power", [P, P], I32))
        r = sb("r", [P, P])
        turns = sb("turns", [P, P])
        arg = sb("arg", [P, 3, P])
        whole = sb("whole", [P, HD * JL])
        trig = sb("trig", [P, 3, P])
        er = sb("er", [P, P])
        th = sb("th", [P, P])
        a = sb("a", [P, P])
        b = sb("b", [P, P])
        c = sb("c", [P, P])
        e = sb("e", [P, P])
        alpha = sb("alpha", [P, P])
        beta = sb("beta", [P, P])
        tj = sb("tj", [P, P, JL])
        ej = sb("ej", [P, P, JL])
        uv = sb("uv", [P, 2, P, IL])
        ei = sb("ei", [P, P, IL])
        ti = uv[:, 0, :, :]
        ks = whole[:, 0:T * P].rearrange("p (k d) -> p k d", k=T)

        def wide(v, n):
            return v.unsqueeze(2).to_broadcast([P, v.shape[1], n])

        def steps(name, n, width):
            return K[name].unsqueeze(1).to_broadcast([P, width, n])
        block = tmp.enter_context(nc.Block(no_gpsimd_drain=True))

        @block.sync
        def _(eng):
            load_rest(eng)

        @block.tensor
        def _(eng):
            for d in range(P):
                if d % HD == 0:
                    eng.wait_ge(s["prod"], 2 * (d // HD) + 2)
                for g in range(T):
                    mm = eng.matmul(ps[JL * g:JL * g + JL, 0, d:3 * P + d + 1:P], tj[:, d, :], ti[:, d, g::T],
                                    start=True, stop=True, skip_group_check=True)
            mm.then_inc(s["ks"], 1)
            eng.wait_ge(s["ksc"], 1)
            eng.wait_ge(*K["weights_in"])
            for f in range(NF // P):
                for k in range(T):
                    mm = eng.matmul(ps[:, 1 + f // T, (f % T) * P:(f % T + 1) * P],
                                    K["fwd"][:, k, f * P:(f + 1) * P], ks[:, k, :],
                                    start=(k == 0), stop=(k == T - 1))
            mm.then_inc(s["kf"], 1)

        @block.scalar
        def _(eng):
            eng.activation(gate[:, :], K["et_gate"], ACT.Exp, scale=-1.0).then_inc(s["gate"], 1)
            eng.wait_ge(s["args"], 1)
            eng.activation(er[:, :], r[:, :], ACT.Exp).then_inc(s["small"], 1)
            eng.activation(th[:, :], r[:, :], ACT.Tanh, scale=0.5).then_inc(s["small"], 1)
            eng.wait_ge(s["args"], 2)
            eng.activation(trig[:, :, :], arg[:, :, :], ACT.Sin, scale=TURN).then_inc(s["trig"], 1)
            eng.wait_ge(s["targs"], 2)
            eng.activation(ei[:, :, :], ei[:, :, :], ACT.Exp).then_inc(s["tab"], 1)
            eng.activation(ej[:, :, :], ej[:, :, :], ACT.Exp).then_inc(s["tab"], 1)
            for part in range(P // HD):
                h = slice(part * HD, (part + 1) * HD)
                for c in range(2):
                    eng.wait_ge(s["iargs"], 3 * part + c + 1)
                    eng.activation(uv[:, c, h, :], uv[:, c, h, :], ACT.Sin, scale=TURN).then_inc(s["tab"], 1)
                eng.wait_ge(s["iargs"], 3 * part + 3)
                eng.activation(tj[:, h, :], tj[:, h, :], ACT.Sin, scale=TURN).then_inc(s["tab"], 1)

        @block.gpsimd
        def _(eng):
            eng.wait_ge(s["args"], 1)
            eng.tensor_tensor(ei[:, :, :], wide(r[:, :], IL), steps("irow", IL, P), ALU.mult).then_inc(s["targs"], 1)
            eng.tensor_tensor(ej[:, :, :], wide(r[:, :], JL), steps("jrow", JL, P), ALU.mult).then_inc(s["targs"], 1)

        @block.vector
        def _(eng):
            link = chained(eng, s["chain"])

            def fraction(x, w):
                link(eng.tensor_scalar(w, x, MAGIC, None, ALU.add))
                link(eng.tensor_scalar(w, w, -MAGIC, None, ALU.add))
                return eng.tensor_tensor(x, x, w, ALU.subtract)

            def turned(x, w, a, b, phase):
                link(eng.tensor_tensor(x, a, b, ALU.mult))
                link(eng.tensor_scalar(w, x, phase, MAGIC, ALU.add, ALU.add))
                link(eng.tensor_scalar(w, w, -MAGIC, None, ALU.add))
                return eng.scalar_tensor_tensor(x, x, phase, w, ALU.add, ALU.subtract)
            link(eng.tensor_scalar(r[:, :], K["log_dt"], LOG_LEAST, LOG_MOST, ALU.max, ALU.min))
            link(eng.tensor_scalar(near[:, :], r[:, :], 1.0 / LN2, None, ALU.mult))
            link(eng.tensor_scalar(near[:, :], near[:, :], MAGIC, None, ALU.add))
            link(eng.tensor_scalar(near[:, :], near[:, :], -MAGIC, None, ALU.add))
            link(eng.scalar_tensor_tensor(r[:, :], near[:, :], -LN2_HIGH, r[:, :], ALU.mult, ALU.add))
            link(eng.scalar_tensor_tensor(r[:, :], near[:, :], LN2_HIGH - LN2, r[:, :], ALU.mult, ALU.add))
            link(eng.tensor_scalar(dt[:, :], r[:, :], SERIES[-1], None, ALU.mult))
            for term in SERIES[-2:0:-1]:
                link(eng.scalar_tensor_tensor(dt[:, :], dt[:, :], term, r[:, :], ALU.add, ALU.mult))
            link(eng.tensor_scalar(power[:, :], near[:, :], EXP_BIAS, EXP_UNIT, ALU.add, ALU.mult))
            link(eng.scalar_tensor_tensor(dt[:, :], dt[:, :], 1.0, power[:, :].bitcast(F32), ALU.add, ALU.mult))
            eng.tensor_tensor(r[:, :], dt[:, :], s4[:, 0, :], ALU.mult).then_inc(s["args"], 1)
            eng.wait_ge(s["args"], 1)
            link(eng.scalar_tensor_tensor(turns[:, :], s4[:, 1, :], INV2PI, dt[:, :], ALU.mult, ALU.mult))
            link(eng.tensor_copy(arg[:, 0, :], turns[:, :]))
            link(eng.tensor_scalar(arg[:, 1, :], turns[:, :], 0.25, None, ALU.add))
            link(eng.tensor_scalar(arg[:, 2, :], turns[:, :], 0.5, None, ALU.mult))
            fraction(arg[:, :, :], whole[:, 0:3 * P].rearrange("p (a b) -> p a b", a=3)).then_inc(s["args"], 1)
            eng.wait_ge(s["args"], 2)
            def tables(part):
                h = slice(part * HD, (part + 1) * HD)
                wi = whole[:, 0:HD * IL].rearrange("p (d i) -> p d i", i=IL)
                wj = whole[:, 0:HD * JL].rearrange("p (d j) -> p d j", j=JL)
                for c, phase in enumerate(("phase", "phase2")):
                    turned(uv[:, c, h, :], wi, wide(turns[:, h], IL), steps("irow", IL, HD), K[phase])\
                        .then_inc(s["iargs"], 1)
                    eng.wait_ge(s["iargs"], 3 * part + c + 1)
                turned(tj[:, h, :], wj, wide(turns[:, h], JL), steps("jrow", JL, HD), K["phase"])\
                    .then_inc(s["iargs"], 1)
                eng.wait_ge(s["iargs"], 3 * part + 3)
            tables(0)
            eng.wait_ge(s["small"], 2)
            eng.wait_ge(s["trig"], 1)
            link(eng.scalar_tensor_tensor(th[:, :], er[:, :], 1.0, th[:, :], ALU.add, ALU.mult))
            link(eng.tensor_tensor(th[:, :], th[:, :], trig[:, 1, :], ALU.mult))
            link(eng.scalar_tensor_tensor(a[:, :], trig[:, 2, :], -2.0, trig[:, 2, :], ALU.mult, ALU.mult))
            link(eng.tensor_tensor(a[:, :], a[:, :], th[:, :], ALU.add))
            link(eng.tensor_tensor(b[:, :], er[:, :], trig[:, 0, :], ALU.mult))
            link(eng.tensor_tensor(c[:, :], s4[:, 2, :], a[:, :], ALU.mult))
            link(eng.tensor_tensor(e[:, :], s4[:, 3, :], b[:, :], ALU.mult))
            link(eng.tensor_tensor(c[:, :], c[:, :], e[:, :], ALU.subtract))
            link(eng.tensor_tensor(b[:, :], s4[:, 2, :], b[:, :], ALU.mult))
            link(eng.tensor_tensor(e[:, :], s4[:, 3, :], a[:, :], ALU.mult))
            link(eng.tensor_tensor(e[:, :], e[:, :], b[:, :], ALU.add))
            link(eng.tensor_tensor(a[:, :], s4[:, 0, :], s4[:, 0, :], ALU.mult))
            link(eng.tensor_tensor(b[:, :], s4[:, 1, :], s4[:, 1, :], ALU.mult))
            link(eng.tensor_tensor(a[:, :], a[:, :], b[:, :], ALU.add))
            link(eng.reciprocal(er[:, :], a[:, :]))
            link(eng.tensor_tensor(a[:, :], c[:, :], s4[:, 0, :], ALU.mult))
            link(eng.tensor_tensor(b[:, :], e[:, :], s4[:, 1, :], ALU.mult))
            link(eng.tensor_tensor(a[:, :], a[:, :], b[:, :], ALU.add))
            link(eng.scalar_tensor_tensor(alpha[:, :], a[:, :], K["sign"], er[:, :], ALU.mult, ALU.mult))
            link(eng.tensor_tensor(a[:, :], c[:, :], s4[:, 1, :], ALU.mult))
            link(eng.tensor_tensor(b[:, :], e[:, :], s4[:, 0, :], ALU.mult))
            link(eng.tensor_tensor(a[:, :], a[:, :], b[:, :], ALU.subtract))
            link(eng.tensor_tensor(beta[:, :], a[:, :], er[:, :], ALU.mult))
            for part in range(P // HD):
                h = slice(part * HD, (part + 1) * HD)
                if part:
                    tables(part)
                eng.wait_ge(s["tab"], 2 + 3 * part + 2)
                link(eng.tensor_tensor(uv[:, 0, h, :], uv[:, 0, h, :], wide(alpha[:, h], IL), ALU.mult))
                link(eng.tensor_tensor(uv[:, 1, h, :], uv[:, 1, h, :], wide(beta[:, h], IL), ALU.mult))
                link(eng.tensor_tensor(uv[:, 0, h, :], uv[:, 0, h, :], uv[:, 1, h, :], ALU.add))
                eng.scalar_tensor_tensor(ti[:, h, :], uv[:, 0, h, :], 2.0, ei[:, h, :], ALU.mult, ALU.mult)\
                   .then_inc(s["prod"], 1)
                eng.wait_ge(s["tab"], 2 + 3 * part + 3)
                eng.tensor_tensor(tj[:, h, :], tj[:, h, :], ej[:, h, :], ALU.mult).then_inc(s["prod"], 1)
            nbias = K["nbias"]
            eng.wait_ge(*K["first_in"])
            eng.wait_ge(s["gate"], 1)
            link(eng.tensor_scalar(gate[:, :], gate[:, :], 1.0, None, ALU.add))
            link(eng.reciprocal(gate[:, :], gate[:, :]))
            link(eng.tensor_scalar(nbias[:, :], K["skew"][:, :], gate[:, 0:1], K["is_gate"], ALU.mult, ALU.add))
            link(eng.tensor_scalar(nbias[:, :], nbias[:, :], -1.0, None, ALU.mult))
            eng.wait_ge(s["ks"], 1)
            eng.tensor_copy(ks[:, :, :], ps[:, 0, :].rearrange("p (k d) -> p k d", k=T)).then_inc(s["ksc"], 1)
            eng.wait_ge(s["kf"], 1)
            eng.tensor_copy(kf[:, :, :], ps[:, 1:3, :].rearrange("p b (f d) -> p (b f) d", d=P))
    for sem in s.values():
        nc.gpsimd.sem_clear(sem)
    nc.all_engine_barrier()



E_SEMS = ("proj qk v mask sc scr mx mr neg e a rs r dg at atc ct ctc film filmc xo asum xm xi xit xitc dft y inv "
          "h1 hg h2 chain " + norm_names("nin", "nffn", "nout", "post"))
ROUNDS = TOPK // 8


def cross1(nc, K, ps, X, s, stored):
    with ExitStack() as stack:
        def sb(name, shape):
            return stack.enter_context(nc.sbuf_tensor(f"c1_{name}", shape, F32))
        L = norm_tiles(nc, stack, "c1")
        ctx = K["ctx"]
        qt = sb("qt", [P, S])
        kt = sb("kt", [P, M])
        v = sb("v", [P, P])
        vr = sb("vr", [MR, P])
        vm = sb("vm", [P, M])
        tm = sb("tm", [P, T])
        xn = sb("xn", [P, S])
        sc = sb("sc", [P, 2, XH, M])
        wk = sb("wk", [P, XH, M])
        m8 = sb("m8", [P, ROUNDS, XH, 8])
        neg = sb("neg", [P, 2, XH])
        e = sb("e", [P, 2, XH, M])
        a = sb("a", [P, 2, XH, M])
        rs = sb("rs", [P, 2, XH])
        r = sb("r", [P, 2, XH])
        dg = sb("dg", [P, 2, XH, P])
        at = sb("at", [P, S])
        atr = sb("atr", [MR, S])
        ct = sb("ct", [P, S])
        fb = sb("fb", [P, 4])
        film = sb("film", [P, 4, S])
        xi = sb("xi", [P, S])
        xo = sb("xo", [P, S])
        asum = sb("asum", [P, M])
        xit = sb("xit", [P, T, P])
        kf = K["kf"]
        y = sb("y", [P, NF // P, P])
        m = sb("m", [P, 4, T, P])
        hn = sb("hn", [P, S])
        hg = sb("hg", [P, FT, S])
        z = sb("z", [P, S])
        nin = norm_of(K, L, s, "nin", (4, 5), (6, 7), xn, scale=K["x1_gin"], shift=K["x1_bin"])
        nffn = norm_of(K, L, s, "nffn", (4, 5), (0, 1), hn, scale=K["x1_gffn"], shift=K["x1_bffn"])
        nout = norm_of(K, L, s, "nout", (4, 5), (2, 3), z, scale=K["x1_gout"], shift=K["x1_bout"])
        post = norm_of(K, L, s, "post", (4, 5), (0, 1), X)
        block = stack.enter_context(nc.Block(no_gpsimd_drain=True))

        @block.sync
        def _(eng):
            eng.wait_ge(stored, 16)

        @block.tensor
        def _(eng):
            eng.matmul(ps[:, 0, :], K["x1_wq"][:, :], X[:, :], start=True, stop=True).then_inc(s["proj"], 1)
            eng.matmul(ps[:, 1, 0:M], K["x1_wk"][:, :], ctx[:, 0:M], start=True, stop=True)\
               .then_inc(s["proj"], 1)
            eng.matmul(ps[:, 2, 0:P], ctx[:, 0:P], K["x1_wv"][:, :], start=True, stop=True)\
               .then_inc(s["proj"], 1)
            eng.matmul(ps[0:MR, 3, 0:P], ctx[:, P:M], K["x1_wv"][:, :], start=True, stop=True)\
               .then_inc(s["proj"], 1)

            def scores(t):
                if t == 0:
                    eng.wait_ge(s["qk"], 2)
                    eng.wait_ge(s["v"], 2)
                else:
                    eng.wait_ge(s["scr"], t)
                for h in range(XH):
                    mm = eng.matmul(ps[:, h, 0:M], qt[XD * h:XD * h + XD, t * P:(t + 1) * P],
                                    kt[XD * h:XD * h + XD, :], start=True, stop=True)
                mm.then_inc(s["sc"], 1)
            scores(0)
            norm_tensor(eng, ps, nin)
            scores(1)
            for t in range(T):
                q = slice(t * P, (t + 1) * P)
                if t < T - 1:
                    eng.wait_ge(s["a"], XH * (t + 1))
                    eng.wait_ge(s["dg"], XH * (t + 1))
                else:
                    eng.wait_ge(s["asum"], XH)
                if t == 0:
                    eng.wait_ge(nin["out"], 2)
                else:
                    eng.wait_ge(s["xitc"], t)
                for at_, cols, rows in ((0, slice(0, P), P), (P, slice(P, M), MR)):
                    if t == T - 1:
                        mm = eng.transpose(ps[0:rows, 4, at_:at_ + P], asum[:, cols], K["ident"])
                        continue
                    for h in range(XH):
                        mm = eng.matmul(ps[0:rows, 4, at_:at_ + P], a[:, t % 2, h, cols],
                                        dg[:, t % 2, h, :], start=(h == 0), stop=(h == XH - 1))
                mm.then_inc(s["at"], 1)
                if t + 2 < T:
                    scores(t + 2)
                eng.wait_ge(s["atc"], 2 * (t + 1))
                eng.matmul(ps[:, 4, 2 * P:3 * P], v[:, :], at[:, q], start=True, stop=False)
                eng.matmul(ps[:, 4, 2 * P:3 * P], vr[:, :], atr[:, q], start=False, stop=True)\
                   .then_inc(s["ct"], 1)
                eng.wait_ge(s["ctc"], t + 1)
                if t:
                    eng.wait_ge(s["filmc"], 4 * t)
                for n, w in enumerate(("x1_win", "x1_win", "x1_wout", "x1_wout")):
                    mm = eng.matmul(ps[:, 5, n * P:(n + 1) * P], K[w][:, (n % 2) * P:(n % 2 + 1) * P], ct[:, q],
                                    start=True, stop=True)
                mm.then_inc(s["film"], 1)
                eng.wait_ge(s["xi"], t + 1)
                eng.transpose(ps[:, 4, 3 * P:4 * P], xi[:, q], K["ident"]).then_inc(s["xit"], 1)
                eng.wait_ge(s["xitc"], t + 1)
                for f in range(NF // P):
                    mm = eng.matmul(ps[:, 6 + f // T, (f % T) * P:(f % T + 1) * P],
                                    K["fwd"][:, t, f * P:(f + 1) * P], xit[:, t, :],
                                    start=(t == 0 and f % T == 0), stop=(t == T - 1), skip_group_check=True)
                    if t == T - 1 and f % T == T - 1:
                        mm.then_inc(s["dft"], 1)
            eng.wait_ge(s["y"], 1)
            for f in range(NF // P):
                if f == T:
                    eng.wait_ge(s["y"], 2)
                mm = eng.matmul(ps[:, 3, :], y[:, f, :], K["inv"][:, f, :], start=(f == 0),
                                stop=(f == NF // P - 1))
            mm.then_inc(s["inv"], 1)
            norm_tensor(eng, ps, nffn)
            eng.wait_ge(nffn["out"], 2)
            for f in range(FT):
                eng.matmul(ps[:, f, :], K["x1_w1"][:, f * P:(f + 1) * P], hn[:, :], start=True, stop=True)\
                   .then_inc(s["h1"], 1)
            for f in range(FT):
                eng.wait_ge(s["hg"], f + 1)
                mm = eng.matmul(ps[:, 6, :], K["x1_w2"][:, f, :], hg[:, f, :], start=(f == 0), stop=(f == FT - 1))
            mm.then_inc(s["h2"], 1)
            norm_tensor(eng, ps, nout)
            norm_tensor(eng, ps, post)

        @block.scalar
        def _(eng):
            norm_scalar(eng, ps, nin)

            def exponentials(t):
                eng.wait_ge(s["neg"], t + 1)
                if t >= 2:
                    eng.wait_ge(s["a"], XH * (t - 1))
                for h in range(XH):
                    eng.activation(e[:, t % 2, h, :], sc[:, t % 2, h, :], ACT.Exp, bias=neg[:, t % 2, h:h + 1])\
                       .then_inc(s["e"], 1)
            exponentials(0)
            for t in range(T):
                if t + 1 < T:
                    exponentials(t + 1)
                q = slice(t * P, (t + 1) * P)
                eng.wait_ge(s["at"], t + 1)
                eng.activation(at[:, q], ps[:, 4, 0:P], ACT.Copy).then_inc(s["atc"], 1)
                eng.activation(atr[:, q], ps[0:MR, 4, P:2 * P], ACT.Copy).then_inc(s["atc"], 1)
                eng.wait_ge(s["ct"], t + 1)
                eng.activation(ct[:, q], ps[:, 4, 2 * P:3 * P], ACT.Copy).then_inc(s["ctc"], 1)
                eng.wait_ge(s["mask"], 1)
                eng.wait_ge(s["film"], t + 1)
                for n in range(4):
                    eng.activation(film[:, n, q], ps[:, 5, n * P:(n + 1) * P], ACT.Identity, bias=fb[:, n:n + 1],
                                   scale=K["mod_gate"]).then_inc(s["filmc"], 1)
                eng.wait_ge(s["xit"], t + 1)
                eng.activation(xit[:, t, :], ps[:, 4, 3 * P:4 * P], ACT.Copy).then_inc(s["xitc"], 1)
            norm_scalar(eng, ps, nffn)
            for f in range(FT):
                eng.wait_ge(s["h1"], f + 1)
                eng.activation(hg[:, f, :], ps[:, f, :], ACT.Gelu, bias=K["x1_b1"][:, f:f + 1])\
                   .then_inc(s["hg"], 1)
            norm_scalar(eng, ps, nout)
            norm_scalar(eng, ps, post)

        @block.gpsimd
        def _(eng):
            for t in range(T):
                q = slice(t * P, (t + 1) * P)
                if t < T - 1:
                    eng.wait_ge(s["r"], t + 1)
                    if t >= 2:
                        eng.wait_ge(s["at"], t - 1)
                    for h in range(XH):
                        eng.tensor_scalar(dg[:, t % 2, h, :], K["ident"], r[:, t % 2, h:h + 1], None, ALU.mult)\
                           .then_inc(s["dg"], 1)
                eng.wait_ge(nin["out"], 2)
                eng.wait_ge(s["filmc"], 4 * t + 2)
                eng.tensor_tensor(xi[:, q], xn[:, q], film[:, 0, q], ALU.mult).then_inc(s["xm"], 1)
                eng.wait_ge(s["xm"], t + 1)
                eng.tensor_tensor(xi[:, q], xi[:, q], film[:, 1, q], ALU.add).then_inc(s["xi"], 1)
            eng.wait_ge(s["filmc"], 4 * T)
            eng.tensor_tensor(xo[:, :], film[:, 3, :], X[:, :], ALU.add).then_inc(s["xo"], 1)

        @block.vector
        def _(eng):
            link = chained(eng, s["chain"])
            eng.wait_ge(s["proj"], 1)
            eng.tensor_scalar(qt[:, :], ps[:, 0, :], float(XD) ** -0.5, None, ALU.mult).then_inc(s["qk"], 1)
            eng.wait_ge(s["proj"], 2)
            eng.tensor_copy(kt[:, :], ps[:, 1, 0:M]).then_inc(s["qk"], 1)
            eng.wait_ge(s["proj"], 3)
            eng.tensor_copy(v[:, :], ps[:, 2, 0:P]).then_inc(s["v"], 1)
            eng.wait_ge(s["proj"], 4)
            eng.tensor_copy(vr[:, :], ps[0:MR, 3, 0:P]).then_inc(s["v"], 1)
            link(eng.tensor_scalar(vm[:, :], K["vmask"][:, :], -FAR, FAR, ALU.mult, ALU.add))
            link(eng.tensor_scalar(tm[:, :], K["tmask"][:, :], 1.0 / XH, None, ALU.mult))
            for n, name in enumerate(("x1_fin", "x1_fout")):
                link(eng.tensor_scalar(fb[:, 2 * n:2 * n + 2], K[name], K["mod_gate"], None, ALU.mult))
            for n in (0, 2):
                i = eng.tensor_scalar(fb[:, n:n + 1], fb[:, n:n + 1], 1.0, None, ALU.add)
                if n == 0:
                    link(i)
            i.then_inc(s["mask"], 1)

            def put_x(h):
                c = slice(h * LN_HALF, (h + 1) * LN_HALF)
                return eng.tensor_copy(L["y"][:, c], X[:, c])
            norm_input(eng, nin, put_x)

            n_mr = 0
            for t in range(T):
                eng.wait_ge(s["sc"], t + 1)
                if t >= 2:
                    eng.wait_ge(s["e"], XH * (t - 1))
                eng.tensor_tensor(sc[:, t % 2, :, :], ps[:, 0:XH, 0:M],
                                  vm[:, :].unsqueeze(1).to_broadcast([P, XH, M]), ALU.add).then_inc(s["scr"], 1)
                eng.wait_ge(s["scr"], t + 1)
                if t == 0:
                    norm_statistics(eng, ps, nin)
                for k in range(ROUNDS):
                    for h in range(XH):
                        src = sc[:, t % 2, h, :] if k == 0 else wk[:, h, :]
                        if k:
                            eng.wait_ge(s["mr"], n_mr + h + 1 - XH)
                        eng.max(m8[:, k, h, :], src).then_inc(s["mx"], 1)
                    if k == 0:
                        eng.wait_ge(s["mx"], t * ROUNDS * XH + XH)
                        eng.tensor_scalar(neg[:, t % 2, :], m8[:, 0, :, 0], -1.0, None, ALU.mult)\
                           .then_inc(s["neg"], 1)
                    for h in range(XH):
                        src = sc[:, t % 2, h, :] if k == 0 else wk[:, h, :]
                        eng.wait_ge(s["mx"], n_mr + h + 1)
                        eng.match_replace(wk[:, h, :], m8[:, k, h, :], src, TAKEN).then_inc(s["mr"], 1)
                    n_mr += XH
                    if t == 0 and k == 1:
                        norm_factors(eng, ps, nin)
                    if t == 0 and k == 3:
                        norm_output(eng, ps, nin)
                for h in range(XH):
                    eng.wait_ge(s["mr"], n_mr - XH + h + 1)
                    eng.wait_ge(s["e"], XH * t + h + 1)
                    if t >= 2 and h == 0:
                        eng.wait_ge(s["at"], t - 1)
                    eng.scalar_tensor_tensor(a[:, t % 2, h, :], wk[:, h, :], TAKEN / 2, e[:, t % 2, h, :],
                                             ALU.is_le, ALU.mult, accum_out=rs[:, t % 2, h:h + 1])\
                       .then_inc(s["a"], 1)
                eng.wait_ge(s["a"], XH * (t + 1))
                link(eng.reciprocal(rs[:, t % 2, :], rs[:, t % 2, :]))
                eng.tensor_scalar(r[:, t % 2, :], rs[:, t % 2, :], tm[:, t:t + 1], None, ALU.mult)\
                   .then_inc(s["r"], 1)
            eng.wait_ge(s["r"], T)
            for h in range(XH):
                src, f = a[:, (T - 1) % 2, h, :], r[:, (T - 1) % 2, h:h + 1]
                if h == 0:
                    eng.tensor_scalar(asum[:, :], src, f, None, ALU.mult).then_inc(s["asum"], 1)
                else:
                    eng.wait_ge(s["asum"], h)
                    eng.scalar_tensor_tensor(asum[:, :], src, f, asum[:, :], ALU.mult, ALU.add)\
                       .then_inc(s["asum"], 1)
            re, im = ps[:, 6, :].rearrange("p (f d) -> p f d", f=T), ps[:, 7, :].rearrange("p (f d) -> p f d", f=T)
            eng.wait_ge(s["dft"], 1)
            link(eng.tensor_tensor(m[:, 0, :, :], re, kf[:, 0:T, :], ALU.mult))
            link(eng.tensor_tensor(m[:, 2, :, :], re, kf[:, T:, :], ALU.mult))
            eng.wait_ge(s["dft"], 2)
            link(eng.tensor_tensor(m[:, 1, :, :], im, kf[:, T:, :], ALU.mult))
            link(eng.tensor_tensor(m[:, 3, :, :], im, kf[:, 0:T, :], ALU.mult))
            eng.tensor_tensor(y[:, 0:T, :], m[:, 0, :, :], m[:, 1, :, :], ALU.subtract).then_inc(s["y"], 1)
            eng.tensor_tensor(y[:, T:, :], m[:, 2, :, :], m[:, 3, :, :], ALU.add).then_inc(s["y"], 1)

            eng.wait_ge(s["filmc"], 4 * T)
            eng.wait_ge(s["xo"], 1)
            eng.wait_ge(s["inv"], 1)

            def put_text(h):
                c = slice(h * LN_HALF, (h + 1) * LN_HALF)
                link(eng.scalar_tensor_tensor(z[:, c], xi[:, c], K["x1_dskip"], ps[:, 3, c], ALU.mult, ALU.add))
                link(eng.tensor_tensor(z[:, c], z[:, c], film[:, 2, c], ALU.mult))
                return eng.tensor_tensor(L["y"][:, c], z[:, c], xo[:, c], ALU.add)
            norm_vector(eng, ps, nffn, put_text)
            eng.wait_ge(s["h2"], 1)

            def put_fed(h):
                c = slice(h * LN_HALF, (h + 1) * LN_HALF)
                return eng.scalar_tensor_tensor(L["y"][:, c], ps[:, 6, c], K["x1_b2"], L["y"][:, c],
                                                ALU.add, ALU.add)
            norm_vector(eng, ps, nout, put_fed)

            def put_sum(h):
                c = slice(h * LN_HALF, (h + 1) * LN_HALF)
                return eng.tensor_tensor(L["y"][:, c], X[:, c], z[:, c], ALU.add)
            norm_vector(eng, ps, post, put_sum)



F_SEMS = ("pad gates bg m8 rp wk sel gs ee wt wtt wts wtf esel hid h gate sg h2 wx h3 down busy fb chain achain "
          + norm_names("r0", "r1", "post"))


def experts1(nc, K, ps, X, s, result, fetch_next, store):
    with ExitStack() as stack:
        def sb(name, shape):
            return stack.enter_context(nc.sbuf_tensor(f"e1_{name}", shape, F32))
        L = norm_tiles(nc, stack, "e1")
        gt = sb("gt", [P, HOPS, T, E1])
        bg = sb("bg", [P, HOPS, T, 16])
        m8 = sb("m8", [P, HOPS, T, 8])
        rp = sb("rp", [P, HOPS, T, 8])
        wk = sb("wk", [P, HOPS, T, 16])
        sel = sb("sel", [P, HOPS, T, E1])
        gs = sb("gs", [P, HOPS, T, E1])
        ee = sb("ee", [P, HOPS, T, E1])
        tot = sb("tot", [P, HOPS, T])
        wt = sb("wt", [P, HOPS, T, E1])
        wb = stack.enter_context(nc.sbuf_tensor("e1_wb", [P, HOPS, T, 2, E1], BF16))
        w3 = sb("w3", [P, HOPS, T, 3, E1])
        wtt = sb("wtt", [3 * E1, HOPS, S])
        wtb = stack.enter_context(nc.sbuf_tensor("e1_wtb", [3 * E1, HOPS, S], BF16))
        esel = stack.enter_context(nc.sbuf_tensor("e1_esel", [3 * E1, E1, P], BF16))
        xf = [X, sb("xf0", [P, S]), sb("xf1", [P, S])]
        h = sb("h", [P, 2, S])
        g = sb("g", [P, 2, S])
        h2 = sb("h2", [P, 2, S])
        h3 = sb("h3", [P, 2, S])
        sdown2 = sb("sdown2", [P, 1])
        hop = [norm_of(K, L, s, f"r{j}", (0, 1), (2, 3), xf[j + 1], centred=False,
                       scale=K["f1_norm"][:, j:j + 1], eps="eps6") for j in range(HOPS)]
        post = norm_of(K, L, s, "post", (4, 5), (0, 1), result)
        NU = E1 + NSH
        block = stack.enter_context(nc.Block(no_gpsimd_drain=True))

        def weights(u):
            if u < E1:
                return (K["f1_up"][:, u, :], K["f1_g"][:, u, :], K["f1_down"][:, u, :],
                        K["f1_bup"][:, u:u + 1], K["f1_bg"][:, u:u + 1])
            n = u - E1
            return (K["f1_sup"][:, n * P:(n + 1) * P], K["f1_swg"][:, :], K["f1_swdown"][:, :],
                    K["f1_sup_b"][:, n:n + 1], K["f1_sg"])
        ORDER = list(range(E1, NU)) + list(range(E1))

        @block.sync
        def _(eng):
            fetch_next(eng)
            eng.wait_ge(post["out"], 2)
            store(eng)

        @block.tensor
        def _(eng):
            for j in range(HOPS):
                base = j * NU
                if j:
                    eng.wait_ge(s[f"r{j - 1}_out"], 2)
                for t in range(T):
                    mm = eng.matmul(ps[:, 7, t * E1:(t + 1) * E1], xf[j][:, t * P:(t + 1) * P],
                                    K["f1_router"][:, j, :], start=True, stop=True)
                mm.then_inc(s["gates"], 1)

                def up(i):
                    n = base + i
                    if n >= 2:
                        eng.wait_ge(s["h"], n - 1)
                    eng.matmul(ps[:, n % 2, :], weights(ORDER[i])[0], xf[j][:, :], start=True, stop=True)\
                       .then_inc(s["hid"], 1)

                def gate(i):
                    n = base + i
                    eng.wait_ge(s["h"], n + 1)
                    if n >= 2:
                        eng.wait_ge(s["sg"], n - 1)
                    eng.matmul(ps[:, 2 + n % 2, :], weights(ORDER[i])[1], h[:, n % 2, :], start=True,
                               stop=True).then_inc(s["gate"], 1)

                def spread(i):
                    e = ORDER[i]
                    if e >= E1:
                        return
                    n = j * E1 + e
                    if e == 0:
                        eng.wait_ge(s["wts"], j + 1)
                        eng.wait_ge(s["esel"], 1)
                    if n >= 2:
                        eng.wait_ge(s["h3"], n - 1)
                    eng.matmul(ps[:, 4 + n % 2, :], esel[:, e, :], wtb[:, j, :], start=True, stop=True)\
                       .then_inc(s["wx"], 1)

                def down(i):
                    n, e = base + i, ORDER[i]
                    if e < E1:
                        eng.wait_ge(s["h3"], j * E1 + e + 1)
                        src = h3[:, (j * E1 + e) % 2, :]
                    else:
                        eng.wait_ge(s["h2"], n + 1)
                        src = h2[:, n % 2, :]
                    if n % NU == 0 and j:
                        eng.wait_ge(s["r0_y"], 2)
                    eng.matmul(ps[:, 6, :], weights(e)[2], src, start=(i == 0), stop=False,
                               skip_group_check=True).then_inc(s["down"], 1)

                def routing():
                    eng.wait_ge(s["wt"], j + 1)
                    eng.wait_ge(s["bg"], j + 1)
                    for t in range(T):
                        mm = eng.transpose(ps[0:3 * E1, 7, t * P:(t + 1) * P],
                                           w3[:, j, t, :, :].rearrange("p a e -> p (a e)"), K["ident"])
                    mm.then_inc(s["wtt"], 1)

                up(0)
                up(1)
                gate(0)
                for i in range(NU):
                    if i + 2 < NU:
                        up(i + 2)
                    if i + 1 < NU:
                        gate(i + 1)
                    if i == NSH - 1:
                        routing()
                        spread(NSH)
                    if i >= NSH and i + 1 < NU:
                        spread(i + 1)
                    down(i)
                eng.wait_ge(s["wtf"], j + 1)
                eng.matmul(ps[:, 6, :], K["f1_bdown"][:, :], wtt[:, j, :], start=False, stop=True,
                           skip_group_check=True).then_inc(s["fb"], 1)
                norm_tensor(eng, ps, hop[j])
            norm_tensor(eng, ps, post)

        @block.scalar
        def _(eng):
            for j in range(HOPS):
                def hidden(i):
                    n = j * NU + i
                    eng.wait_ge(s["hid"], n + 1)
                    if n >= 2:
                        eng.wait_ge(s["h2"], n - 1)
                    eng.activation(h[:, n % 2, :], ps[:, n % 2, :], ACT.Identity, bias=weights(ORDER[i])[3])\
                       .then_inc(s["h"], 1)

                def silu(i):
                    n = j * NU + i
                    eng.wait_ge(s["gate"], n + 1)
                    eng.activation(g[:, n % 2, :], ps[:, 2 + n % 2, :], ACT.Silu, bias=weights(ORDER[i])[4])\
                       .then_inc(s["sg"], 1)
                hidden(0)
                hidden(1)
                eng.wait_ge(s["gs"], j + 1)
                eng.activation(ee[:, j, :, :], gs[:, j, :, :], ACT.Tanh, scale=0.5).then_inc(s["ee"], 1)
                for i in range(NU):
                    silu(i)
                    if i == 1:
                        eng.wait_ge(s["wtt"], j + 1)
                        eng.activation(wtb[:, j, :], ps[0:3 * E1, 7, :], ACT.Copy).then_inc(s["wts"], 1)
                        eng.activation(wtt[:, j, :], ps[0:3 * E1, 7, :], ACT.Copy).then_inc(s["wtf"], 1)
                    if i + 2 < NU:
                        hidden(i + 2)
                norm_scalar(eng, ps, hop[j])
            norm_scalar(eng, ps, post)

        @block.gpsimd
        def _(eng):
            eng.memset(bg[:, :, :, E1:], FAR).then_inc(s["pad"], 1)
            eng.memset(rp[:, :, :, 2:], FAR).then_inc(s["pad"], 1)
            eng.tensor_copy(esel[:, :, :], K["esel"][:, :, :]).then_inc(s["esel"], 1)

        @block.vector
        def _(eng):
            link = chained(eng, s["chain"])
            link(eng.tensor_scalar(sdown2[:, :], K["f1_sdown"], float(NSH), None, ALU.mult))
            for j in range(HOPS):
                def route():
                    eng.wait_ge(s["gates"], j + 1)
                    link(eng.tensor_tensor(gt[:, j, :, :], ps[:, 7, 0:T * E1].rearrange("p (t e) -> p t e", t=T),
                                           K["f1_rb"][:, j * E1:(j + 1) * E1].unsqueeze(1).to_broadcast([P, T, E1]),
                                           ALU.add))
                    eng.wait_ge(s["pad"], 2)
                    eng.tensor_tensor(bg[:, j, :, 0:E1], gt[:, j, :, :],
                                      K["f1_gb"][:, j * E1:(j + 1) * E1].unsqueeze(1).to_broadcast([P, T, E1]),
                                      ALU.add).then_inc(s["bg"], 1)
                    eng.wait_ge(s["bg"], j + 1)
                    for t in range(T):
                        i = eng.max(m8[:, j, t, :], bg[:, j, t, :])
                        i.then_inc(s["m8"], 1)
                    eng.wait_ge(s["m8"], T * (j + 1))
                    link(eng.tensor_copy(rp[:, j, :, 0:2], m8[:, j, :, 0:2]))
                    for t in range(T):
                        eng.match_replace(wk[:, j, t, :], rp[:, j, t, :], bg[:, j, t, :], TAKEN)\
                           .then_inc(s["wk"], 1)
                    eng.wait_ge(s["wk"], T * (j + 1))
                    link(eng.tensor_scalar(sel[:, j, :, :], wk[:, j, :, 0:E1], TAKEN / 2, None, ALU.is_le))
                    link(eng.tensor_tensor(gs[:, j, :, :], sel[:, j, :, :], gt[:, j, :, :], ALU.mult))
                    link(eng.tensor_reduce(tot[:, j, :], gs[:, j, :, :], AX, ALU.add))
                    eng.scalar_tensor_tensor(gs[:, j, :, :], gt[:, j, :, :], 2.0,
                                             tot[:, j, :].unsqueeze(2).to_broadcast([P, T, E1]), ALU.mult,
                                             ALU.subtract).then_inc(s["gs"], 1)
                    eng.wait_ge(s["ee"], j + 1)
                    link(eng.scalar_tensor_tensor(wt[:, j, :, :], ee[:, j, :, :], 1.0, sel[:, j, :, :], ALU.add,
                                                  ALU.mult))
                    link(eng.tensor_scalar(wt[:, j, :, :], wt[:, j, :, :], 0.5, None, ALU.mult))
                    for i in range(2):
                        link(eng.tensor_copy(wb[:, j, :, i, :], wt[:, j, :, :]))
                        link(eng.tensor_copy(w3[:, j, :, i, :], wb[:, j, :, i, :]))
                        r = eng.tensor_tensor((wt[:, j, :, :], w3[:, j, :, 2, :])[i], wt[:, j, :, :],
                                              wb[:, j, :, i, :], ALU.subtract)
                        if i == 0:
                            link(r)
                    r.then_inc(s["wt"], 1)
                route()
                for i in range(NU):
                    n, e = j * NU + i, ORDER[i]
                    eng.wait_ge(s["sg"], n + 1)
                    if n >= 2:
                        eng.wait_ge(s["down"], n - 1)
                    eng.tensor_tensor(h2[:, n % 2, :], h[:, n % 2, :], g[:, n % 2, :], ALU.mult)\
                       .then_inc(s["h2"], 1)
                    if e < E1:
                        m = j * E1 + e
                        eng.wait_ge(s["h2"], n + 1)
                        eng.wait_ge(s["wx"], m + 1)
                        eng.tensor_tensor(h3[:, m % 2, :], h2[:, n % 2, :], ps[:, 4 + m % 2, :], ALU.mult)\
                           .then_inc(s["h3"], 1)

                def put_y(hf, j=j):
                    c = slice(hf * LN_HALF, (hf + 1) * LN_HALF)
                    eng.wait_ge(s["fb"], j + 1)
                    return eng.scalar_tensor_tensor(L["y"][:, c], ps[:, 6, c], sdown2[:, 0:1], xf[j][:, c],
                                                    ALU.add, ALU.add)
                norm_vector(eng, ps, hop[j], put_y)

            def put_y(hf):
                c = slice(hf * LN_HALF, (hf + 1) * LN_HALF)
                return eng.tensor_tensor(L["y"][:, c], xf[2][:, c], X[:, c], ALU.add)
            norm_vector(eng, ps, post, put_y)



WEIGHTS = {
    "m_win": [P, WIN], "m_wout": [P, 2, P],
    "x0_wq": [P, P], "x0_wk": [DC, P], "x0_wv": [DC, P], "x0_wo": [P, P],
    "f0_gate": [P, E0],
    "a1_wq": [P, P], "a1_wk": [P, P], "a1_wv": [P, P], "a1_wo": [P, P],
    "x1_wq": [P, P], "x1_wk": [DC, P], "x1_wv": [DC, P], "x1_win": [P, 2 * P], "x1_wout": [P, 2 * P],
    "x1_w1": [P, FF], "x1_w2": [P, FT, P],
    "f1_router": [P, HOPS, E1], "f1_up": [P, E1, P], "f1_g": [P, E1, P], "f1_down": [P, E1, P],
    "f1_bdown": [3 * E1, P], "f1_sup": [P, NSH * P], "f1_swg": [P, P], "f1_swdown": [P, P],
    "esel": [3 * E1, E1, P], "fwd": [P, T, NF], "inv": [P, NF // P, S],
}
WEIGHT_SOURCE = {
    "m_wout": "(k p) n -> p k n", 
    "x1_w2": "(k p) n -> p k n", "f1_router": "c p e -> p c e", "f1_up": "e p n -> p e n",
    "f1_g": "e p n -> p e n", "f1_down": "e p n -> p e n",
}
NEEDED_FIRST = ("m_win", "m_wout")
SETUP_SEMS = "tables first weights"


def setup(nc, stack, I, K, s, s4):
    def keep(name, shape, dt=F32):
        return stack.enter_context(nc.sbuf_tensor(f"k_{name}", shape, dt))
    cols = keep("cols", [P, NCOL])
    rows_ = keep("rows", [P, NROW])
    small = keep("small", [P, NSMALL])
    skew = keep("skew", [P, RW])
    tiles = {n: keep(n, shape) for n, shape in WEIGHTS.items()}
    for n, (a, w) in COL.items():
        K[n] = cols[:, a:a + w]
    for n, (a, w) in ROW.items():
        K[n] = rows_[:, a:a + w]
    for i, n in enumerate(("ident", "centre", "upper", "ones", "shift", "shift_last", "masked")):
        K[n] = small[:, i * P:(i + 1) * P]
    at = 7 * P
    K["headmask"] = small[:, at:at + HG]
    at += HG
    K["colmask"] = small[:, at:at + HG * P].rearrange("p (j n) -> p j n", j=HG)
    at += HG * P
    K["restmask"] = small[:, at:at + HG * P].rearrange("p (j n) -> p j n", j=HG)
    at += HG * P
    K["colmask_dj"] = small[:, at:at + HG * P].rearrange("p (j n) -> p j n", j=HG)
    K.update(tiles)
    K["skew"] = skew
    loads = {"tables": [(s4[:, :, :], I["s4"]), (cols[:, :], I["cols"]),
                        (rows_[:, :], bass.AP(I["rows"].tensor, 0, [[0, P], [1, NROW]]))],
             "first": [(small[:, :], I["small"]), (skew[:, :], I["skew"])], "weights": []}
    for n, tile in tiles.items():
        src = I[n].rearrange(WEIGHT_SOURCE[n], p=P) if n in WEIGHT_SOURCE else I[n]
        loads["first" if n in NEEDED_FIRST else "weights"].append((tile[tuple(slice(None) for _ in tile.shape)], src))
    for sem, group in loads.items():
        K[f"{sem}_in"] = (s[sem], 16 * len(group))

    def load(eng, sem):
        for dst, src in loads[sem]:
            eng.dma_start(dst, src).then_inc(s[sem], 16)
    return load


def decoder(nc, I, out):
    with ExitStack() as stack:
        K = {}
        ps = stack.enter_context(nc.psum_tensor("ps", [P, 8, S], F32))
        xin = stack.enter_context(nc.sbuf_tensor("xin", [P, S], F32))
        X = stack.enter_context(nc.sbuf_tensor("x", [P, S], F32))
        result = stack.enter_context(nc.sbuf_tensor("result", [P, S], F32))
        K["ot"] = stack.enter_context(nc.sbuf_tensor("ot", [P, S], F32))
        K["ctx"] = stack.enter_context(nc.sbuf_tensor("ctx", [DC, MP], F32))
        K["vmask"] = stack.enter_context(nc.sbuf_tensor("vmask", [P, M], U8))
        K["tmask"] = stack.enter_context(nc.sbuf_tensor("tmask", [P, T], U8))
        middle = nc.dram_tensor("middle", (B, P, S), F32, kind="Internal").ap()
        contexts = nc.dram_tensor("contexts", (B, P, S), F32, kind="Internal").ap()
        parts_dram = [nc.dram_tensor(n, (3, P, S), BF16, kind="Internal").ap() for n in ("q_parts", "k_parts")]
        cross_dram = [parts_dram[0], nc.dram_tensor("cross_k_parts", (3, P, M), BF16, kind="Internal").ap()]
        s_set = semaphores(nc, stack, "set", SETUP_SEMS)
        s_io = semaphores(nc, stack, "io", "first second stored")
        K["nbias"] = stack.enter_context(nc.sbuf_tensor("nbias", [P, RW], F32))
        K["kf"] = stack.enter_context(nc.sbuf_tensor("kf", [P, NF // P, P], F32))

        def fetch_first(eng, b):
            eng.dma_start(xin[:, :], I["x"][b]).then_inc(s_io["first"], 16)
            eng.dma_start(K["ctx"][:, :], I["ctx"][b]).then_inc(s_io["first"], 16)
            eng.wait_ge(s_io["first"], 32)

        def fetch_second(eng, b):
            eng.dma_start(xin[:, :], middle[b]).then_inc(s_io["second"], 16)
            eng.dma_start(K["ot"][:, :], contexts[b]).then_inc(s_io["second"], 16)
            eng.dma_start(K["ctx"][:, :], I["ctx"][b]).then_inc(s_io["second"], 16)
            eng.dma_start(K["vmask"][:, :], bass.AP(I["vmask"].tensor, b * M, [[0, P], [1, M]]))\
               .then_inc(s_io["second"], 16)
            eng.dma_start(K["tmask"][:, :], I["tmask"][b]).then_inc(s_io["second"], 16)
            eng.wait_ge(s_io["second"], 80)

        held = [stack.enter_context(ExitStack())]

        def layer(code, names, *args):
            own = stack.enter_context(ExitStack())
            s = semaphores(nc, own, code.__name__, names)
            code(nc, K, ps, *args[:args.index(None)], s, *args[args.index(None) + 1:])
            for sem in s.values():
                nc.gpsimd.sem_clear(sem)
            held[0].close()
            held[0] = own

        s4 = stack.enter_context(nc.sbuf_tensor("s4", [P, 4, P], F32))
        load = setup(nc, stack, I, K, s_set, s4)
        with nc.Block(no_gpsimd_drain=True) as block:
            @block.sync
            def _(eng):
                load(eng, "tables")
                eng.wait_ge(*K["tables_in"])

        def load_rest(eng):
            load(eng, "first")
            load(eng, "weights")
            fetch_first(eng, 0)
            eng.wait_ge(*K["first_in"])
        kernel_spectrum(nc, stack, K, s4, ps, load_rest)
        nc.gpsimd.sem_clear(s_io["first"])
        with nc.Fori(0, B) as b:
            layer(mixer, A_SEMS, xin, X, None)
            layer(cross0, B_SEMS, X, None, cross_dram)
            layer(experts0, C_SEMS, X, None, I["experts"], lambda eng: fetch_first(eng, (b + 1) % B))
            nc.gpsimd.sem_clear(s_io["first"])
            layer(attn1, D_SEMS, X, None, b, contexts, parts_dram, middle)
        with nc.Block(no_gpsimd_drain=True) as block:
            @block.sync
            def _(eng):
                fetch_second(eng, 0)
        nc.gpsimd.sem_clear(s_io["second"])
        nc.sync.dma_start(result[:, :], middle[0]).then_inc(s_io["stored"], 16)
        with nc.Fori(0, B) as b:
            layer(attn1_out, O_SEMS, xin, X, None)
            layer(cross1, E_SEMS, X, None, s_io["stored"])
            nc.gpsimd.sem_clear(s_io["stored"])
            layer(experts1, F_SEMS, X, None, result, lambda eng: fetch_second(eng, (b + 1) % B),
                  lambda eng: eng.dma_start(out[b], result[:, :]).then_inc(s_io["stored"], 16))
            nc.gpsimd.sem_clear(s_io["second"])
        nc.sync.wait_ge(s_io["stored"], 16)
        held[0].close()


def laid_out(inputs):
    a = {k: np.asarray(v) for k, v in inputs.items()}
    f = np.float32
    by_width = np.arange(P).reshape(4, HG, DH).transpose(2, 1, 0).reshape(-1)
    by_group = np.arange(P).reshape(4, HG, DH).transpose(0, 2, 1).reshape(-1)
    cols = {
        "x0_bq": a["L0_xattn_bq"][by_width],
        "x0_bk": a["L0_xattn_bkv"].reshape(NH, 2, DH)[:, 0].reshape(-1)[by_width],
        "x0_bv": a["L0_xattn_bkv"].reshape(NH, 2, DH)[:, 1].reshape(-1), "x0_bo": a["L0_xattn_bo"],
        "f0_b2": a["L0_ffn_b2"].T,
        "a1_bq": a["L1_attn_bq"][by_width], "a1_bk": a["L1_attn_bk"][by_width], "a1_bv": a["L1_attn_bv"][by_group], "a1_bo": a["L1_attn_bo"],
        "x1_fin": a["L1_xattn_b_film_in"].reshape(2, P).T, "x1_fout": a["L1_xattn_b_film_out"].reshape(2, P).T,
        "x1_gin": a["L1_xattn_g_norm_in"], "x1_bin": a["L1_xattn_b_norm_in"],
        "x1_gout": a["L1_xattn_g_norm_out"], "x1_bout": a["L1_xattn_b_norm_out"],
        "x1_gffn": a["L1_xattn_g_ffn"], "x1_bffn": a["L1_xattn_b_ffn"],
        "x1_b1": a["L1_xattn_b1"].reshape(FT, P).T, "x1_b2": a["L1_xattn_b2"], "x1_dskip": a["L1_xattn_D_skip"],
        "f1_bup": a["L1_ffn_exp_bup"].T, "f1_bg": a["L1_ffn_exp_bg"].T,
        "f1_sup_b": a["L1_ffn_share_bup"].reshape(NSH, P).T, "f1_sg": a["L1_ffn_share_bg"],
        "f1_sdown": a["L1_ffn_share_bdown"], "f1_norm": a["L1_ffn_norm_w"].T,
        "m_dcol": np.repeat(a["L0_attn_D_param"], PD).reshape(2, P).T,
        "one": np.ones(P, f), "sign": np.repeat(np.array([1.0, -1.0], f), P // 2),
        "phase": np.repeat(np.array([0.25, 0.0], f), P // 2), "phase2": np.repeat(np.array([0.0, 0.25], f), P // 2),
        "eps5": np.full(P, EPS5, f), "eps6": np.full(P, EPS6, f), "oneD": np.full(P, 1.0 / D, f),
        "half_pi": np.full(P, PI / 2, f),
    }
    packed_cols = np.concatenate([cols[n].reshape(P, w) for n, (_, w) in COL.items()], 1)
    rws = {
        "m_bias8": np.concatenate([a["L0_attn_dt_bias"], np.zeros(HM, f)]),
        "m_bbias": a["L0_attn_B_bias"], "m_cbias": a["L0_attn_C_bias"],
        "m_bnw": a["L0_attn_B_norm_w"], "m_cnw": a["L0_attn_C_norm_w"],
        "et_gate": a["L1_attn_et_gate"], "is_gate": a["L1_attn_is_gate"], "mod_gate": a["L1_xattn_mod_gate"],
        "log_dt": a["L1_xattn_log_dt"], "f1_rb": a["L1_ffn_router_b"], "f1_gb": a["L1_ffn_gate_bias"],
        "jrow": np.arange(JL, dtype=f), "irow": JL * np.arange(IL, dtype=f),
    }
    packed_rows = np.concatenate([rws[n].reshape(-1) for n in ROW])
    at = np.clip(np.arange(RW)[None, :] - np.arange(P)[:, None] - (S - P) + TBL // 2, 0, TBL - 1)
    small, fwd, inv = shape_constants()
    wkv = a["L0_xattn_Wkv"].reshape(NH, 2, DH, DC)
    ctx = np.concatenate([a["ctx_768"].transpose(0, 2, 1), np.zeros((B, DC, MP - M), f)], 2)

    experts = np.concatenate([a["L0_ffn_w1"], a["L0_ffn_b1"].reshape(E0, FT, P).transpose(0, 2, 1),
                              a["L0_ffn_w2"].reshape(E0, FT, P, P).transpose(0, 2, 1, 3).reshape(E0, P, FF)], 2)

    def twice(m):
        return np.concatenate([m.T, m.T], 0)
    arrays = {
        "x": a["x"].transpose(0, 2, 1), "ctx": ctx,
        "vmask": a["mask_BxS2_bf1"], "tmask": a["mask_BxS_bf1"].reshape(B, T, P).transpose(0, 2, 1),
        "cols": packed_cols, "rows": packed_rows, "small": small, "fwd": fwd, "inv": inv,
        "skew": a["L1_attn_time_bias"].reshape(-1)[at],
        "m_win": a["L0_attn_W_in"].T, "m_wout": a["L0_attn_W_out"].T,
        "x0_wq": a["L0_xattn_Wq"].T[:, by_width], "x0_wk": wkv[:, 0].reshape(P, DC).T[:, by_width], "x0_wv": wkv[:, 1].reshape(P, DC).T,
        "x0_wo": a["L0_xattn_Wo"].T,
        "f0_gate": a["L0_ffn_gate_w"], "experts": experts,
        "a1_wq": a["L1_attn_Wq"].T[:, by_width], "a1_wk": a["L1_attn_Wk"].T[:, by_width], "a1_wv": a["L1_attn_Wv"].T[:, by_group],
        "a1_wo": a["L1_attn_Wo"].T,
        "x1_wq": a["L1_xattn_Wq"], "x1_wk": a["L1_xattn_Wk"], "x1_wv": a["L1_xattn_Wv"],
        "x1_win": a["L1_xattn_W_film_in"], "x1_wout": a["L1_xattn_W_film_out"],
        "x1_w1": a["L1_xattn_W1"], "x1_w2": a["L1_xattn_W2"],
        "f1_router": a["L1_ffn_router_W"], "f1_up": a["L1_ffn_exp_Wup"], "f1_g": a["L1_ffn_exp_Wg"],
        "esel": np.tile(np.repeat(np.eye(E1, dtype=f)[:, :, None], P, 2), (3, 1, 1)), "f1_down": a["L1_ffn_exp_Wdown"], "f1_bdown": np.tile(a["L1_ffn_exp_bdown"], (3, 1)),
        "f1_sup": a["L1_ffn_share_Wup"], "f1_swg": a["L1_ffn_share_Wg"], "f1_swdown": a["L1_ffn_share_Wdown"],
        "s4": np.stack([twice(a["L1_xattn_A_re"]), twice(a["L1_xattn_A_im"]), twice(a["L1_xattn_C_re"]),
                        twice(a["L1_xattn_C_im"])], 1),
    }
    return {n: np.ascontiguousarray(v) for n, v in arrays.items()}


def kernel(**inputs):
    import concourse.bacc as bacc
    from concourse.bass_utils import run_bass_kernel_spmd

    arrays = laid_out(inputs)
    nc = bacc.Bacc("TRN2", target_bir_lowering=False, num_devices=1)
    I = {n: nc.dram_tensor(f"in_{n}", a.shape, mybir.dt.from_np(a.dtype), kind="ExternalInput").ap()
         for n, a in arrays.items()}
    out = nc.dram_tensor("out_y", (B, D, S), F32, kind="ExternalOutput").ap()
    decoder(nc, I, out)
    r = run_bass_kernel_spmd(nc, [{f"in_{n}": a for n, a in arrays.items()}], core_ids=[0])
    return np.ascontiguousarray(r.results[0]["out_y"].transpose(0, 2, 1))
```
